# Optimizing a Trainium2 kernel written in Bass

```python
import numpy as np
import jax
import jax.numpy as jnp

def _softmax(x, axis=-1):
    return jax.nn.softmax(x, axis=axis)

def _gelu(x):
    return jax.nn.gelu(x, approximate=True)

def _silu(x):
    return jax.nn.silu(x)

def _sigmoid(x):
    return jax.nn.sigmoid(x)

def _layernorm(x, axis=-1, eps=1e-05):
    m = jnp.mean(x, axis=axis, keepdims=True)
    v = jnp.var(x, axis=axis, keepdims=True)
    return (x - m) / jnp.sqrt(v + eps)

def _scatter_add(tgt, idx, src, axis=0):
    return tgt.at[idx].add(src)

def _segment_sum(src, seg, n):
    return jax.ops.segment_sum(src, seg, n)
kernel_name = 'mk_gnn_preln_d4_gnn_r32_aa1ee0'

def setup_inputs(seed: int=0):
    np.random.seed(seed)
    _w = jnp.asarray

    def _rec_inputs():
        import jax
        import jax.numpy as jnp
        _gk = jax.random.key(seed)
        x = -6.415e-05 + 1 * jax.random.normal(jax.random.fold_in(_gk, 1), (625, 512), jnp.float32)
        src = jax.random.randint(jax.random.fold_in(_gk, 2), (10000,), 0, 625, jnp.int32)
        dst = jnp.minimum((625 * jax.random.uniform(jax.random.fold_in(_gk, 3), (10000,)) ** 2.0).astype(jnp.int32), 19999)
        _o = jnp.argsort(dst, stable=True)
        src = src[_o]
        dst = dst[_o]
        edge_attr_128 = -0.00010739 + 0.99994 * jax.random.normal(jax.random.fold_in(_gk, 12), (10000, 128), jnp.float32)
        edge_attr_4 = 0.00171547 + 0.999346 * jax.random.normal(jax.random.fold_in(_gk, 13), (10000, 4), jnp.float32)
        edge_attr_8 = -0.000521468 + 0.999954 * jax.random.normal(jax.random.fold_in(_gk, 14), (10000, 8), jnp.float32)
        edge_attr_8_n2 = -0.000521468 + 0.999954 * jax.random.normal(jax.random.fold_in(_gk, 15), (10000, 8), jnp.float32)
        edge_type_8 = jax.random.randint(jax.random.fold_in(_gk, 17), (10000,), 0, 8, jnp.int32)
        edge_weight = jax.random.uniform(jax.random.fold_in(_gk, 18), (10000,), jnp.float32, 0.0, 0.999999)
        return (x, src, dst, edge_attr_128, edge_attr_4, edge_attr_8, edge_attr_8_n2, edge_type_8, edge_weight)
    x, src, dst, edge_attr_128, edge_attr_4, edge_attr_8, edge_attr_8_n2, edge_type_8, edge_weight = _rec_inputs()

    def _L0_gnn_setup():
        import jax, jax.numpy as jnp
        import numpy as np
        N = 625
        E = 20000
        D = 512
        H = 8
        DH = D // H
        EPS = 1e-05

        def layer_norm(x, g, b):
            mu = x.mean(-1, keepdims=True)
            var = ((x - mu) ** 2).mean(-1, keepdims=True)
            return (x - mu) * jax.lax.rsqrt(var + EPS) * g + b
        key = jax.random.key(seed)
        ks = jax.random.split(key, 12)
        return dict(node_feature=jax.random.normal(ks[0], (N, D), jnp.float32), src=jax.random.randint(ks[1], (E,), 0, N, dtype=jnp.int32), dst=jax.random.randint(ks[2], (E,), 0, N, dtype=jnp.int32), dist_attn=jax.random.normal(ks[3], (E, H), jnp.float32), path_attn=jax.random.normal(ks[4], (E, H), jnp.float32), Wqkv=jax.random.normal(ks[5], (D, 3 * D), jnp.float32) / np.float32(np.sqrt(D)), bqkv=jnp.zeros((3 * D,), jnp.float32), Wo=jax.random.normal(ks[6], (D, D), jnp.float32) / np.float32(np.sqrt(D)), bo=jnp.zeros((D,), jnp.float32), ln1_g=jnp.ones((D,), jnp.float32), ln1_b=jnp.zeros((D,), jnp.float32), W1=jax.random.normal(ks[7], (D, 4 * D), jnp.float32) / np.float32(np.sqrt(D)), b1=jnp.zeros((4 * D,), jnp.float32), W2=jax.random.normal(ks[8], (4 * D, D), jnp.float32) / np.float32(np.sqrt(4 * D)), b2=jnp.zeros((D,), jnp.float32), ln2_g=jnp.ones((D,), jnp.float32), ln2_b=jnp.zeros((D,), jnp.float32))
    _L0_gnn_all = _L0_gnn_setup()
    _L0_gnn_in = {k: v for k, v in _L0_gnn_all.items() if k in ('Wqkv', 'bqkv', 'Wo', 'bo', 'ln1_g', 'ln1_b', 'W1', 'b1', 'W2', 'b2', 'ln2_g', 'ln2_b')}
    del _L0_gnn_all

    def _L1_gnn_setup():
        import jax, jax.numpy as jnp
        import numpy as np
        MUL = 128
        N_NODES = 10000
        N_EDGES = 5000
        R_BASIS = 8
        HIDDEN = 64
        W_NUMEL = 4 * MUL
        SQRT3 = 3.0 ** 0.5
        SILU_2MOM = 1.679177
        AVG_NUM_NEIGHBORS = 10.0

        def _lin_irreps(x0, x1, W0, W1):
            y0 = x0 @ W0 / jnp.sqrt(jnp.float32(W0.shape[0]))
            y1 = jnp.einsum('num,uv->nvm', x1, W1) / jnp.sqrt(jnp.float32(W1.shape[0]))
            return (y0, y1)

        def _forward(node_feats, edge_attrs, edge_feats, edge_index, W_up0, W_up1, W_mlp1, W_mlp2, W_mlp3, W_mlp4, W_out0, W_out1):
            num_nodes = node_feats.shape[0]
            sender, receiver = (edge_index[0], edge_index[1])
            x0 = node_feats[:, :MUL]
            x1 = node_feats[:, MUL:].reshape(num_nodes, MUL, 3)
            x0, x1 = _lin_irreps(x0, x1, W_up0, W_up1)
            h = edge_feats
            for W in (W_mlp1, W_mlp2, W_mlp3):
                h = SILU_2MOM * jax.nn.silu(h @ W / jnp.sqrt(jnp.float32(W.shape[0])))
            tpw = h @ W_mlp4 / jnp.sqrt(jnp.float32(W_mlp4.shape[0]))
            w1, w2, w3, w4 = jnp.split(tpw, 4, axis=-1)
            s0 = x0[sender]
            s1 = x1[sender]
            y0 = edge_attrs[:, 0:1]
            y1 = edge_attrs[:, 1:4]
            p1 = w1 * s0 * y0
            p2 = (w2 * s0)[:, :, None] * y1[:, None, :]
            p3 = w3[:, :, None] * s1 * y0[:, None, :]
            p4 = w4 * jnp.einsum('eum,em->eu', s1, y1) / SQRT3
            m0 = jnp.concatenate([p1, p4], axis=-1)
            m1 = jnp.concatenate([p2, p3], axis=1)
            msg0 = jax.ops.segment_sum(m0, receiver, num_segments=num_nodes)
            msg1 = jax.ops.segment_sum(m1, receiver, num_segments=num_nodes)
            o0, o1 = _lin_irreps(msg0, msg1, W_out0, W_out1)
            out = jnp.concatenate([o0, o1.reshape(num_nodes, 3 * MUL)], axis=-1)
            return out / AVG_NUM_NEIGHBORS
        key = jax.random.key(seed)
        ks = jax.random.split(key, 12)
        rn = lambda k, s: jax.random.normal(k, s, dtype=jnp.float32)
        return {'node_feats': rn(ks[0], (N_NODES, 4 * MUL)), 'edge_attrs': rn(ks[1], (N_EDGES, 4)), 'edge_feats': rn(ks[2], (N_EDGES, R_BASIS)), 'edge_index': jax.random.randint(ks[3], (2, N_EDGES), 0, N_NODES), 'W_up0': rn(ks[4], (MUL, MUL)), 'W_up1': rn(ks[5], (MUL, MUL)), 'W_mlp1': rn(ks[6], (R_BASIS, HIDDEN)), 'W_mlp2': rn(ks[7], (HIDDEN, HIDDEN)), 'W_mlp3': rn(ks[8], (HIDDEN, HIDDEN)), 'W_mlp4': rn(ks[9], (HIDDEN, W_NUMEL)), 'W_out0': rn(ks[10], (2 * MUL, MUL)), 'W_out1': rn(ks[11], (2 * MUL, MUL))}
    _L1_gnn_all = _L1_gnn_setup()
    _L1_gnn_in = {k: v for k, v in _L1_gnn_all.items() if k in ('W_up0', 'W_up1', 'W_mlp1', 'W_mlp2', 'W_mlp3', 'W_mlp4', 'W_out0', 'W_out1')}
    del _L1_gnn_all

    def _L2_gnn_setup():
        import jax, jax.numpy as jnp
        import numpy as np
        N_NODES = 625
        N_EDGES = 3125
        IN = 512
        HID = 512
        OUT = 512
        EF = 128
        NH = 16
        HEAD = OUT // NH

        def _ln(x):
            mu = jnp.mean(x, axis=-1, keepdims=True)
            var = jnp.var(x, axis=-1, keepdims=True)
            return (x - mu) / jnp.sqrt(var + 1e-05)

        def _mlp(x, W1, b1, g, be, W2, b2):
            hdn = x @ W1 + b1
            hdn = _ln(hdn) * g + be
            hdn = jax.nn.relu(hdn)
            return hdn @ W2 + b2
        key = jax.random.key(seed)
        ks = jax.random.split(key, 16)

        def w(k, i, o):
            return jax.random.normal(k, (i, o), jnp.float32) / np.float32(np.sqrt(i))
        inp = {'h': jax.random.normal(ks[0], (N_NODES, IN), jnp.float32), 'edge_feat': jax.random.normal(ks[1], (N_EDGES, EF), jnp.float32), 'edge_index': jax.random.randint(ks[2], (2, N_EDGES), 0, N_NODES, jnp.int32)}
        inp['hk_W1'] = w(ks[3], IN + EF, HID)
        inp['hk_b1'] = jnp.zeros((HID,), jnp.float32)
        inp['hk_g'] = jnp.ones((HID,), jnp.float32)
        inp['hk_be'] = jnp.zeros((HID,), jnp.float32)
        inp['hk_W2'] = w(ks[4], HID, OUT)
        inp['hk_b2'] = jnp.zeros((OUT,), jnp.float32)
        inp['hv_W1'] = w(ks[5], IN + EF, HID)
        inp['hv_b1'] = jnp.zeros((HID,), jnp.float32)
        inp['hv_g'] = jnp.ones((HID,), jnp.float32)
        inp['hv_be'] = jnp.zeros((HID,), jnp.float32)
        inp['hv_W2'] = w(ks[6], HID, OUT)
        inp['hv_b2'] = jnp.zeros((OUT,), jnp.float32)
        inp['hq_W1'] = w(ks[7], IN, HID)
        inp['hq_b1'] = jnp.zeros((HID,), jnp.float32)
        inp['hq_g'] = jnp.ones((HID,), jnp.float32)
        inp['hq_be'] = jnp.zeros((HID,), jnp.float32)
        inp['hq_W2'] = w(ks[8], HID, OUT)
        inp['hq_b2'] = jnp.zeros((OUT,), jnp.float32)
        inp['no_W1'] = w(ks[9], 2 * HID, HID)
        inp['no_b1'] = jnp.zeros((HID,), jnp.float32)
        inp['no_g'] = jnp.ones((HID,), jnp.float32)
        inp['no_be'] = jnp.zeros((HID,), jnp.float32)
        inp['no_W2'] = w(ks[10], HID, HID)
        inp['no_b2'] = jnp.zeros((HID,), jnp.float32)
        return inp
    _L2_gnn_all = _L2_gnn_setup()
    _L2_gnn_in = {k: v for k, v in _L2_gnn_all.items() if k in ('hk_W1', 'hk_b1', 'hk_g', 'hk_be', 'hk_W2', 'hk_b2', 'hv_W1', 'hv_b1', 'hv_g', 'hv_be', 'hv_W2', 'hv_b2', 'hq_W1', 'hq_b1', 'hq_g', 'hq_be', 'hq_W2', 'hq_b2', 'no_W1', 'no_b1', 'no_g', 'no_be', 'no_W2', 'no_b2')}
    del _L2_gnn_all

    def _L3_gnn_setup():
        import jax, jax.numpy as jnp
        import numpy as np
        N, IN_DIM, H, D, E = (50000, 512, 8, 64, 25000)
        NEG_SLOPE = 0.2
        LN_EPS = 1e-05
        key = jax.random.key(seed)
        ks = jax.random.split(key, 8)
        x = jax.random.normal(ks[0], (N, IN_DIM), dtype=jnp.float32)
        edge_index = jax.random.randint(ks[1], (2, E), 0, N, dtype=jnp.int64)
        edge_type = jax.random.randint(ks[2], (E,), 0, 8, dtype=jnp.int64)
        edge_weight = jax.random.uniform(ks[3], (E,), dtype=jnp.float32)
        W = jax.random.normal(ks[4], (H * D, IN_DIM), dtype=jnp.float32) * (1.0 / np.sqrt(IN_DIM))
        a_src = jax.random.normal(ks[5], (H, D), dtype=jnp.float32) * (1.0 / np.sqrt(D))
        a_dst = jax.random.normal(ks[6], (H, D), dtype=jnp.float32) * (1.0 / np.sqrt(D))
        et_emb = jax.random.normal(ks[7], (8, H), dtype=jnp.float32)
        ln_gamma = jnp.ones((H * D,), dtype=jnp.float32)
        ln_beta = jnp.zeros((H * D,), dtype=jnp.float32)
        return {'x': x, 'edge_index': edge_index, 'edge_type': edge_type, 'edge_weight': edge_weight, 'W': W, 'a_src': a_src, 'a_dst': a_dst, 'et_emb': et_emb, 'ln_gamma': ln_gamma, 'ln_beta': ln_beta}
    _L3_gnn_all = _L3_gnn_setup()
    _L3_gnn_in = {k: v for k, v in _L3_gnn_all.items() if k in ('W', 'a_src', 'a_dst', 'et_emb', 'ln_gamma', 'ln_beta')}
    del _L3_gnn_all
    return {'x': x, 'src': src, 'dst': dst, 'edge_attr_128': edge_attr_128, 'edge_attr_4': edge_attr_4, 'edge_attr_8': edge_attr_8, 'edge_attr_8_n2': edge_attr_8_n2, 'edge_type_8': edge_type_8, 'edge_weight': edge_weight, 'L0_gnn_Wqkv': _L0_gnn_in['Wqkv'], 'L0_gnn_bqkv': _L0_gnn_in['bqkv'], 'L0_gnn_Wo': _L0_gnn_in['Wo'], 'L0_gnn_bo': _L0_gnn_in['bo'], 'L0_gnn_ln1_g': _L0_gnn_in['ln1_g'], 'L0_gnn_ln1_b': _L0_gnn_in['ln1_b'], 'L0_gnn_W1': _L0_gnn_in['W1'], 'L0_gnn_b1': _L0_gnn_in['b1'], 'L0_gnn_W2': _L0_gnn_in['W2'], 'L0_gnn_b2': _L0_gnn_in['b2'], 'L0_gnn_ln2_g': _L0_gnn_in['ln2_g'], 'L0_gnn_ln2_b': _L0_gnn_in['ln2_b'], 'L1_gnn_W_up0': _L1_gnn_in['W_up0'], 'L1_gnn_W_up1': _L1_gnn_in['W_up1'], 'L1_gnn_W_mlp1': _L1_gnn_in['W_mlp1'], 'L1_gnn_W_mlp2': _L1_gnn_in['W_mlp2'], 'L1_gnn_W_mlp3': _L1_gnn_in['W_mlp3'], 'L1_gnn_W_mlp4': _L1_gnn_in['W_mlp4'], 'L1_gnn_W_out0': _L1_gnn_in['W_out0'], 'L1_gnn_W_out1': _L1_gnn_in['W_out1'], 'L2_gnn_hk_W1': _L2_gnn_in['hk_W1'], 'L2_gnn_hk_b1': _L2_gnn_in['hk_b1'], 'L2_gnn_hk_g': _L2_gnn_in['hk_g'], 'L2_gnn_hk_be': _L2_gnn_in['hk_be'], 'L2_gnn_hk_W2': _L2_gnn_in['hk_W2'], 'L2_gnn_hk_b2': _L2_gnn_in['hk_b2'], 'L2_gnn_hv_W1': _L2_gnn_in['hv_W1'], 'L2_gnn_hv_b1': _L2_gnn_in['hv_b1'], 'L2_gnn_hv_g': _L2_gnn_in['hv_g'], 'L2_gnn_hv_be': _L2_gnn_in['hv_be'], 'L2_gnn_hv_W2': _L2_gnn_in['hv_W2'], 'L2_gnn_hv_b2': _L2_gnn_in['hv_b2'], 'L2_gnn_hq_W1': _L2_gnn_in['hq_W1'], 'L2_gnn_hq_b1': _L2_gnn_in['hq_b1'], 'L2_gnn_hq_g': _L2_gnn_in['hq_g'], 'L2_gnn_hq_be': _L2_gnn_in['hq_be'], 'L2_gnn_hq_W2': _L2_gnn_in['hq_W2'], 'L2_gnn_hq_b2': _L2_gnn_in['hq_b2'], 'L2_gnn_no_W1': _L2_gnn_in['no_W1'], 'L2_gnn_no_b1': _L2_gnn_in['no_b1'], 'L2_gnn_no_g': _L2_gnn_in['no_g'], 'L2_gnn_no_be': _L2_gnn_in['no_be'], 'L2_gnn_no_W2': _L2_gnn_in['no_W2'], 'L2_gnn_no_b2': _L2_gnn_in['no_b2'], 'L3_gnn_W': _L3_gnn_in['W'], 'L3_gnn_a_src': _L3_gnn_in['a_src'], 'L3_gnn_a_dst': _L3_gnn_in['a_dst'], 'L3_gnn_et_emb': _L3_gnn_in['et_emb'], 'L3_gnn_ln_gamma': _L3_gnn_in['ln_gamma'], 'L3_gnn_ln_beta': _L3_gnn_in['ln_beta']}

def reference(x, src, dst, edge_attr_128, edge_attr_4, edge_attr_8, edge_attr_8_n2, edge_type_8, edge_weight, L0_gnn_Wqkv, L0_gnn_bqkv, L0_gnn_Wo, L0_gnn_bo, L0_gnn_ln1_g, L0_gnn_ln1_b, L0_gnn_W1, L0_gnn_b1, L0_gnn_W2, L0_gnn_b2, L0_gnn_ln2_g, L0_gnn_ln2_b, L1_gnn_W_up0, L1_gnn_W_up1, L1_gnn_W_mlp1, L1_gnn_W_mlp2, L1_gnn_W_mlp3, L1_gnn_W_mlp4, L1_gnn_W_out0, L1_gnn_W_out1, L2_gnn_hk_W1, L2_gnn_hk_b1, L2_gnn_hk_g, L2_gnn_hk_be, L2_gnn_hk_W2, L2_gnn_hk_b2, L2_gnn_hv_W1, L2_gnn_hv_b1, L2_gnn_hv_g, L2_gnn_hv_be, L2_gnn_hv_W2, L2_gnn_hv_b2, L2_gnn_hq_W1, L2_gnn_hq_b1, L2_gnn_hq_g, L2_gnn_hq_be, L2_gnn_hq_W2, L2_gnn_hq_b2, L2_gnn_no_W1, L2_gnn_no_b1, L2_gnn_no_g, L2_gnn_no_be, L2_gnn_no_W2, L2_gnn_no_b2, L3_gnn_W, L3_gnn_a_src, L3_gnn_a_dst, L3_gnn_et_emb, L3_gnn_ln_gamma, L3_gnn_ln_beta):
    import jax
    import jax.numpy as jnp

    def _L0_gnn_ref(node_feature, src, dst, dist_attn, path_attn, Wqkv, bqkv, Wo, bo, ln1_g, ln1_b, W1, b1, W2, b2, ln2_g, ln2_b):
        import jax, jax.numpy as jnp
        import numpy as np
        N = 625
        E = 20000
        D = 512
        H = 8
        DH = D // H
        EPS = 1e-05

        def layer_norm(x, g, b):
            mu = x.mean(-1, keepdims=True)
            var = ((x - mu) ** 2).mean(-1, keepdims=True)
            return (x - mu) * jax.lax.rsqrt(var + EPS) * g + b
        h = layer_norm(node_feature, ln1_g, ln1_b)
        qkv = (h @ Wqkv + bqkv).reshape(N, 3, H, DH)
        q = qkv[:, 0] * D ** (-0.5)
        k = qkv[:, 1]
        v = qkv[:, 2]
        logits = jnp.einsum('ehd,ehd->eh', q[src], k[dst])
        a = logits + dist_attn + path_attn
        mx = jax.ops.segment_max(a, dst, num_segments=N)
        e = jnp.exp(a - mx[dst])
        s = jax.ops.segment_sum(e, dst, num_segments=N)
        sa = e / s[dst]
        msg = v[src] * sa[:, :, None]
        agg = jax.ops.segment_sum(msg, dst, num_segments=N).reshape(N, D)
        x = agg @ Wo + bo
        h1 = node_feature + x
        h2 = layer_norm(h1, ln2_g, ln2_b)
        h2 = jax.nn.gelu(h2 @ W1 + b1, approximate=False) @ W2 + b2
        return h1 + h2

    def _L1_gnn_ref(node_feats, edge_attrs, edge_feats, edge_index, W_up0, W_up1, W_mlp1, W_mlp2, W_mlp3, W_mlp4, W_out0, W_out1):
        import jax, jax.numpy as jnp
        import numpy as np
        MUL = 128
        N_NODES = 10000
        N_EDGES = 5000
        R_BASIS = 8
        HIDDEN = 64
        W_NUMEL = 4 * MUL
        SQRT3 = 3.0 ** 0.5
        SILU_2MOM = 1.679177
        AVG_NUM_NEIGHBORS = 10.0

        def _lin_irreps(x0, x1, W0, W1):
            y0 = x0 @ W0 / jnp.sqrt(jnp.float32(W0.shape[0]))
            y1 = jnp.einsum('num,uv->nvm', x1, W1) / jnp.sqrt(jnp.float32(W1.shape[0]))
            return (y0, y1)

        def _forward(node_feats, edge_attrs, edge_feats, edge_index, W_up0, W_up1, W_mlp1, W_mlp2, W_mlp3, W_mlp4, W_out0, W_out1):
            num_nodes = node_feats.shape[0]
            sender, receiver = (edge_index[0], edge_index[1])
            x0 = node_feats[:, :MUL]
            x1 = node_feats[:, MUL:].reshape(num_nodes, MUL, 3)
            x0, x1 = _lin_irreps(x0, x1, W_up0, W_up1)
            h = edge_feats
            for W in (W_mlp1, W_mlp2, W_mlp3):
                h = SILU_2MOM * jax.nn.silu(h @ W / jnp.sqrt(jnp.float32(W.shape[0])))
            tpw = h @ W_mlp4 / jnp.sqrt(jnp.float32(W_mlp4.shape[0]))
            w1, w2, w3, w4 = jnp.split(tpw, 4, axis=-1)
            s0 = x0[sender]
            s1 = x1[sender]
            y0 = edge_attrs[:, 0:1]
            y1 = edge_attrs[:, 1:4]
            p1 = w1 * s0 * y0
            p2 = (w2 * s0)[:, :, None] * y1[:, None, :]
            p3 = w3[:, :, None] * s1 * y0[:, None, :]
            p4 = w4 * jnp.einsum('eum,em->eu', s1, y1) / SQRT3
            m0 = jnp.concatenate([p1, p4], axis=-1)
            m1 = jnp.concatenate([p2, p3], axis=1)
            msg0 = jax.ops.segment_sum(m0, receiver, num_segments=num_nodes)
            msg1 = jax.ops.segment_sum(m1, receiver, num_segments=num_nodes)
            o0, o1 = _lin_irreps(msg0, msg1, W_out0, W_out1)
            out = jnp.concatenate([o0, o1.reshape(num_nodes, 3 * MUL)], axis=-1)
            return out / AVG_NUM_NEIGHBORS
        return _forward(node_feats, edge_attrs, edge_feats, edge_index, W_up0, W_up1, W_mlp1, W_mlp2, W_mlp3, W_mlp4, W_out0, W_out1)

    def _L2_gnn_ref(h, edge_feat, edge_index, hk_W1, hk_b1, hk_g, hk_be, hk_W2, hk_b2, hv_W1, hv_b1, hv_g, hv_be, hv_W2, hv_b2, hq_W1, hq_b1, hq_g, hq_be, hq_W2, hq_b2, no_W1, no_b1, no_g, no_be, no_W2, no_b2):
        import jax, jax.numpy as jnp
        import numpy as np
        N_NODES = 625
        N_EDGES = 3125
        IN = 512
        HID = 512
        OUT = 512
        EF = 128
        NH = 16
        HEAD = OUT // NH

        def _ln(x):
            mu = jnp.mean(x, axis=-1, keepdims=True)
            var = jnp.var(x, axis=-1, keepdims=True)
            return (x - mu) / jnp.sqrt(var + 1e-05)

        def _mlp(x, W1, b1, g, be, W2, b2):
            hdn = x @ W1 + b1
            hdn = _ln(hdn) * g + be
            hdn = jax.nn.relu(hdn)
            return hdn @ W2 + b2
        N = h.shape[0]
        src, dst = (edge_index[0], edge_index[1])
        kv_in = jnp.concatenate([h[src], edge_feat], axis=-1)
        k = _mlp(kv_in, hk_W1, hk_b1, hk_g, hk_be, hk_W2, hk_b2).reshape(-1, NH, HEAD)
        v = _mlp(kv_in, hv_W1, hv_b1, hv_g, hv_be, hv_W2, hv_b2).reshape(-1, NH, HEAD)
        q = _mlp(h, hq_W1, hq_b1, hq_g, hq_be, hq_W2, hq_b2).reshape(-1, NH, HEAD)
        logits = jnp.sum(q[dst] * k, axis=-1) / np.float32(np.sqrt(HEAD))
        mx = jax.ops.segment_max(logits, dst, num_segments=N)
        ex = jnp.exp(logits - mx[dst])
        den = jax.ops.segment_sum(ex, dst, num_segments=N)
        alpha = ex / den[dst]
        m = alpha[..., None] * v
        out = jax.ops.segment_sum(m, dst, num_segments=N).reshape(N, OUT)
        out = _mlp(jnp.concatenate([out, h], axis=-1), no_W1, no_b1, no_g, no_be, no_W2, no_b2)
        return out + h

    def _L3_gnn_ref(x, edge_index, edge_type, edge_weight, W, a_src, a_dst, et_emb, ln_gamma, ln_beta):
        import jax, jax.numpy as jnp
        import numpy as np
        N, IN_DIM, H, D, E = (50000, 512, 8, 64, 25000)
        NEG_SLOPE = 0.2
        LN_EPS = 1e-05
        n, h_, d_ = (x.shape[0], a_src.shape[0], a_src.shape[1])
        h = (x @ W.T).reshape(n, h_, d_)
        src, dst = (edge_index[0], edge_index[1])
        h_src = h[src]
        e_src = jnp.einsum('ehd,hd->eh', h_src, a_src)
        e_dst = jnp.einsum('ehd,hd->eh', h[dst], a_dst)
        e = jax.nn.leaky_relu(e_src + e_dst, NEG_SLOPE)
        e = e * (1.0 + et_emb[edge_type])
        e = e * edge_weight[:, None]
        e_max = jnp.zeros((n, h_), x.dtype).at[dst].max(e)
        e = jnp.exp(e - e_max[dst])
        e_sum = jnp.zeros((n, h_), x.dtype).at[dst].add(e)
        alpha = e / (e_sum[dst] + 1e-10)
        msg = h_src * alpha[:, :, None]
        out = jnp.zeros((n, h_, d_), x.dtype).at[dst].add(msg).reshape(n, h_ * d_)
        out = out + x
        mu = jnp.mean(out, axis=-1, keepdims=True)
        var = jnp.var(out, axis=-1, keepdims=True)
        return (out - mu) / jnp.sqrt(var + LN_EPS) * ln_gamma + ln_beta
    edge_index = jnp.stack([src, dst])
    h = jnp.maximum(_layernorm(x, axis=-1), 0.0)
    x = x + _L0_gnn_ref(h, src, dst, edge_attr_8, edge_attr_8_n2, L0_gnn_Wqkv, L0_gnn_bqkv, L0_gnn_Wo, L0_gnn_bo, L0_gnn_ln1_g, L0_gnn_ln1_b, L0_gnn_W1, L0_gnn_b1, L0_gnn_W2, L0_gnn_b2, L0_gnn_ln2_g, L0_gnn_ln2_b)
    h = jnp.maximum(_layernorm(x, axis=-1), 0.0)
    x = x + _L1_gnn_ref(h, edge_attr_4, edge_attr_8, edge_index, L1_gnn_W_up0, L1_gnn_W_up1, L1_gnn_W_mlp1, L1_gnn_W_mlp2, L1_gnn_W_mlp3, L1_gnn_W_mlp4, L1_gnn_W_out0, L1_gnn_W_out1)
    h = jnp.maximum(_layernorm(x, axis=-1), 0.0)
    x = x + _L2_gnn_ref(h, edge_attr_128, edge_index, L2_gnn_hk_W1, L2_gnn_hk_b1, L2_gnn_hk_g, L2_gnn_hk_be, L2_gnn_hk_W2, L2_gnn_hk_b2, L2_gnn_hv_W1, L2_gnn_hv_b1, L2_gnn_hv_g, L2_gnn_hv_be, L2_gnn_hv_W2, L2_gnn_hv_b2, L2_gnn_hq_W1, L2_gnn_hq_b1, L2_gnn_hq_g, L2_gnn_hq_be, L2_gnn_hq_W2, L2_gnn_hq_b2, L2_gnn_no_W1, L2_gnn_no_b1, L2_gnn_no_g, L2_gnn_no_be, L2_gnn_no_W2, L2_gnn_no_b2)
    h = jnp.maximum(_layernorm(x, axis=-1), 0.0)
    x = x + _L3_gnn_ref(h, edge_index, edge_type_8, edge_weight, L3_gnn_W, L3_gnn_a_src, L3_gnn_a_dst, L3_gnn_et_emb, L3_gnn_ln_gamma, L3_gnn_ln_beta)
    return x

_drawn_inputs = setup_inputs


def setup_inputs(seed=0):
    import zlib

    import numpy as np

    out = dict(_drawn_inputs(seed))
    spreads = {'L0_gnn_bqkv': (0.0, 0.1),
     'L0_gnn_bo': (0.0, 0.1),
     'L0_gnn_ln1_g': (1.0, 0.2),
     'L0_gnn_ln1_b': (0.0, 0.1),
     'L0_gnn_b1': (0.0, 0.1),
     'L0_gnn_b2': (0.0, 0.1),
     'L0_gnn_ln2_g': (1.0, 0.2),
     'L0_gnn_ln2_b': (0.0, 0.1),
     'L2_gnn_hk_b1': (0.0, 0.8),
     'L2_gnn_hk_g': (1.0, 0.6),
     'L2_gnn_hk_be': (0.0, 0.8),
     'L2_gnn_hk_b2': (0.0, 2.0),
     'L2_gnn_hv_b1': (0.0, 0.413),
     'L2_gnn_hv_g': (1.0, 0.541),
     'L2_gnn_hv_be': (0.0, 0.517),
     'L2_gnn_hv_b2': (0.0, 0.354),
     'L2_gnn_hq_b1': (0.0, 0.8),
     'L2_gnn_hq_g': (1.0, 0.6),
     'L2_gnn_hq_be': (0.0, 0.8),
     'L2_gnn_hq_b2': (0.0, 0.8),
     'L2_gnn_no_b1': (0.0, 0.268),
     'L2_gnn_no_g': (1.0, 0.2),
     'L2_gnn_no_be': (0.0, 0.326),
     'L2_gnn_no_b2': (0.0, 0.1),
     'L3_gnn_ln_gamma': (1.0, 0.2),
     'L3_gnn_ln_beta': (0.0, 0.28)}
    factors = {'L2_gnn_hk_W1': 3.167, 'L2_gnn_hk_W2': 3.145, 'L2_gnn_hq_W1': 3.83, 'L2_gnn_hq_W2': 3.184}
    for name, (base, spread) in spreads.items():
        noise = np.random.default_rng([zlib.crc32(name.encode()), seed]).standard_normal(out[name].shape)
        drawn = base * np.exp(spread * noise) if base else spread * noise
        out[name] = jnp.asarray(drawn.astype(out[name].dtype))
    for name, factor in factors.items():
        out[name] = (out[name] * factor).astype(out[name].dtype)
    return out
```

```python
import math
from contextlib import ExitStack

import concourse.bass as bass
from concourse import mybir

F32 = mybir.dt.float32
I32 = mybir.dt.int32
BF16 = mybir.dt.bfloat16
ALU = mybir.AluOpType
ACT = mybir.ActivationFunctionType
AX = mybir.AxisListType

P = 128
NODES, D = 625, 512
NB = 5
EDGES = 10000
EP, EC = 125, 80
NT = EDGES // P + 1 + NB
U = 4
NI = NT // U
SLOTS = NT * P
PAD_NODE = NODES
RS = 24
RW = RS + 128
F_SRC, F_DST, F_W, F_TYPE, F_A4, F_A8, F_A8N = 0, 1, 2, 3, 4, 8, 16
SEG = SLOTS // P
BIG = 1.0e30
EPS = 1e-5
ACC = NB * D


class Env:
    pass


def hold(eng, *waits):
    waits = [(sem, value) for sem, value in waits if not (isinstance(value, int) and value <= 0)]
    for sem, value in waits:
        eng.wait_ge(sem, value)
    if waits:
        eng.nop(nofuse=True)


def turns(eng, n, body):
    body(0)
    with eng.Fori(1, n) as it:
        body(it)


class Steps:

    def __init__(self, eng, sem, base=0):
        self.eng, self.sem, self.base, self.n = eng, sem, base, 0

    def __call__(self, ins):
        ins.then_inc(self.sem, 1)
        self.n += 1

    def settle(self):
        hold(self.eng, (self.sem, self.base + self.n))



def ln_vector(v, e, s, src):
    for b in range(NB):
        v.bn_stats(e.stats[:, b, :], src[:, b, :]).then_inc(s.stats, 1)
    for b in range(NB):
        v.wait_ge(s.stats, b + 1)
        v.bn_aggr(e.mv[:, b, :], e.stats[:, b, :]).then_inc(s.aggr, 1)
    v.wait_ge(s.aggr, NB)
    v.tensor_scalar(e.vare[:, :], e.mv[:, :, 1], EPS, None, ALU.add).then_inc(s.vare, 1)
    v.wait_ge(s.sd, 1)
    v.reciprocal(e.rstd[:, :], e.sd[:, :]).then_inc(s.rstd, 1)
    v.wait_ge(s.rstd, 1)
    v.scalar_tensor_tensor(out=e.nbias[:, :], in0=e.mv[:, :, 0], scalar=-1.0, in1=e.rstd[:, :],
                           op0=ALU.mult, op1=ALU.mult).then_inc(s.norm, 1)


def ln_scalar(a, e, s, src, dst, func):
    a.wait_ge(s.vare, 1)
    a.activation(e.sd[:, :], e.vare[:, :], ACT.Sqrt).then_inc(s.sd, 1)
    a.wait_ge(s.norm, 1)
    for b in range(NB):
        a.activation(dst[:, b, :], src[:, b, :], func, bias=e.nbias[:, b:b + 1],
                     scale=e.rstd[:, b:b + 1]).then_inc(s.normed, 1)


def ln_sems(e, name):
    s = Env()
    s.stats, s.aggr, s.vare, s.sd = e.sem(f"{name}_stats"), e.sem(f"{name}_aggr"), e.sem(f"{name}_vare"), e.sem(f"{name}_sd")
    s.rstd, s.norm, s.normed = e.sem(f"{name}_rstd"), e.sem(f"{name}_norm"), e.sem(f"{name}_normed")
    return s


def node_ln(e, name, src, dst, func):
    s = ln_sems(e, name)
    with e.nc.Block() as block:
        @block.vector
        def _(v):
            ln_vector(v, e, s, src)

        @block.scalar
        def _(a):
            ln_scalar(a, e, s, src, dst, func)


def node_linear(e, name, srcs, dstT, gb, funcT, lin, evac, ln=None):
    nc = e.nc
    s = ln_sems(e, name) if ln else None
    turned, copied = e.sem(f"{name}_turned"), e.sem(f"{name}_copied")
    summed, taken = e.sem(f"{name}_summed"), e.sem(f"{name}_taken")
    chunks = [(t, c) for t in srcs for c in range(4)]
    KC = len(chunks)
    G = KC // 4
    R = 4
    with nc.Block() as block:
        @block.vector
        def _(v):
            if ln:
                ln_vector(v, e, s, ln[0])
            g = 0
            for b in range(NB):
                for n in range(len(lin)):
                    v.wait_ge(summed, g + 1)
                    evac(v, b, n, e.ps[2 + g % R]).then_inc(taken, 1)
                    g += 1

        @block.scalar
        def _(a):
            if ln:
                ln_scalar(a, e, s, ln[0], ln[1], ACT.Identity)
            for b in range(NB):
                for q in range(G):
                    k = b * G + q
                    a.wait_ge(turned, k + 1)
                    ps = e.ps[k % 2].rearrange("p (c n) -> p c n", c=4)
                    if gb is None:
                        a.activation(dstT[:, 4 * q:4 * q + 4, b * P:(b + 1) * P], ps[:, :, :],
                                     funcT).then_inc(copied, 1)
                    else:
                        for c in range(4):
                            i = a.activation(dstT[:, 4 * q + c, b * P:(b + 1) * P], ps[:, c, :], funcT,
                                             scale=gb[0][:, c:c + 1], bias=gb[1][:, c:c + 1])
                        i.then_inc(copied, 1)

        @block.tensor
        def _(pe):
            def turn(b):
                for q in range(G):
                    k = b * G + q
                    if ln and q == 0:
                        pe.wait_ge(s.normed, b + 1)
                    if k >= 2:
                        pe.wait_ge(copied, k - 1)
                    for c in range(4):
                        t, cc = chunks[4 * q + c]
                        i = pe.transpose(e.ps[k % 2][:, c * P:(c + 1) * P], t[:, b, cc * P:(cc + 1) * P],
                                         e.ident[:, :])
                    i.then_inc(turned, 1)
            turn(0)
            g = 0
            for b in range(NB):
                if b + 1 < NB:
                    turn(b + 1)
                pe.wait_ge(copied, (b + 1) * G)
                for n, (w, bias) in enumerate(lin):
                    if g >= R:
                        pe.wait_ge(taken, g - R + 1)
                    ps = e.ps[2 + g % R]
                    for k in range(KC):
                        i = pe.matmul(ps[:, :], dstT[:, k, b * P:(b + 1) * P], w[:, k, :],
                                      start=(k == 0), stop=(k == KC - 1 and bias is None))
                    if bias is not None:
                        i = pe.matmul(ps[:, :], e.ones[0:1, :], bias, start=False, stop=True)
                    i.then_inc(summed, 1)
                    g += 1


def store_table(e, name, pairs):
    done = e.sem(f"{name}_stored")
    with e.nc.Block() as block:
        @block.sync
        def _(sp):
            for table, tile in pairs:
                sp.dma_start(table.rearrange("(b p) n -> p b n", p=P), tile).then_inc(done, 16)
            sp.wait_ge(done, 16 * len(pairs))



def prepare(e, i):
    nc = e.nc
    built, loaded, filled = e.sem("built"), e.sem("loaded"), e.sem("filled")
    ph_ready = e.sem("phantom_ready")
    with nc.Block() as block:
        @block.gpsimd
        def _(g):
            g.memset(e.ident[:, :], 0.0).then_inc(built, 1)
            g.memset(e.lower[:, :], 0.0).then_inc(built, 1)
            g.memset(e.window[:, :], 1.0).then_inc(built, 1)
            g.memset(e.x[:, NB - 1, :], 0.0).then_inc(built, 1)
            g.wait_ge(built, 4)
            g.affine_select(out=e.ident[:, :], in_=e.ident[:, :], compare_op=ALU.not_equal, fill=1.0,
                            base=0, pattern=[[-1, P]], channel_multiplier=1).then_inc(built, 1)
            g.affine_select(out=e.lower[:, :], in_=e.lower[:, :], compare_op=ALU.is_ge, fill=1.0,
                            base=0, pattern=[[-1, P]], channel_multiplier=1).then_inc(built, 1)
            g.affine_select(out=e.window[:, :], in_=e.window[:, :], compare_op=ALU.is_ge, fill=0.0,
                            base=EC - 1, pattern=[[-1, 2 * EC]], channel_multiplier=0).then_inc(built, 1)
            g.iota(e.nodeno[:, :], pattern=[[1, NB * P]], base=0, channel_multiplier=0,
                   allow_small_or_imprecise_dtypes=True).then_inc(built, 1)
            g.iota(e.lane[:, :], pattern=[[1, P]], base=0, channel_multiplier=0,
                   allow_small_or_imprecise_dtypes=True).then_inc(built, 1)
            g.iota(e.tile_at[:, :], pattern=[[P, NT]], base=0, channel_multiplier=0,
                   allow_small_or_imprecise_dtypes=True).then_inc(built, 1)
            g.wait_ge(built, 10)

        @block.vector
        def _(v):
            steps = Steps(v, e.sem("prep_steps"))
            steps(v.memset(e.phantom[:, :, :], 0.0))
            steps(v.memset(e.ones[:, :], 1.0))
            steps(v.memset(e.zeros[:, :], 0.0))
            steps(v.memset(e.onesb[:, :], 1.0))
            steps(v.memset(e.zerosb[:, :], 0.0))
            steps.settle()
            v.memset(e.phantom[:, :, F_DST:F_DST + 1], float(PAD_NODE)).then_inc(ph_ready, 1)

        @block.sync
        def _(sp):
            sp.wait_ge(ph_ready, 1)
            view = e.rec.rearrange("(p j k) f -> p j (k f)", p=P, k=e.PK)
            for j in range(SEG // e.PK):
                sp.dma_start(view[:, j, :], e.phantom.rearrange("p k f -> p (k f)")).then_inc(filled, 16)
            sp.wait_ge(filled, 16 * (SEG // e.PK))

        @block.scalar
        def _(a):
            a.wait_ge(built, 4)
            a.dma_start(e.x[:, 0:NB - 1, :], i["x"][0:(NB - 1) * P, :].rearrange("(b p) n -> p b n", p=P)).then_inc(loaded, 16)
            a.dma_start(e.x[0:NODES - (NB - 1) * P, NB - 1, :], i["x"][(NB - 1) * P:NODES, :]).then_inc(loaded, 16)
            for tile, src in ((e.srcs, i["src"]), (e.dsts, i["dst"]), (e.kinds, i["edge_type_8"]), (e.weights, i["edge_weight"])):
                a.dma_start(tile[:, :], src.rearrange("(p c) -> p c", c=EC)).then_inc(loaded, 16)
            for tile, src in ((e.a4, i["edge_attr_4"]), (e.a8, i["edge_attr_8"]), (e.a8n, i["edge_attr_8_n2"]),
                              (e.a128, i["edge_attr_128"])):
                a.dma_start(tile[:, :, :], src.rearrange("(p c) f -> p c f", c=EC)).then_inc(loaded, 16)
            for tile, src in e.loads0:
                a.dma_start(tile, src).then_inc(loaded, 16)
            a.wait_ge(loaded, 16 * (10 + len(e.loads0)))


def count_edges(e):
    nc = e.nc
    fields = e.sem("fields")
    marked, used, cleared = e.sem("cnt_marked"), e.sem("cnt_used"), e.sem("cnt_cleared")
    with nc.Block() as block:
        @block.vector
        def _(v):
            for at, n, src in ((F_SRC, 1, e.srcs), (F_DST, 1, e.dsts), (F_TYPE, 1, e.kinds), (F_W, 1, e.weights)):
                v.tensor_copy(e.small[:, :, at:at + 1], src[:, :, None]).then_inc(fields, 1)
            for at, n, src in ((F_A4, 4, e.a4), (F_A8, 8, e.a8), (F_A8N, 8, e.a8n)):
                v.tensor_copy(e.small[:, :, at:at + n], src[:, :, :]).then_inc(fields, 1)
            v.tensor_copy(e.dstf[:, :], e.dsts[:, :]).then_inc(fields, 1)
            v.wait_ge(fields, 8)
            def turn(it):
                for u in range(U):
                    hold(v, (used, it * U + (u + 1)))
                    v.tensor_scalar(e.mark[:, u, :], e.nodeno[0:EP, :], e.dstf[:, bass.ds(it * U + u, 1)], None,
                                    ALU.is_equal).then_inc(marked, 1)
            turns(v, EC // U, turn)

        @block.tensor
        def _(pe):
            outs = ((e.ps[0][:, :], e.ps[2][:, :], 0, 512), (e.ps[1][:, 0:P], e.ps[3][:, 0:P], 512, 640))
            for cnt, pre, a, b in outs:
                pe.matmul(cnt, e.zerosb[:, 0:P], e.zerosb[:, 0:b - a], start=True, stop=True)
                pe.matmul(pre, e.zerosb[:, 0:P], e.zerosb[:, 0:b - a], start=True, stop=True)
            pe.sem_inc(used, U)
            def turn(it):
                for u in range(U):
                    hold(pe, (marked, it * U + (u + 1)))
                    for cnt, pre, a, b in outs:
                        pe.matmul(cnt, e.onesb[0:EP, 0:P], e.mark[:, u, a:b], start=False, stop=True,
                                  skip_group_check=True)
                        i = pe.matmul(pre, e.lowerb[0:EP, :], e.mark[:, u, a:b], start=False, stop=True,
                                      skip_group_check=True)
                    i.then_inc(used, 1)
            turns(pe, EC // U, turn)

def place_edges(e):
    nc = e.nc
    with nc.Block() as block:
        @block.vector
        def _(v):
            steps = Steps(v, e.sem("place_steps"))
            steps(v.tensor_copy(e.cnt[:, 0:512], e.ps[0][:, :]))
            steps(v.tensor_copy(e.cnt[:, 512:640], e.ps[1][:, 0:P]))
            steps(v.memset(e.blk[:, :], 0.0))
            steps.settle()
            steps(v.tensor_reduce(e.bsum[:, :], e.cnt.rearrange("p (b n) -> p b n", b=NB), AX.X, ALU.add))
            steps.settle()
            steps(v.tensor_scalar(e.bsumi[:, :], e.bsum[:, :], float(P - 1), None, ALU.add))
            steps.settle()
            steps(v.tensor_scalar(e.btile[:, :], e.bsumi[:, :], 7, 7, ALU.arith_shift_right, ALU.logical_shift_left))
            steps.settle()
            steps(v.tensor_copy(e.bsize[:, :], e.btile[:, :]))
            steps.settle()
            steps(v.tensor_tensor_scan(e.bend[:, :], e.zeros[:, 0:NB], e.bsize[:, :], 0.0, ALU.add, ALU.add))
            steps.settle()
            steps(v.tensor_tensor(e.bstart[:, :], e.bend[:, :], e.bsize[:, :], ALU.subtract))
            steps.settle()
            for b in range(NB):
                steps(v.tensor_tensor_scan(e.base[:, b * P:(b + 1) * P], e.zeros[:, 0:P],
                                           e.cnt[:, b * P:(b + 1) * P], e.bstart[:, b:b + 1], ALU.add, ALU.add))
            for b in range(1, NB):
                steps.settle()
                steps(v.scalar_tensor_tensor(out=e.blk[:, :], in0=e.tile_at[:, :], scalar=e.bstart[:, b:b + 1],
                                             in1=e.blk[:, :], op0=ALU.is_ge, op1=ALU.add))
            steps.settle()
            steps(v.tensor_copy(e.blki[:, :], e.blk[:, :]))
            steps(v.tensor_tensor(e.base[:, :], e.base[:, :], e.cnt[:, :], ALU.subtract))
            steps.settle()
            steps(v.tensor_tensor(e.base[:, 0:512], e.base[:, 0:512], e.ps[2][:, :], ALU.add))
            steps(v.tensor_tensor(e.base[:, 512:640], e.base[:, 512:640], e.ps[3][:, 0:P], ALU.add))
            steps.settle()
            rank = e.sem("rank")
            def turn(it):
                for u in range(U):
                    c = it * U + u
                    hold(v, (rank, it * (2 * U) + 2 * u))
                    v.scalar_tensor_tensor(out=e.junk[:, 0, :], in0=e.nodeno[0:EP, :],
                                           scalar=e.dstf[:, bass.ds(c, 1)], in1=e.base[0:EP, :], op0=ALU.is_equal,
                                           op1=ALU.mult, accum_out=e.slota[:, bass.ds(c, 1)]).then_inc(rank, 1)
                    v.scalar_tensor_tensor(out=e.junk[:, 1, 0:EC], in0=e.dstf[:, :],
                                           scalar=e.dstf[:, bass.ds(c, 1)], in1=e.window[0:EP, bass.ds(EC - c, EC)],
                                           op0=ALU.is_equal, op1=ALU.mult,
                                           accum_out=e.slotb[:, bass.ds(c, 1)]).then_inc(rank, 1)
            turns(v, EC // U, turn)
            v.wait_ge(rank, 2 * EC)
            v.tensor_tensor(e.sloti[:, :], e.slota[:, :], e.slotb[:, :], ALU.add).then_inc(rank, 1)
            v.wait_ge(rank, 2 * EC + 1)


def scatter_records(e):
    nc = e.nc
    staged = e.sem("rec_staged")
    written = e.landed()
    cols, gone = e.sem("rec_cols"), e.sem("rec_gone")
    with nc.Block() as block:
        @block.scalar
        def _(a):
            def turn(it):
                for u in range(U):
                    hold(a, (written[u], it * 16))
                    a.activation(e.recbuf[:, u, 0:RS], e.small[:, bass.ds(it * U + u, 1), :].rearrange("p a f -> p (a f)"), ACT.Copy).then_inc(staged, 1)
                    a.activation(e.recbuf[:, u, RS:RW], e.a128[:, bass.ds(it * U + u, 1), :].rearrange("p a f -> p (a f)"), ACT.Copy).then_inc(staged, 1)
            turns(a, EC // U, turn)

        @block.gpsimd
        def _(g):
            def turn(it):
                hold(g, *[(written[u], it * 16) for u in range(U)])
                g.tensor_copy(e.slotbuf[:, :], e.sloti[:, bass.ds(it * U, U)]).then_inc(cols, 1)
                hold(g, (cols, it + 1))
                for u in range(U):
                    hold(g, (staged, it * (2 * U) + 2 * (u + 1)))
                    g.indirect_dma_start(e.rec[:, :], bass.IndirectOffsetOnAxis(ap=e.slotbuf[:, u:u + 1], axis=0),
                                         e.recbuf[:, u, :], None).then_inc(written[u], 16)
            turns(g, EC // U, turn)
            for u in range(U):
                g.wait_ge(written[u], 16 * (EC // U))


def load_sorted(e):
    nc = e.nc
    ld, dt, dd = e.sem("srt_loaded"), e.sem("srt_turned"), e.sem("srt_dst")
    sv, emb = e.sem("srt_steps"), e.sem("srt_row")
    with nc.Block() as block:
        @block.sync
        def _(sp):
            sp.dma_start(e.srt[:, :, :], e.rec[:, 0:RS].rearrange("(t p) f -> p t f", p=P)).then_inc(ld, 16)
            sp.wait_ge(sv, 2)
            sp.dma_start(e.dstd[1:1 + SLOTS, :].rearrange("(t p) a -> t (p a)", p=P), e.dstT[0:NT, :]).then_inc(dd, 16)
            sp.dma_start(e.dstd[0:1, :], e.guard[0:1, 0:1]).then_inc(dd, 16)
            sp.dma_start(e.dstd[SLOTS + 1:SLOTS + 2, :], e.guard[0:1, 1:2]).then_inc(dd, 16)
            sp.wait_ge(dd, 48)
            for k in range(3):
                sp.dma_start(e.seg3[:, k, :], e.dstd[k:k + SLOTS, :].rearrange("(p j) a -> p (j a)", p=P)).then_inc(dd, 16)

        @block.tensor
        def _(pe):
            pe.wait_ge(ld, 16)
            pe.transpose(e.ps[0][0:NT, 0:P], e.srt[:, :, F_DST], e.ident[:, :]).then_inc(dt, 1)
            pe.wait_ge(sv, e.ROWS_AT)
            for k in range(2):
                i = pe.matmul(e.ps[1][0:16, k * P:(k + 1) * P], e.whole[:, k:k + 1].to_broadcast([P, 16]), e.ident[:, :],
                              start=True, stop=True)
            i.then_inc(emb, 1)

        @block.vector
        def _(v):
            st = Steps(v, sv)
            v.wait_ge(dt, 1)
            st(v.tensor_copy(e.dstT[0:NT, :], e.ps[0][0:NT, 0:P]))
            st(v.memset(e.guard[0:1, :], -7.0))
            v.wait_ge(ld, 16)
            st(v.tensor_copy(e.srcI[:, :], e.srt[:, :, F_SRC]))
            st(v.tensor_copy(e.dstI[:, :], e.srt[:, :, F_DST]))
            st(v.scalar_tensor_tensor(out=e.dloc[:, :], in0=e.blk[:, :], scalar=-float(P), in1=e.srt[:, :, F_DST],
                                      op0=ALU.mult, op1=ALU.add))
            st(v.tensor_tensor(e.asum[:, :, :], e.srt[:, :, F_A8:F_A8 + 8], e.srt[:, :, F_A8N:F_A8N + 8], ALU.add))
            v.wait_ge(dd, 96)
            st(v.tensor_tensor(e.pen[:, 0, :], e.seg3[:, 1, :], e.seg3[:, 0, :], ALU.is_equal))
            st(v.tensor_tensor(e.pen[:, 1, :], e.seg3[:, 1, :], e.seg3[:, 2, :], ALU.is_equal))
            st.settle()
            st(v.tensor_scalar(e.pen[:, :, :], e.pen[:, :, :], -1.0, BIG, ALU.add, ALU.mult))
            st.settle()
            st(v.tensor_reduce(e.whole[:, :], e.pen[:, :, :], AX.X, ALU.min))
            for h in range(16):
                st(v.tensor_copy(e.penF[:, h, :], e.pen[:, 0, :]))
                st(v.tensor_copy(e.penB[:, h, :], e.pen[:, 1, :]))
            st.settle()
            st(v.memset(e.penF[:, :, 0:1], -BIG))
            st(v.memset(e.penB[:, :, SEG - 1:SEG], -BIG))
            assert st.n >= e.ROWS_AT
            v.wait_ge(emb, 1)
            st(v.tensor_copy(e.wrow[0:16, :], e.ps[1][0:16, 0:2 * P]))
            st(v.memset(e.fac[:, :, :], 1.0))
            st.settle()
            for k in range(8):
                st(v.scalar_tensor_tensor(out=e.fack[:, :, :], in0=e.srt[:, :, F_TYPE:F_TYPE + 1].to_broadcast([P, NT, 8]),
                                          scalar=float(k), in1=e.emb[:, k:k + 1, :].to_broadcast([P, NT, 8]),
                                          op0=ALU.is_equal, op1=ALU.mult))
                st.settle()
                st(v.tensor_tensor(e.fac[:, :, :], e.fac[:, :, :], e.fack[:, :, :], ALU.add))
                st.settle()
            st(v.tensor_tensor(e.fac[:, :, :], e.fac[:, :, :], e.srt[:, :, F_W:F_W + 1].to_broadcast([P, NT, 8]), ALU.mult))
            st.settle()



def segment_softmax(e, name, H, floor_zero):
    nc = e.nc
    io, sv = e.sem(f"{name}_io"), e.sem(f"{name}_steps")
    turned, ex = e.sem(f"{name}_turned"), e.sem(f"{name}_exp")
    W = H * SEG
    A = e.segA[:, 0:W]
    Fw = e.segF[:, 0:W]
    A3 = A.rearrange("p (h j) -> p h j", h=H)
    F3 = Fw.rearrange("p (h j) -> p h j", h=H)
    penF = e.penF[:, 0:H, :].rearrange("p h j -> p (h j)")
    penB = e.penB[:, 0:H, :].rearrange("p h j -> p (h j)")
    marks = {}
    with nc.Block() as block:
        @block.vector
        def _(v):
            st = Steps(v, sv)
            v.wait_ge(io, 32)
            st(v.tensor_copy(e.edge0[:, 0:H], A3[:, :, 0]))
            st(v.tensor_tensor_scan(Fw, penF, A, -BIG, ALU.add, ALU.max))
            st.settle()
            st(v.tensor_copy(e.ends[:, 0:H], F3[:, :, SEG - 1]))
            marks["f"] = st.n
            st(v.memset(e.carry[0:H, 0:1], -BIG))
            v.wait_ge(turned, 1)
            st(v.tensor_tensor_scan(e.carry[0:H, 1:P + 1], e.wrow[0:H, 0:P], e.ps[0][0:H, 0:P], -BIG, ALU.add, ALU.max))
            marks["fc"] = st.n
            v.wait_ge(turned, 2)
            st(v.scalar_tensor_tensor(out=A3[:, :, 0], in0=e.ps[1][:, 0:H], scalar=e.pen[:, 0, 0:1], in1=e.edge0[:, 0:H],
                                      op0=ALU.add, op1=ALU.max))
            st.settle()
            st(v.tensor_tensor_scan(Fw, penF, A, -BIG, ALU.add, ALU.max))
            st.settle()
            st(v.tensor_copy(A3[:, :, 0], e.edge0[:, 0:H]))
            st(v.tensor_tensor_scan(e.segB[:, 0:W][:, ::-1], penB[:, ::-1], Fw[:, ::-1], -BIG, ALU.add, ALU.max))
            st.settle()
            st(v.tensor_copy(e.ends[:, 0:H], e.segB[:, 0:W].rearrange("p (h j) -> p h j", h=H)[:, :, 0]))
            marks["b"] = st.n
            st(v.memset(e.carry[0:H, P:P + 1], -BIG))
            v.wait_ge(turned, 3)
            st(v.tensor_tensor_scan(e.carry[0:H, 0:P][:, ::-1], e.wrow[0:H, P:2 * P][:, ::-1],
                                    e.ps[0][0:H, 0:P][:, ::-1], -BIG, ALU.add, ALU.max))
            marks["bc"] = st.n
            v.wait_ge(turned, 4)
            st(v.scalar_tensor_tensor(out=F3[:, :, SEG - 1], in0=e.ps[1][:, 0:H], scalar=e.pen[:, 1, SEG - 1:SEG],
                                      in1=F3[:, :, SEG - 1], op0=ALU.add, op1=ALU.max))
            st.settle()
            st(v.tensor_tensor_scan(e.segB[:, 0:W][:, ::-1], penB[:, ::-1], Fw[:, ::-1], -BIG, ALU.add, ALU.max))
            st.settle()
            if floor_zero:
                st(v.tensor_scalar(e.segB[:, 0:W], e.segB[:, 0:W], 0.0, None, ALU.max))
                st.settle()
            v.tensor_tensor(A, A, e.segB[:, 0:W], ALU.subtract).then_inc(ex, 1)

        @block.tensor
        def _(pe):
            for k, m in enumerate(("f", "fc", "b", "bc")):
                pe.wait_ge(sv, marks[m])
                if k % 2 == 0:
                    i = pe.transpose(e.ps[0][0:H, 0:P], e.ends[:, 0:H], e.ident[:, :])
                else:
                    a = 0 if k == 1 else 1
                    i = pe.transpose(e.ps[1][:, 0:H], e.carry[0:H, a:a + P], e.ident[0:H, 0:H])
                i.then_inc(turned, 1)

        @block.scalar
        def _(a):
            a.wait_ge(ex, 1)
            a.activation(A, A, ACT.Exp).then_inc(ex, 1)

        @block.sync
        def _(sp):
            sp.dma_start(e.rowd[0:H, 0:SLOTS].rearrange("h (a n) -> h a n", a=NI),
                         e.rowT[0:H, 0:SLOTS].rearrange("h (a n) -> h a n", a=NI)).then_inc(io, 16)
            sp.wait_ge(io, 16)
            sp.dma_start(A3, e.rowd[0:H, 0:SLOTS].rearrange("h (p j) -> p h j", p=P)).then_inc(io, 16)
            sp.wait_ge(ex, 2)
            sp.dma_start(e.rowd2[0:H, 0:SLOTS].rearrange("h (p j) -> p h j", p=P), A3).then_inc(io, 16)
            sp.wait_ge(io, 48)
            sp.dma_start(e.rowT[0:H, 0:SLOTS].rearrange("h (a n) -> h a n", a=NI),
                         e.rowd2[0:H, 0:SLOTS].rearrange("h (a n) -> h a n", a=NI)).then_inc(io, 16)
            sp.wait_ge(io, 64)


def gather_loop(g, e, name, fetches, free, got, extra=None):
    cols = e.sem(f"{name}_cols")
    K = len(fetches)

    def turn(it):
        for u in range(U):
            t = it * U + u
            hold(g, (free, t + 1))
            for k, (index, table, buf) in enumerate(fetches):
                g.tensor_copy(e.idx[:, k, u:u + 1], index[:, bass.ds(t, 1)]).then_inc(cols, 1)
            hold(g, (cols, t * K + K))
            for k, (index, table, buf) in enumerate(fetches):
                g.indirect_dma_start(buf[:, u, :], None, table[:, :],
                                     bass.IndirectOffsetOnAxis(ap=e.idx[:, k, u:u + 1], axis=0)).then_inc(got[k][u], 16)
            if extra:
                extra(g, it, u)
    turns(g, NI, turn)


def gather_sems(e, name, n):
    return [e.landed() for k in range(n)]


def row_transposes(pe, e, it, lg, H, lg_ready, ps, row_free, turned):
    hold(pe, (lg_ready, it + 1), (row_free, it))
    for u in range(U):
        i = pe.transpose(ps[0:H, u * P:(u + 1) * P], lg[:, u, 0:H], e.ident[:, :])
    i.then_inc(turned, 1)


def logits_l0(e):
    H, DH = 8, 64
    nc = e.nc
    got = gather_sems(e, "a0", 2)
    free, turned, rows = e.sem("a0_free"), e.sem("a0_turned"), e.sem("a0_rows")
    ready, st0 = e.sem("a0_ready"), e.sem("a0_steps")
    with nc.Block() as block:
        @block.gpsimd
        def _(g):
            gather_loop(g, e, "a0", [(e.srcI, e.tq, e.gb0), (e.dstI, e.tk, e.gb1)], free, got)

        @block.vector
        def _(v):
            v.sem_inc(free, U)
            def turn(it):
                for u in range(U):
                    hold(v, (got[0][u], it * 16 + 16), (got[1][u], it * 16 + 16))
                    v.tensor_tensor(e.gb2[:, u, :], e.gb0[:, u, :], e.gb1[:, u, :], ALU.mult).then_inc(free, 1)
                hold(v, (free, it * U + 2 * U), (turned, it))
                v.tensor_reduce(e.lg[:, :, 0:H], e.gb2[:, :, :].rearrange("p u (h d) -> p u h d", h=H), AX.X,
                                ALU.add).then_inc(st0, 1)
                hold(v, (st0, it + 1))
                v.tensor_tensor(e.lg[:, :, 0:H], e.lg[:, :, 0:H], e.asum[:, bass.ds(it * U, U), :], ALU.add).then_inc(ready, 1)
                hold(v, (ready, it + 1))
            turns(v, NI, turn)

        @block.tensor
        def _(pe):
            def turn(it):
                row_transposes(pe, e, it, e.lg, H, ready, e.ps[0], rows, turned)
            turns(pe, NI, turn)

        @block.scalar
        def _(a):
            def turn(it):
                hold(a, (turned, it + 1))
                a.activation(e.rowT[0:H, bass.ds(it * (U * P), U * P)], e.ps[0][0:H, :], ACT.Copy).then_inc(rows, 1)
            turns(a, NI, turn)

def weighted_sums(e, name, H, table):
    DH = D // H
    nc = e.nc
    got = gather_sems(e, name, 1) if table is not None else [[e.sem(f"{name}_got{u}") for u in range(U)]]
    free, rowin, wts = e.sem(f"{name}_free"), e.sem(f"{name}_rowin"), e.sem(f"{name}_weights")
    turned, oh, msg = e.sem(f"{name}_turned"), e.sem(f"{name}_marks"), e.sem(f"{name}_msgs")
    with nc.Block() as block:
        if table is not None:
            @block.gpsimd
            def _(g):
                gather_loop(g, e, name, [(e.srcI, table, e.gb0)], free, got)
        else:
            @block.sync
            def _(sp):
                def turn(it):
                    for u in range(U):
                        hold(sp, (free, it * U + (u + 1)))
                        sp.dma_start(e.gb0[:, u, :], e.vd[bass.ds((it * U + u) * P, P), :]).then_inc(got[0][u], 16)
                turns(sp, NI, turn)

        @block.scalar
        def _(a):
            def turn(it):
                hold(a, (turned, it))
                a.activation(e.rowb[0:H, :], e.rowT[0:H, bass.ds(it * (U * P), U * P)], ACT.Copy).then_inc(rowin, 1)
                hold(a, (turned, it + 1))
                a.activation(e.wt[:, bass.ds(it * U, U), 0:H], e.ps[7][:, 0:U * H].rearrange("p (u h) -> p u h", u=U),
                             ACT.Copy).then_inc(wts, 1)
            turns(a, NI, turn)

        @block.vector
        def _(v):
            def turn(it):
                hold(v, (wts, it + 1))
                for u in range(U):
                    hold(v, (got[0][u], it * 16 + 16), (free, it * U + (u + 1)))
                    v.tensor_scalar(e.oh[:, u, :], e.lane[:, :], e.dloc[:, bass.ds(it * U + u, 1)], None,
                                    ALU.is_equal).then_inc(oh, 1)
                    v.tensor_tensor(e.gb2[:, u, :].rearrange("p (h d) -> p h d", h=H),
                                    e.gb0[:, u, :].rearrange("p (h d) -> p h d", h=H),
                                    e.wt[:, bass.ds(it * U + u, 1), 0:H].rearrange("p a h -> p h a").to_broadcast([P, H, DH]),
                                    ALU.mult).then_inc(msg, 1)
            turns(v, NI, turn)

        @block.tensor
        def _(pe):
            for b in range(NB):
                pe.matmul(e.acc[:, b * D:(b + 1) * D], e.zeros[:, 0:P], e.zeros[:, :], start=True, stop=True)
            pe.matmul(e.ps[6][:, :], e.zeros[:, 0:P], e.zeros[:, :], start=True, stop=True)
            pe.sem_inc(free, U)
            def turn(it):
                hold(pe, (rowin, it + 1), (wts, it))
                for u in range(U):
                    i = pe.transpose(e.ps[7][:, u * H:(u + 1) * H], e.rowb[0:H, u * P:(u + 1) * P], e.ident[0:H, 0:H])
                i.then_inc(turned, 1)
                for u in range(U):
                    blk = pe.value_load(e.blki[0:1, bass.ds(it * U + u, 1)], min_val=0, max_val=NB - 1)
                    hold(pe, (oh, it * U + (u + 1)), (msg, it * U + (u + 1)))
                    pe.matmul(e.ps[6][:, bass.ds(blk * 16, H)], e.oh[:, u, :],
                              e.wt[:, bass.ds(it * U + u, 1), 0:H].rearrange("p a h -> p (a h)"), start=False, stop=True,
                              skip_group_check=True)
                    pe.matmul(e.acc[:, bass.ds(blk * D, D)], e.oh[:, u, :], e.gb2[:, u, :], start=False, stop=True,
                              skip_group_check=True).then_inc(free, 1)
            turns(pe, NI, turn)

def divide_sums(e, name, H, guard, bias=None):
    DH = D // H
    den = e.ps[6][:, 0:NB * 16].rearrange("p (b h) -> p b h", b=NB)[:, :, 0:H]
    with e.nc.Block() as block:
        @block.vector
        def _(v):
            st = Steps(v, e.sem(f"{name}_steps"))
            if guard == "add":
                st(v.tensor_scalar(e.rden[:, :, 0:H], den, 1e-10, None, ALU.add))
            else:
                st(v.tensor_scalar(e.rden[:, :, 0:H], den, 0.5, None, ALU.max))
            st(v.tensor_scalar(e.some[:, :], den[:, :, 0], 0.0, None, ALU.is_gt))
            st.settle()
            st(v.reciprocal(e.rden[:, :, 0:H], e.rden[:, :, 0:H]))
            st.settle()
            for b in range(NB):
                st(v.tensor_tensor(e.t0[:, b, :].rearrange("p (h d) -> p h d", h=H),
                                   e.acc[:, b * D:(b + 1) * D].rearrange("p (h d) -> p h d", h=H),
                                   e.rden[:, b, 0:H, None].to_broadcast([P, H, DH]), ALU.mult))
            st.settle()
            if bias is not None:
                for b in range(NB):
                    st(v.scalar_tensor_tensor(out=e.t0[:, b, :], in0=bias, scalar=e.some[:, b:b + 1], in1=e.t0[:, b, :],
                                              op0=ALU.mult, op1=ALU.add))
                st.settle()


def ffn(e):
    nc = e.nc
    M = 4 * D // P
    up, gel, down, got = e.sem("f_up"), e.sem("f_gelu"), e.sem("f_down"), e.sem("f_got")
    with nc.Block() as block:
        @block.tensor
        def _(pe):
            for m in range(M):
                for q, (a, b) in enumerate(((0, 512), (512, 640))):
                    k = 2 * m + q
                    if k >= 4:
                        pe.wait_ge(gel, k - 3)
                    for c in range(4):
                        i = pe.matmul(e.ps[k % 4][:, 0:b - a], e.W1[:, c, m * P:(m + 1) * P], e.hT[:, c, a:b],
                                      start=(c == 0), stop=(c == 3))
                    i.then_inc(up, 1)
            pe.wait_ge(gel, 2 * M)
            for b in range(NB):
                if b >= 4:
                    pe.wait_ge(got, b - 3)
                for m in range(M):
                    pe.matmul(e.ps[4 + b % 4][:, :], e.uT[:, m, b * P:(b + 1) * P], e.W2[:, m, :], start=(m == 0),
                              stop=False)
                pe.matmul(e.ps[4 + b % 4][:, :], e.ones[0:1, :], e.b2r[0:1, :], start=False, stop=True).then_inc(down, 1)

        @block.scalar
        def _(a_):
            for m in range(M):
                for q, (a, b) in enumerate(((0, 512), (512, 640))):
                    k = 2 * m + q
                    a_.wait_ge(up, k + 1)
                    a_.activation(e.uT[:, m, a:b], e.ps[k % 4][:, 0:b - a], ACT.Gelu, bias=e.b1c[:, m:m + 1]).then_inc(gel, 1)

        @block.vector
        def _(v):
            st = Steps(v, e.sem("f_steps"))
            for b in range(NB):
                st(v.tensor_tensor(e.x[:, b, :], e.x[:, b, :], e.h1[:, b, :], ALU.add))
            st.settle()
            for b in range(NB):
                v.wait_ge(down, b + 1)
                v.tensor_tensor(e.x[:, b, :], e.ps[4 + b % 4][:, :], e.x[:, b, :], ALU.add).then_inc(got, 1)



def l1_table(e):
    nc = e.nc
    turned, copied, summed, taken = (e.sem(f"u_{f}") for f in ("turned", "copied", "summed", "taken"))
    scale = 1.0 / math.sqrt(P) * SILU_2MOM / math.sqrt(64.0)
    with nc.Block() as block:
        @block.tensor
        def _(pe):
            for b in range(NB):
                if b >= 2:
                    pe.wait_ge(copied, b - 1)
                for c in range(4):
                    src = e.h[:, b, 0:P] if c == 0 else e.h[:, b, P:D].rearrange("p (u m) -> p m u", m=3)[:, c - 1, :]
                    i = pe.transpose(e.ps[b % 2][:, c * P:(c + 1) * P], src, e.ident[:, :])
                i.then_inc(turned, 1)
            for b in range(NB):
                pe.wait_ge(copied, b + 1)
                if b >= 2:
                    pe.wait_ge(taken, b - 1)
                for c in range(4):
                    i = pe.matmul(e.ps[2 + b % 2][:, c * P:(c + 1) * P], e.hT[:, c, b * P:(b + 1) * P],
                                  (e.Wup0 if c == 0 else e.Wup1)[:, :], start=True, stop=True)
                i.then_inc(summed, 1)

        @block.scalar
        def _(a):
            for b in range(NB):
                a.wait_ge(turned, b + 1)
                a.activation(e.hT[:, 0:4, b * P:(b + 1) * P], e.ps[b % 2].rearrange("p (c n) -> p c n", c=4),
                             ACT.Copy).then_inc(copied, 1)

        @block.vector
        def _(v):
            for b in range(NB):
                v.wait_ge(summed, b + 1)
                v.tensor_scalar(e.t0[:, b, :], e.ps[2 + b % 2][:, :], scale, None, ALU.mult).then_inc(taken, 1)


SILU_2MOM = 1.679177


def l1_mlp(e):
    nc = e.nc
    sems = {f: e.sem(f"m_{f}") for f in ("fin", "ft", "ftc", "mm1", "a1", "mm2", "a2", "mm3", "a3")}
    with nc.Block() as block:
        @block.scalar
        def _(a):
            def turn(it):
                hold(a, (sems["ft"], it))
                a.activation(e.fin[:, :, :], e.srt[:, bass.ds(it * U, U), F_A8:F_A8 + 8], ACT.Copy).then_inc(sems["fin"], 1)
                hold(a, (sems["ft"], it + 1), (sems["mm1"], it))
                a.activation(e.fT[0:8, :], e.ps[0][0:8, :], ACT.Copy).then_inc(sems["ftc"], 1)
                hold(a, (sems["mm1"], it + 1), (sems["mm2"], it))
                a.activation(e.hh1[0:64, :], e.ps[1][0:64, :], ACT.Silu, scale=1.0 / math.sqrt(8.0)).then_inc(sems["a1"], 1)
                hold(a, (sems["mm2"], it + 1), (sems["mm3"], it))
                a.activation(e.hh2[0:64, :], e.ps[2][0:64, :], ACT.Silu, scale=SILU_2MOM / 8.0).then_inc(sems["a2"], 1)
                hold(a, (sems["mm3"], it + 1))
                a.activation(e.h3[0:64, bass.ds(it * (U * P), U * P)], e.ps[3][0:64, :], ACT.Silu,
                             scale=SILU_2MOM / 8.0).then_inc(sems["a3"], 1)
            turns(a, NI, turn)

        @block.tensor
        def _(pe):
            def turn(it):
                hold(pe, (sems["fin"], it + 1), (sems["ftc"], it))
                for u in range(U):
                    i = pe.transpose(e.ps[0][0:8, u * P:(u + 1) * P], e.fin[:, u, :], e.ident[:, :])
                i.then_inc(sems["ft"], 1)
                hold(pe, (sems["ftc"], it + 1), (sems["a1"], it))
                pe.matmul(e.ps[1][0:64, :], e.Wm1[0:8, :], e.fT[0:8, :], start=True, stop=True).then_inc(sems["mm1"], 1)
                hold(pe, (sems["a1"], it + 1), (sems["a2"], it))
                pe.matmul(e.ps[2][0:64, :], e.Wm2[0:64, :], e.hh1[0:64, :], start=True, stop=True).then_inc(sems["mm2"], 1)
                hold(pe, (sems["a2"], it + 1), (sems["a3"], it))
                pe.matmul(e.ps[3][0:64, :], e.Wm3[0:64, :], e.hh2[0:64, :], start=True, stop=True).then_inc(sems["mm3"], 1)
            turns(pe, NI, turn)

def l1_pass(e, name, second):
    nc = e.nc
    got = gather_sems(e, name, 1)
    free, hr, w, msg = (e.sem(f"{name}_{f}") for f in ("free", "hid", "w", "msg"))
    scaled = e.sem(f"{name}_scaled")
    W4 = e.Wm4[0:64, :].rearrange("p (a b n) -> p a b n", a=2, b=2)[:, :, 1 if second else 0, :]
    K = 6 if second else 3

    def y(t, m):
        return e.srt[:, bass.ds(t, 1), F_A4 + m:F_A4 + m + 1].rearrange("p a f -> p (a f)")

    with nc.Block() as block:
        @block.gpsimd
        def _(g):
            def hidden(g, it, u):
                g.tensor_copy(e.h3r[0:64, u, :], e.h3[0:64, bass.ds((it * U + u) * P, P)]).then_inc(hr, 1)
            gather_loop(g, e, name, [(e.srcI, e.ts, e.gb0)], free, got, hidden)

        @block.scalar
        def _(a):
            if second:
                def turn(it):
                    for u in range(U):
                        hold(a, (msg, it * (K * U) + (K * u + 2)))
                        for m in range(3):
                            i = a.activation(e.gb2[:, u, m * P:(m + 1) * P], e.t2[:, u, :], ACT.Copy,
                                             scale=y(it * U + u, m + 1))
                        i.then_inc(scaled, 1)
                turns(a, NI, turn)

        @block.vector
        def _(v):
            def turn(it):
                for u in range(U):
                    t = it * U + u
                    at = it * (K * U) + K * u
                    hold(v, (got[0][u], it * 16 + 16), (free, it * U + (u + 1)), (w, it * U + (u + 1)))
                    ps = e.ps[5 + u % 3]
                    s0, s1 = e.gb0[:, u, 0:P], e.gb0[:, u, P:D]
                    if not second:
                        v.tensor_scalar(e.oh[:, u, :], e.lane[:, :], e.dloc[:, bass.ds(t, 1)], y(t, 0), ALU.is_equal,
                                        ALU.mult).then_inc(msg, 1)
                        v.tensor_tensor(e.gb2[:, u, 0:P], s0, ps[:, 0:P], ALU.mult).then_inc(msg, 1)
                        v.tensor_tensor(e.gb2[:, u, P:D].rearrange("p (m n) -> p m n", m=3),
                                        s1.rearrange("p (m n) -> p m n", m=3),
                                        ps[:, None, P:2 * P].to_broadcast([P, 3, P]), ALU.mult).then_inc(msg, 1)
                    else:
                        v.tensor_scalar(e.oh[:, u, :], e.lane[:, :], e.dloc[:, bass.ds(t, 1)], None,
                                        ALU.is_equal).then_inc(msg, 1)
                        v.tensor_tensor(e.t2[:, u, :], s0, ps[:, 0:P], ALU.mult).then_inc(msg, 1)
                        v.tensor_scalar(e.dot[:, 0, :], s1[:, 0:P], y(t, 1), None, ALU.mult).then_inc(msg, 1)
                        hold(v, (msg, at + 3))
                        v.scalar_tensor_tensor(out=e.dot[:, 1, :], in0=s1[:, P:2 * P], scalar=y(t, 2), in1=e.dot[:, 0, :],
                                               op0=ALU.mult, op1=ALU.add).then_inc(msg, 1)
                        hold(v, (msg, at + 4))
                        v.scalar_tensor_tensor(out=e.dot[:, 2, :], in0=s1[:, 2 * P:3 * P], scalar=y(t, 3), in1=e.dot[:, 1, :],
                                               op0=ALU.mult, op1=ALU.add).then_inc(msg, 1)
                        hold(v, (msg, at + 5))
                        v.scalar_tensor_tensor(out=e.gb2[:, u, 3 * P:D], in0=e.dot[:, 2, :], scalar=1.0 / math.sqrt(3.0),
                                               in1=ps[:, P:2 * P], op0=ALU.mult, op1=ALU.mult).then_inc(msg, 1)
            turns(v, NI, turn)

        @block.tensor
        def _(pe):
            for b in range(NB):
                pe.matmul(e.acc[:, b * D:(b + 1) * D], e.zeros[:, 0:P], e.zeros[:, :], start=True, stop=True)
            pe.sem_inc(free, U)
            def turn(it):
                def radial(u):
                    hold(pe, (hr, it * U + (u + 1)), (msg, it * (K * U) + (K if u == 3 else 0)))
                    pe.matmul(e.ps[5 + u % 3][:, 0:2 * P], e.h3r[0:64, u, :], W4, start=True, stop=True).then_inc(w, 1)
                for u in range(3):
                    radial(u)
                for u in range(U):
                    blk = pe.value_load(e.blki[0:1, bass.ds(it * U + u, 1)], min_val=0, max_val=NB - 1)
                    hold(pe, (msg, it * (K * U) + K * (u + 1)), *([(scaled, it * U + (u + 1))] if second else []))
                    pe.matmul(e.acc[:, bass.ds(blk * D, D)], e.oh[:, u, :], e.gb2[:, u, :], start=False, stop=True,
                              skip_group_check=True).then_inc(free, 1)
                    if u == 0:
                        radial(3)
            turns(pe, NI, turn)

def take_sums(e, name, dst):
    taken = e.sem(f"{name}_taken")
    with e.nc.Block() as block:
        @block.vector
        def _(v):
            for b in range(NB):
                v.tensor_copy(dst[:, b, :], e.acc[:, b * D:(b + 1) * D]).then_inc(taken, 1)
            v.wait_ge(taken, NB)


def l1_out(e, first, second):
    nc = e.nc
    turned, copied, summed, taken = (e.sem(f"o_{f}") for f in ("turned", "copied", "summed", "taken"))
    scale = 1.0 / math.sqrt(2.0 * P) / 10.0
    with nc.Block() as block:
        @block.tensor
        def _(pe):
            for b in range(NB):
                for q, t in enumerate((first, second)):
                    k = 2 * b + q
                    if k >= 2:
                        pe.wait_ge(copied, k - 1)
                    for c in range(4):
                        i = pe.transpose(e.ps[k % 2][:, c * P:(c + 1) * P], t[:, b, c * P:(c + 1) * P], e.ident[:, :])
                    i.then_inc(turned, 1)
            for b in range(NB):
                pe.wait_ge(copied, 2 * b + 2)
                if b >= 2:
                    pe.wait_ge(taken, 2 * b - 2)
                ps = e.ps[2 + b % 2]
                for c, (k0, k1, W) in enumerate(((0, 7, e.Wo0), (4, 1, e.Wo1), (5, 2, e.Wo1), (6, 3, e.Wo1))):
                    pe.matmul(ps[:, c * P:(c + 1) * P], e.dT[:, k0, b * P:(b + 1) * P], W[:, 0, :], start=True, stop=False)
                    i = pe.matmul(ps[:, c * P:(c + 1) * P], e.dT[:, k1, b * P:(b + 1) * P], W[:, 1, :], start=False, stop=True)
                i.then_inc(summed, 1)

        @block.scalar
        def _(a):
            for b in range(NB):
                for q in range(2):
                    k = 2 * b + q
                    a.wait_ge(turned, k + 1)
                    a.activation(e.dT[:, 4 * q:4 * q + 4, b * P:(b + 1) * P], e.ps[k % 2].rearrange("p (c n) -> p c n", c=4),
                                 ACT.Copy).then_inc(copied, 1)

        @block.vector
        def _(v):
            for b in range(NB):
                v.wait_ge(summed, b + 1)
                ps = e.ps[2 + b % 2]
                v.scalar_tensor_tensor(out=e.x[:, b, 0:P], in0=ps[:, 0:P], scalar=scale, in1=e.x[:, b, 0:P],
                                       op0=ALU.mult, op1=ALU.add).then_inc(taken, 1)
                xv = e.x[:, b, P:D].rearrange("p (n m) -> p m n", m=3)
                v.scalar_tensor_tensor(out=xv, in0=ps[:, P:D].rearrange("p (m n) -> p m n", m=3), scalar=scale, in1=xv,
                                       op0=ALU.mult, op1=ALU.add).then_inc(taken, 1)



def l2_edges(e):
    H, HD = 16, 32
    nc = e.nc
    name = "e2"
    got = gather_sems(e, name, 2)
    egot = e.landed()
    vst = [e.sem(f"{name}_vst{u}") for u in range(U)]
    (free, ta, eac, m1, added, st, vare, sdr, norm, xnr, tx, rl, m2k, m2v, vo, lgr, rt, rc) = (
        e.sem(f"{name}_{f}") for f in ("free", "ta", "eac", "m1", "added", "steps", "vare", "sd", "norm", "xn", "tx",
                                       "relu", "m2k", "m2v", "vout", "logits", "rowt", "rowc"))
    M1 = e.psum[:, 512:1536]
    LN = 6
    PR = 2

    class T:

        def __init__(self, it, off):
            self.n, self.u, self.turn = it * U + off, off % U, it + off // U
            self.r = off % 2

    def steps_loop(eng, head, body, tail):
        head()
        def turn(it):
            for u in range(U):
                body(T(it, u + 2), T(it, u + 1), T(it, u))
        turns(eng, (NT - 4) // U, turn)
        for s in (NT - 3, NT - 2):
            body(T(0, s + 1), T(0, s), T(0, s - 1))
        tail(T(0, NT - 1), T(0, NT - 2))

    with nc.Block() as block:
        @block.gpsimd
        def _(g):
            def attr(g, it, u):
                g.dma_start(e.ea[:, u, :], e.rec[bass.ds((it * U + u) * P, P), RS:RW]).then_inc(egot[u], 16)
            gather_loop(g, e, name, [(e.srcI, e.tkv, e.gkv), (e.dstI, e.tq2, e.qg)], free, got, attr)

        @block.sync
        def _(sp):
            def turn(it):
                for u in range(U):
                    hold(sp, (vo, it * U + (u + 1)))
                    sp.dma_start(e.vd[bass.ds((it * U + u) * P, P), :], e.vout[:, u, :]).then_inc(vst[u], 16)
            turns(sp, NI, turn)
            for u in range(U):
                sp.wait_ge(vst[u], 16 * NI)

        @block.tensor
        def _(pe):
            def first(t):
                hold(pe, (egot[t.u], t.turn * 16 + 16))
                pe.transpose(e.ps[0][:, t.u * P:(t.u + 1) * P], e.ea[:, t.u, :], e.ident[:, :]).then_inc(ta, 1)
                hold(pe, (eac, t.n + 1), (added, t.n))
                pe.matmul(e.ps[1][:, :], e.eaT[:, t.u, :], e.hkW1e[:, :], start=True, stop=True)
                pe.matmul(e.ps[2][:, :], e.eaT[:, t.u, :], e.hvW1e[:, :], start=True, stop=True).then_inc(m1, 1)

            def second(t):
                hold(pe, (xnr, t.n + 1), (rl, t.n))
                for c in range(8):
                    i = pe.transpose(e.ps[3 + c // 4][:, c % 4 * P:(c % 4 + 1) * P], e.hid[:, t.r, c * P:(c + 1) * P], e.ident[:, :])
                i.then_inc(tx, 1)
                hold(pe, (rl, t.n + 1), (lgr, t.n * (PR + 1)))
                for c in range(4):
                    i = pe.matmul(e.ps[5][:, :], e.hTe[:, t.r, c * P:(c + 1) * P], e.hkW2[:, c, :], start=(c == 0), stop=(c == 3))
                i.then_inc(m2k, 1)
                hold(pe, (vo, t.n))
                for c in range(4):
                    i = pe.matmul(e.ps[6][:, :], e.hTe[:, t.r, (4 + c) * P:(5 + c) * P], e.hvW2[:, c, :], start=(c == 0), stop=(c == 3))
                i.then_inc(m2v, 1)

            def row(t):
                hold(pe, (lgr, t.n * (PR + 1) + (PR + 1)), (rc, t.n))
                pe.transpose(e.ps[7][0:H, t.u * P:(t.u + 1) * P], e.lg[:, t.u, 0:H], e.ident[:, :]).then_inc(rt, 1)

            pe.sem_inc(tx, 2)

            def head():
                first(T(0, 0))
                first(T(0, 1))
                second(T(0, 0))

            def body(t1, t0, tb):
                first(t1)
                second(t0)
                row(tb)

            def tail(t0, tb):
                second(t0)
                row(tb)
                row(t0)
            steps_loop(pe, head, body, tail)

        @block.scalar
        def _(a):
            def turned_in(t):
                hold(a, (ta, t.n + 1))
                a.activation(e.eaT[:, t.u, :], e.ps[0][:, t.u * P:(t.u + 1) * P], ACT.Copy).then_inc(eac, 1)

            def norm_in(t):
                hold(a, (vare, t.n + 1))
                a.activation(e.sd2[:, t.r, :], e.va2[:, t.r, :], ACT.Sqrt).then_inc(sdr, 1)
                hold(a, (norm, t.n + 1))
                for k in range(2):
                    i = a.activation(e.hid[:, t.r, k * D:(k + 1) * D], e.hid[:, t.r, k * D:(k + 1) * D], ACT.Identity,
                                     scale=e.rs2[:, t.r, k:k + 1], bias=e.nb2[:, t.r, k:k + 1])
                i.then_inc(xnr, 1)

            def relu_in(t):
                hold(a, (tx, t.n + 3))
                for c in range(8):
                    i = a.activation(e.hTe[:, t.r, c * P:(c + 1) * P], e.ps[3 + c // 4][:, c % 4 * P:(c % 4 + 1) * P], ACT.Relu,
                                     scale=e.gkvc[:, c:c + 1], bias=e.bkvc[:, c:c + 1])
                i.then_inc(rl, 1)

            def value_out(t):
                hold(a, (m2v, t.n + 1), (vst[t.u], t.turn * 16))
                a.activation(e.vout[:, t.u, :], e.ps[6][:, :], ACT.Copy).then_inc(vo, 1)

            def row_out(t):
                hold(a, (rt, t.n + 1))
                a.activation(e.rowT[0:H, bass.ds(t.n * P, P)], e.ps[7][0:H, t.u * P:(t.u + 1) * P], ACT.Copy).then_inc(rc, 1)

            def head():
                turned_in(T(0, 0))
                norm_in(T(0, 0))
                turned_in(T(0, 1))
                relu_in(T(0, 0))
                norm_in(T(0, 1))
                value_out(T(0, 0))

            def body(t1, t0, tb):
                turned_in(t1)
                relu_in(t0)
                norm_in(t1)
                value_out(t0)
                row_out(tb)

            def tail(t0, tb):
                relu_in(t0)
                value_out(t0)
                row_out(tb)
                row_out(t0)
            steps_loop(a, head, body, tail)

        @block.vector
        def _(v):
            def norms(t):
                at = t.n * LN
                hold(v, (m1, t.n + 1), (got[0][t.u], t.turn * 16 + 16), (tx, t.n + 1))
                hid = e.hid[:, t.r, :]
                v.tensor_tensor(hid, M1, e.gkv[:, t.u, :], ALU.add).then_inc(added, 1)
                hold(v, (added, t.n + 1))
                for k in range(2):
                    v.bn_stats(e.st2[:, t.r, k, :], hid[:, k * D:(k + 1) * D]).then_inc(st, 1)
                hold(v, (st, at + 2))
                for k in range(2):
                    v.bn_aggr(e.mv2[:, t.r, k, :], e.st2[:, t.r, k, :]).then_inc(st, 1)
                hold(v, (st, at + 4))
                v.tensor_scalar(e.va2[:, t.r, :], e.mv2[:, t.r, :, 1], EPS, None, ALU.add).then_inc(vare, 1)
                hold(v, (sdr, t.n + 1))
                v.reciprocal(e.rs2[:, t.r, :], e.sd2[:, t.r, :]).then_inc(st, 2)
                hold(v, (st, at + 6))
                v.scalar_tensor_tensor(out=e.nb2[:, t.r, :], in0=e.mv2[:, t.r, :, 0], scalar=-1.0, in1=e.rs2[:, t.r, :],
                                       op0=ALU.mult, op1=ALU.mult).then_inc(norm, 1)

            def product(t):
                at = t.n * (PR + 1)
                hold(v, (m2k, t.n + 1), (got[1][t.u], t.turn * 16 + 16), (rt, t.turn * U))
                v.tensor_tensor(e.prod[:, :], e.ps[5][:, :], e.qg[:, t.u, 0:D], ALU.mult).then_inc(lgr, 1)
                hold(v, (lgr, at + 1))
                v.tensor_reduce(e.lg[:, t.u, 0:H], e.prod.rearrange("p (h d) -> p h d", h=H), AX.X, ALU.add).then_inc(lgr, 1)
                hold(v, (lgr, at + 2))
                v.tensor_tensor(e.lg[:, t.u, 0:H], e.lg[:, t.u, 0:H], e.qg[:, t.u, D:D + H], ALU.add).then_inc(lgr, 1)
                hold(v, (lgr, at + 3))
                v.sem_inc(free, 1)

            v.sem_inc(free, U)

            def head():
                norms(T(0, 0))
                norms(T(0, 1))
                product(T(0, 0))

            def body(t1, t0, tb):
                norms(t1)
                product(t0)

            def tail(t0, tb):
                product(t0)
            steps_loop(v, head, body, tail)


def logits_l3(e):
    H = 8
    nc = e.nc
    got = gather_sems(e, "a3", 2)
    free, turned, rows, ready, st = (e.sem(f"a3_{f}") for f in ("free", "turned", "rows", "ready", "steps"))
    with nc.Block() as block:
        @block.gpsimd
        def _(g):
            gather_loop(g, e, "a3", [(e.srcI, e.tes, e.sg), (e.dstI, e.ted, e.dg)], free, got)

        @block.vector
        def _(v):
            v.sem_inc(free, U)
            def turn(it):
                hold(v, *[(got[k][u], it * 16 + 16) for k in range(2) for u in range(U)])
                hold(v, (turned, it))
                v.tensor_tensor(e.lg2[:, :, :], e.sg[:, :, :], e.dg[:, :, :], ALU.add).then_inc(st, 1)
                hold(v, (st, it * 2 + 1))
                v.sem_inc(free, U)
                v.scalar_tensor_tensor(out=e.lg3[:, :, :], in0=e.lg2[:, :, :], scalar=0.2, in1=e.lg2[:, :, :],
                                       op0=ALU.mult, op1=ALU.max).then_inc(st, 1)
                hold(v, (st, it * 2 + 2))
                v.tensor_tensor(e.lg[:, :, 0:H], e.lg3[:, :, :], e.fac[:, bass.ds(it * U, U), :], ALU.mult).then_inc(ready, 1)
                hold(v, (ready, it + 1))
            turns(v, NI, turn)

        @block.tensor
        def _(pe):
            def turn(it):
                row_transposes(pe, e, it, e.lg, H, ready, e.ps[0], rows, turned)
            turns(pe, NI, turn)

        @block.scalar
        def _(a):
            def turn(it):
                hold(a, (turned, it + 1))
                a.activation(e.rowT[0:H, bass.ds(it * (U * P), U * P)], e.ps[0][0:H, :], ACT.Copy).then_inc(rows, 1)
            turns(a, NI, turn)

def load(e, name, pairs):
    done = e.sem(f"{name}_loaded")
    with e.nc.Block() as block:
        @block.sync
        def _(sp):
            for tile, src in pairs:
                sp.dma_start(tile, src, allow_slow_non_contiguous=True).then_inc(done, 16)
            sp.wait_ge(done, 16 * len(pairs))


def rows(w):
    return w.rearrange("(c p) n -> p c n", p=P)


def column(b):
    return b.rearrange("(c p) -> p c", p=P)


def line(b):
    return b.rearrange("(a n) -> a n", a=1)


def spread(b):
    return line(b).to_broadcast([P, b.shape[0]])


def program(nc, i, out):
    ctx = ExitStack()
    e = Env()
    e.nc = nc
    with ctx:
        uses = {}

        def sb(name, shape, dt=F32, scope=ctx):
            uses[name] = uses.get(name, 0) + 1
            t = scope.enter_context(nc.sbuf_tensor(f"{name}_{uses[name]}", shape, dt))
            return t

        sems = Env()
        sems.scope, sems.held = ctx.enter_context(ExitStack()), []

        def sem(name):
            handle = sems.scope.enter_context(nc.semaphore(name))
            sems.held.append(handle)
            return handle
        e.sem = sem
        sems.landed = [ctx.enter_context(nc.semaphore(f"landed{k}")) for k in range(12 * U)]
        sems.lent = 0

        def landed():
            sems.lent += U
            return sems.landed[sems.lent - U:sems.lent]
        e.landed = landed

        def renew():
            with nc.Block() as block:
                @block.gpsimd
                def _(g):
                    for handle in sems.held:
                        g.sem_clear(handle)
            sems.scope.close()
            sems.held.clear()

        def table(name, n, w):
            return nc.dram_tensor(f"d_{name}", [n, w], F32).ap()

        NN = NB * P
        e.rec = table("rec", SLOTS, RW)
        e.dstd = table("dstd", SLOTS + 2, 1)
        e.rowd = table("rowd", 16, SLOTS)
        e.rowd2 = table("rowd2", 16, SLOTS)
        e.vd = table("vd", SLOTS, D)
        e.tq = table("tq", NN, D)
        e.tk = table("tk", NN, D)
        e.tv = table("tv", NN, D)
        e.ts = table("ts", NN, D)
        e.th = table("th", NN, D)
        e.tkv = table("tkv", NN, 2 * D)
        e.tq2 = table("tq2", NN, D + 16)
        e.tes = table("tes", NN, 8)
        e.ted = table("ted", NN, 8)

        e.psum = ctx.enter_context(nc.psum_tensor("psum", [P, 8 * 512], F32))
        e.ps = [e.psum[:, k * 512:(k + 1) * 512] for k in range(8)]
        e.acc = e.psum[:, 0:ACC]

        e.x = sb("x", [P, NB, D])
        e.h = sb("h", [P, NB, D])
        e.t0 = sb("t0", [P, NB, D])
        e.hT = sb("hT", [P, 4, NB * P])
        e.ident = sb("ident", [P, P])
        e.ones = sb("ones", [P, P])
        e.zeros = sb("zeros", [P, 512])
        e.lane = sb("lane", [P, P])
        e.srcI = sb("srcI", [P, NT], I32)
        e.dstI = sb("dstI", [P, NT], I32)
        e.blki = sb("blki", [P, NT], I32)
        e.dloc = sb("dloc", [P, NT])
        e.asum = sb("asum", [P, NT, 8])
        e.fac = sb("fac", [P, NT, 8])
        e.srt = sb("srt", [P, NT, RS])
        e.pen = sb("pen", [P, 2, SEG])
        e.penF = sb("penF", [P, 16, SEG])
        e.penB = sb("penB", [P, 16, SEG])
        e.wrow = sb("wrow", [16, 2 * P])
        e.stats = sb("stats", [P, NB, 6])
        e.mv = sb("mv", [P, NB, 2])
        e.vare = sb("vare", [P, NB])
        e.sd = sb("sd", [P, NB])
        e.rstd = sb("rstd", [P, NB])
        e.nbias = sb("nbias", [P, NB])
        e.rden = sb("rden", [P, NB, 16])
        e.some = sb("some", [P, NB])
        e.idx = sb("idx", [P, 2, U], I32)
        e.lg = sb("lg", [P, U, 16])
        e.oh = sb("oh", [P, U, P])
        e.edge0 = sb("edge0", [P, 16])
        e.ends = sb("ends", [P, 16])
        e.carry = sb("carry", [16, P + 1])

        with ExitStack() as sc:
            e.PK = 12
            e.lower = sb("lower", [P, P], F32, sc)
            e.lowerb = sb("lowerb", [P, P], BF16, sc)
            e.window = sb("window", [P, 2 * EC], F32, sc)
            e.nodeno = sb("nodeno", [P, NB * P], F32, sc)
            e.tile_at = sb("tile_at", [P, NT], F32, sc)
            e.onesb = sb("onesb", [P, P], BF16, sc)
            e.zerosb = sb("zerosb", [P, 512], BF16, sc)
            e.phantom = sb("phantom", [P, e.PK, RW], F32, sc)
            e.srcs = sb("srcs", [EP, EC], I32, sc)
            e.dsts = sb("dsts", [EP, EC], I32, sc)
            e.kinds = sb("kinds", [EP, EC], I32, sc)
            e.weights = sb("weights", [EP, EC], F32, sc)
            e.a4 = sb("a4", [EP, EC, 4], F32, sc)
            e.a8 = sb("a8", [EP, EC, 8], F32, sc)
            e.a8n = sb("a8n", [EP, EC, 8], F32, sc)
            e.a128 = sb("a128", [EP, EC, P], F32, sc)
            e.small = sb("small", [EP, EC, RS], F32, sc)
            e.dstf = sb("dstf", [EP, EC], F32, sc)
            e.mark = sb("mark", [EP, U, NB * P], BF16, sc)
            e.cnt = sb("cnt", [P, NB * P], F32, sc)
            e.base = sb("base", [P, NB * P], F32, sc)
            e.bsum = sb("bsum", [P, NB], F32, sc)
            e.bsumi = sb("bsumi", [P, NB], I32, sc)
            e.btile = sb("btile", [P, NB], I32, sc)
            e.bsize = sb("bsize", [P, NB], F32, sc)
            e.bend = sb("bend", [P, NB], F32, sc)
            e.bstart = sb("bstart", [P, NB], F32, sc)
            e.blk = sb("blk", [P, NT], F32, sc)
            e.junk = sb("junk", [EP, 2, NB * P], F32, sc)
            e.slota = sb("slota", [EP, EC], F32, sc)
            e.slotb = sb("slotb", [EP, EC], F32, sc)
            e.sloti = sb("sloti", [EP, EC], I32, sc)
            e.recbuf = sb("recbuf", [EP, U, RW], F32, sc)
            e.slotbuf = sb("slotbuf", [EP, U], I32, sc)
            e.dstT = sb("dstT", [P, P], F32, sc)
            e.guard = sb("guard", [1, 2], F32, sc)
            e.seg3 = sb("seg3", [P, 3, SEG], F32, sc)
            e.whole = sb("whole", [P, 2], F32, sc)
            e.fack = sb("fack", [P, NT, 8], F32, sc)
            e.emb = sb("emb", [P, 8, 8], F32, sc)
            e.loads0 = [(e.emb.rearrange("p k h -> p (k h)"),
                         i["L3_gnn_et_emb"].rearrange("k (h a) -> a (k h)", a=1).to_broadcast([P, 64]))]
            e.ROWS_AT = 42
            prepare(e, i)
            lowb = e.sem("lowb")
            with nc.Block() as block:
                @block.vector
                def _(v):
                    v.tensor_copy(e.lowerb[:, :], e.lower[:, :]).then_inc(lowb, 1)
                    v.wait_ge(lowb, 1)
            count_edges(e)
            place_edges(e)
            scatter_records(e)
            load_sorted(e)

        renew()
        with ExitStack() as sc:
            e.h1 = sb("h1", [P, NB, D], F32, sc)
            e.g1c = sb("g1c", [P, 4], F32, sc)
            e.b1lc = sb("b1lc", [P, 4], F32, sc)
            e.g2c = sb("g2c", [P, 4], F32, sc)
            e.b2lc = sb("b2lc", [P, 4], F32, sc)
            with ExitStack() as s2:
                e.Wqkv = sb("Wqkv", [P, 4, 3 * D], F32, s2)
                e.bqkv = sb("bqkv", [1, 3 * D], F32, s2)
                e.tq_ = sb("tq_", [P, NB, D], F32, s2)
                e.tk_ = sb("tk_", [P, NB, D], F32, s2)
                e.tv_ = sb("tv_", [P, NB, D], F32, s2)
                load(e, "w0a", [(e.Wqkv[:, :, :], rows(i["L0_gnn_Wqkv"])), (e.bqkv[:, :], line(i["L0_gnn_bqkv"])),
                                (e.g1c[:, :], column(i["L0_gnn_ln1_g"])), (e.b1lc[:, :], column(i["L0_gnn_ln1_b"])),
                                (e.g2c[:, :], column(i["L0_gnn_ln2_g"])), (e.b2lc[:, :], column(i["L0_gnn_ln2_b"]))])
                node_ln(e, "n0", e.x, e.h, ACT.Relu)

                def evac0(v, b, n, ps):
                    if n == 0:
                        return v.tensor_scalar(e.tq_[:, b, :], ps[:, :], float(D) ** -0.5, None, ALU.mult)
                    return v.tensor_copy((e.tk_, e.tv_)[n - 1][:, b, :], ps[:, :])
                node_linear(e, "qkv", [e.t0], e.hT, (e.g1c, e.b1lc), ACT.Identity,
                            [(e.Wqkv[:, :, n * D:(n + 1) * D], e.bqkv[0:1, n * D:(n + 1) * D]) for n in range(3)],
                            evac0, ln=(e.h, e.t0))
                store_table(e, "t0", [(e.tq, e.tq_[:, :, :]), (e.tk, e.tk_[:, :, :]), (e.tv, e.tv_[:, :, :])])
            with ExitStack() as s2:
                edge_buffers(e, sb, s2)
                e.gb1 = sb("gb1", [P, U, D], F32, s2)
                logits_l0(e)
                segment_softmax(e, "s0", 8, False)
                weighted_sums(e, "b0", 8, e.tv)
                divide_sums(e, "d0", 8, "max")
            with ExitStack() as s2:
                e.Wo = sb("Wo", [P, 4, D], F32, s2)
                e.bor = sb("bor", [1, D], F32, s2)
                e.W1 = sb("W1", [P, 4, 4 * D], F32, s2)
                e.b1c = sb("b1c", [P, 16], F32, s2)
                e.W2 = sb("W2", [P, 16, D], F32, s2)
                e.b2r = sb("b2r", [1, D], F32, s2)
                e.uT = sb("uT", [P, 16, NB * P], F32, s2)
                load(e, "w0b", [(e.Wo[:, :, :], rows(i["L0_gnn_Wo"])), (e.bor[:, :], line(i["L0_gnn_bo"])),
                                (e.W1[:, :, :], rows(i["L0_gnn_W1"])), (e.b1c[:, :], column(i["L0_gnn_b1"])),
                                (e.W2[:, :, :], rows(i["L0_gnn_W2"])), (e.b2r[:, :], line(i["L0_gnn_b2"]))])
                node_linear(e, "wo", [e.t0], e.hT, None, ACT.Copy, [(e.Wo[:, :, :], e.bor[0:1, :])],
                            lambda v, b, n, ps: v.tensor_tensor(e.h1[:, b, :], ps[:, :], e.h[:, b, :], ALU.add))
                node_linear(e, "ln2", [e.t0], e.hT, (e.g2c, e.b2lc), ACT.Identity, [], None, ln=(e.h1, e.t0))
                ffn(e)

        renew()
        with ExitStack() as sc:
            edge_buffers(e, sb, sc, rows_too=False)
            e.Wup0 = sb("Wup0", [P, P], F32, sc)
            e.Wup1 = sb("Wup1", [P, P], F32, sc)
            e.Wm1 = sb("Wm1", [8, 64], F32, sc)
            e.Wm2 = sb("Wm2", [64, 64], F32, sc)
            e.Wm3 = sb("Wm3", [64, 64], F32, sc)
            e.Wm4 = sb("Wm4", [64, 512], F32, sc)
            e.Wo0 = sb("Wo0", [P, 2, P], F32, sc)
            e.Wo1 = sb("Wo1", [P, 2, P], F32, sc)
            e.fin = sb("fin", [P, U, 8], F32, sc)
            e.fT = sb("fT", [8, 512], F32, sc)
            e.hh1 = sb("hh1", [64, 512], F32, sc)
            e.hh2 = sb("hh2", [64, 512], F32, sc)
            e.h3 = sb("h3", [64, SLOTS], F32, sc)
            e.h3r = sb("h3r", [64, U, P], F32, sc)
            e.t2 = sb("t2", [P, U, P], F32, sc)
            e.dot = sb("dot", [P, 3, P], F32, sc)
            e.dT = sb("dT", [P, 8, NB * P], F32, sc)
            load(e, "w1", [(e.Wup0[:, :], i["L1_gnn_W_up0"]), (e.Wup1[:, :], i["L1_gnn_W_up1"]), (e.Wm1[:, :], i["L1_gnn_W_mlp1"]),
                           (e.Wm2[:, :], i["L1_gnn_W_mlp2"]), (e.Wm3[:, :], i["L1_gnn_W_mlp3"]), (e.Wm4[:, :], i["L1_gnn_W_mlp4"]),
                           (e.Wo0[:, :, :], rows(i["L1_gnn_W_out0"])), (e.Wo1[:, :, :], rows(i["L1_gnn_W_out1"]))])
            node_ln(e, "n1", e.x, e.h, ACT.Relu)
            l1_table(e)
            store_table(e, "t1", [(e.ts, e.t0[:, :, :])])
            l1_mlp(e)
            l1_pass(e, "p1", False)
            take_sums(e, "p1", e.h)
            l1_pass(e, "p2", True)
            take_sums(e, "p2", e.t0)
            l1_out(e, e.h, e.t0)

        renew()
        with ExitStack() as sc:
            e.hvb2 = sb("hvb2", [P, D], F32, sc)
            with ExitStack() as s2:
                e.hkW1e = sb("hkW1e", [P, D], F32, s2)
                e.hvW1e = sb("hvW1e", [P, D], F32, s2)
                e.hkW2 = sb("hkW2", [P, 4, D], F32, s2)
                e.hvW2 = sb("hvW2", [P, 4, D], F32, s2)
                e.gkvc = sb("gkvc", [P, 8], F32, s2)
                e.bkvc = sb("bkvc", [P, 8], F32, s2)
                with ExitStack() as s3:
                    e.hkW1 = sb("hkW1", [P, 4, D], F32, s3)
                    e.hvW1 = sb("hvW1", [P, 4, D], F32, s3)
                    e.hqW1 = sb("hqW1", [P, 4, D], F32, s3)
                    e.hqW2 = sb("hqW2", [P, 4, D], F32, s3)
                    e.hkb1 = sb("hkb1", [1, D], F32, s3)
                    e.hvb1 = sb("hvb1", [1, D], F32, s3)
                    e.hqb1 = sb("hqb1", [1, D], F32, s3)
                    e.hqb2 = sb("hqb2", [1, D], F32, s3)
                    e.gqc = sb("gqc", [P, 4], F32, s3)
                    e.bqc = sb("bqc", [P, 4], F32, s3)
                    e.hkb2 = sb("hkb2", [P, D], F32, s3)
                    e.tkv_ = sb("tkv_", [P, NB, 2 * D], F32, s3)
                    e.tq2_ = sb("tq2_", [P, NB, D + 16], F32, s3)
                    load(e, "w2a", [(e.hkW1[:, :, :], rows(i["L2_gnn_hk_W1"][0:D, :])), (e.hkW1e[:, :], i["L2_gnn_hk_W1"][D:D + P, :]),
                                    (e.hvW1[:, :, :], rows(i["L2_gnn_hv_W1"][0:D, :])), (e.hvW1e[:, :], i["L2_gnn_hv_W1"][D:D + P, :]),
                                    (e.hkW2[:, :, :], rows(i["L2_gnn_hk_W2"])), (e.hvW2[:, :, :], rows(i["L2_gnn_hv_W2"])),
                                    (e.hqW1[:, :, :], rows(i["L2_gnn_hq_W1"])), (e.hqW2[:, :, :], rows(i["L2_gnn_hq_W2"])),
                                    (e.hkb1[:, :], line(i["L2_gnn_hk_b1"])), (e.hvb1[:, :], line(i["L2_gnn_hv_b1"])),
                                    (e.hqb1[:, :], line(i["L2_gnn_hq_b1"])), (e.hqb2[:, :], line(i["L2_gnn_hq_b2"])),
                                    (e.gkvc[:, 0:4], column(i["L2_gnn_hk_g"])), (e.gkvc[:, 4:8], column(i["L2_gnn_hv_g"])),
                                    (e.bkvc[:, 0:4], column(i["L2_gnn_hk_be"])), (e.bkvc[:, 4:8], column(i["L2_gnn_hv_be"])),
                                    (e.gqc[:, :], column(i["L2_gnn_hq_g"])), (e.bqc[:, :], column(i["L2_gnn_hq_be"])),
                                    (e.hkb2[:, :], spread(i["L2_gnn_hk_b2"])), (e.hvb2[:, :], spread(i["L2_gnn_hv_b2"]))])
                    node_ln(e, "n2", e.x, e.h, ACT.Relu)

                    def evac2(v, b, n, ps):
                        if n < 2:
                            return v.tensor_copy(e.tkv_[:, b, n * D:(n + 1) * D], ps[:, :])
                        return v.tensor_copy(e.t0[:, b, :], ps[:, :])
                    node_linear(e, "kv1", [e.h], e.hT, None, ACT.Copy,
                                [(e.hkW1[:, :, :], e.hkb1[0:1, :]), (e.hvW1[:, :, :], e.hvb1[0:1, :]),
                                 (e.hqW1[:, :, :], e.hqb1[0:1, :])], evac2)
                    node_linear(e, "q2", [e.t0], e.hT, (e.gqc, e.bqc), ACT.Relu, [(e.hqW2[:, :, :], e.hqb2[0:1, :])],
                                lambda v, b, n, ps: v.tensor_scalar(e.tq2_[:, b, 0:D], ps[:, :], 1.0 / math.sqrt(32.0), None, ALU.mult),
                                ln=(e.t0, e.t0))
                    dots = e.sem("qb2")
                    with nc.Block() as block:
                        @block.vector
                        def _(v):
                            for b in range(NB):
                                v.tensor_tensor(e.t0[:, b, :], e.tq2_[:, b, 0:D], e.hkb2[:, :], ALU.mult).then_inc(dots, 1)
                            v.wait_ge(dots, NB)
                            for b in range(NB):
                                v.tensor_reduce(e.tq2_[:, b, D:D + 16], e.t0[:, b, :].rearrange("p (h d) -> p h d", h=16),
                                                AX.X, ALU.add).then_inc(dots, 1)
                            v.wait_ge(dots, 2 * NB)
                    store_table(e, "t2", [(e.tkv, e.tkv_[:, :, :]), (e.tq2, e.tq2_[:, :, :])])
                e.rowT = sb("rowT", [16, SLOTS], F32, s2)
                with ExitStack() as s3:
                    e.ea = sb("ea", [P, U, P], F32, s3)
                    e.eaT = sb("eaT", [P, U, P], F32, s3)
                    e.gkv = sb("gkv", [P, U, 2 * D], F32, s3)
                    e.qg = sb("qg", [P, U, D + 16], F32, s3)
                    e.hid = sb("hid", [P, 2, 2 * D], F32, s3)
                    e.hTe = sb("hTe", [P, 2, 2 * D], F32, s3)
                    e.prod = sb("prod", [P, D], F32, s3)
                    e.vout = sb("vout", [P, U, D], F32, s3)
                    e.st2 = sb("st2", [P, 2, 2, 6], F32, s3)
                    e.mv2 = sb("mv2", [P, 2, 2, 2], F32, s3)
                    e.va2 = sb("va2", [P, 2, 2], F32, s3)
                    e.sd2 = sb("sd2", [P, 2, 2], F32, s3)
                    e.rs2 = sb("rs2", [P, 2, 2], F32, s3)
                    e.nb2 = sb("nb2", [P, 2, 2], F32, s3)
                    l2_edges(e)
                edge_buffers(e, sb, s2, row_tile=False)
                segment_softmax(e, "s2", 16, False)
                weighted_sums(e, "b2", 16, None)
                divide_sums(e, "d2", 16, "max", bias=e.hvb2[:, :])
            with ExitStack() as s2:
                e.noW1 = sb("noW1", [P, 8, D], F32, s2)
                e.noW2 = sb("noW2", [P, 4, D], F32, s2)
                e.nob1 = sb("nob1", [1, D], F32, s2)
                e.nob2 = sb("nob2", [1, D], F32, s2)
                e.gnc = sb("gnc", [P, 4], F32, s2)
                e.bnc = sb("bnc", [P, 4], F32, s2)
                e.catT = sb("catT", [P, 8, NB * P], F32, s2)
                e.t1 = sb("t1", [P, NB, D], F32, s2)
                load(e, "w2b", [(e.noW1[:, :, :], rows(i["L2_gnn_no_W1"])), (e.noW2[:, :, :], rows(i["L2_gnn_no_W2"])),
                                (e.nob1[:, :], line(i["L2_gnn_no_b1"])), (e.nob2[:, :], line(i["L2_gnn_no_b2"])),
                                (e.gnc[:, :], column(i["L2_gnn_no_g"])), (e.bnc[:, :], column(i["L2_gnn_no_be"]))])
                node_linear(e, "no1", [e.t0, e.h], e.catT, None, ACT.Copy, [(e.noW1[:, :, :], e.nob1[0:1, :])],
                            lambda v, b, n, ps: v.tensor_tensor(e.t1[:, b, :], ps[:, :], e.zeros[:, :], ALU.add))
                xh = e.sem("xh")
                with nc.Block() as block:
                    @block.vector
                    def _(v):
                        for b in range(NB):
                            v.tensor_tensor(e.x[:, b, :], e.x[:, b, :], e.h[:, b, :], ALU.add).then_inc(xh, 1)
                        v.wait_ge(xh, NB)
                node_linear(e, "no2", [e.t1], e.hT, (e.gnc, e.bnc), ACT.Relu, [(e.noW2[:, :, :], e.nob2[0:1, :])],
                            lambda v, b, n, ps: v.tensor_tensor(e.x[:, b, :], ps[:, :], e.x[:, b, :], ALU.add),
                            ln=(e.t1, e.t1))

        renew()
        with ExitStack() as sc:
            edge_buffers(e, sb, sc)
            e.W3 = sb("W3", [P, 4, D], F32, sc)
            e.W3T = sb("W3T", [P, 4, D], F32, sc)
            e.asrc = sb("asrc", [P, D], F32, sc)
            e.adst = sb("adst", [P, D], F32, sc)
            e.gamma = sb("gamma", [P, D], F32, sc)
            e.beta = sb("beta", [P, D], F32, sc)
            e.tes_ = sb("tes_", [P, NB, 8], F32, sc)
            e.ted_ = sb("ted_", [P, NB, 8], F32, sc)
            e.t1 = sb("t1", [P, NB, D], F32, sc)
            e.sg = sb("sg", [P, U, 8], F32, sc)
            e.dg = sb("dg", [P, U, 8], F32, sc)
            e.lg2 = sb("lg2", [P, U, 8], F32, sc)
            e.lg3 = sb("lg3", [P, U, 8], F32, sc)
            load(e, "w3", [(e.W3[:, :, :], rows(i["L3_gnn_W"])),
                           (e.asrc[:, :], spread(i["L3_gnn_a_src"].rearrange("h d -> (h d)"))),
                           (e.adst[:, :], spread(i["L3_gnn_a_dst"].rearrange("h d -> (h d)"))),
                           (e.gamma[:, :], spread(i["L3_gnn_ln_gamma"])), (e.beta[:, :], spread(i["L3_gnn_ln_beta"]))])
            node_ln(e, "n3", e.x, e.h, ACT.Relu)
            wt_, wc_ = e.sem("w3_turned"), e.sem("w3_copied")
            with nc.Block() as block:
                @block.tensor
                def _(pe):
                    for c in range(4):
                        for r in range(4):
                            k = pe.transpose(e.ps[c][:, r * P:(r + 1) * P], e.W3[:, r, c * P:(c + 1) * P], e.ident[:, :])
                        k.then_inc(wt_, 1)

                @block.vector
                def _(v):
                    for c in range(4):
                        v.wait_ge(wt_, c + 1)
                        v.tensor_copy(e.W3T[:, c, :], e.ps[c][:, :]).then_inc(wc_, 1)
            node_linear(e, "l3", [e.h], e.hT, None, ACT.Copy, [(e.W3T[:, :, :], None)],
                        lambda v, b, n, ps: v.tensor_copy(e.t0[:, b, :], ps[:, :]))
            dots3 = e.sem("dots3")
            with nc.Block() as block:
                @block.vector
                def _(v):
                    st = Steps(v, dots3)
                    for vec, dst in ((e.asrc, e.tes_), (e.adst, e.ted_)):
                        for b in range(NB):
                            st(v.tensor_tensor(e.t1[:, b, :], e.t0[:, b, :], vec[:, :], ALU.mult))
                        st.settle()
                        for b in range(NB):
                            st(v.tensor_reduce(dst[:, b, :], e.t1[:, b, :].rearrange("p (h d) -> p h d", h=8), AX.X, ALU.add))
                        st.settle()
            store_table(e, "t3", [(e.th, e.t0[:, :, :]), (e.tes, e.tes_[:, :, :]), (e.ted, e.ted_[:, :, :])])
            logits_l3(e)
            segment_softmax(e, "s3", 8, True)
            weighted_sums(e, "b3", 8, e.th)
            divide_sums(e, "d3", 8, "add")
            fin = e.sem("fin")
            with nc.Block() as block:
                @block.vector
                def _(v):
                    for b in range(NB):
                        v.tensor_tensor(e.t0[:, b, :], e.t0[:, b, :], e.h[:, b, :], ALU.add).then_inc(fin, 1)
                    v.wait_ge(fin, NB)
            node_ln(e, "n4", e.t0, e.t1, ACT.Identity)
            stored = e.sem("stored")
            with nc.Block() as block:
                @block.vector
                def _(v):
                    st = Steps(v, fin, NB)
                    for op, vec in ((ALU.mult, e.gamma), (ALU.add, e.beta)):
                        for b in range(NB):
                            st(v.tensor_tensor(e.t1[:, b, :], e.t1[:, b, :], vec[:, :], op))
                        st.settle()
                    for b in range(NB):
                        st(v.tensor_tensor(e.x[:, b, :], e.t1[:, b, :], e.x[:, b, :], ALU.add))
                    st.settle()

                @block.sync
                def _(sp):
                    sp.wait_ge(fin, 4 * NB)
                    sp.dma_start(out[0:(NB - 1) * P, :].rearrange("(b p) n -> p b n", p=P), e.x[:, 0:NB - 1, :]).then_inc(stored, 16)
                    sp.dma_start(out[(NB - 1) * P:NODES, :], e.x[0:NODES - (NB - 1) * P, NB - 1, :]).then_inc(stored, 16)
                    sp.wait_ge(stored, 32)


def edge_buffers(e, sb, scope, rows_too=True, row_tile=True):
    e.gb0 = sb("gb0", [P, U, D], F32, scope)
    e.gb2 = sb("gb2", [P, U, D], F32, scope)
    if rows_too:
        if row_tile:
            e.rowT = sb("rowT", [16, SLOTS], F32, scope)
        e.rowb = sb("rowb", [16, U * P], F32, scope)
        e.wt = sb("wt", [P, NT, 16], F32, scope)
        e.segA = sb("segA", [P, 16 * SEG], F32, scope)
        e.segF = sb("segF", [P, 16 * SEG], F32, scope)
        e.segB = sb("segB", [P, 16 * SEG], F32, scope)


def kernel(**inputs):
    import numpy as _np
    import concourse.bacc as _bacc
    from concourse import mybir as _mybir
    from concourse.bass_utils import run_bass_kernel_spmd as _run

    nc = _bacc.Bacc("TRN2", target_bir_lowering=False, num_devices=1)
    arrays, args = {}, {}
    for name, a in inputs.items():
        a = _np.ascontiguousarray(a)
        arrays[f"in_{name}"] = a
        args[name] = nc.dram_tensor(f"in_{name}", a.shape, _mybir.dt.from_np(a.dtype), kind="ExternalInput").ap()
    out = nc.dram_tensor("out_0", (NODES, D), _mybir.dt.float32, kind="ExternalOutput").ap()
    program(nc, args, out)
    r = _run(nc, [arrays], core_ids=[0])
    return r.results[0]["out_0"]
```

```python
import math
from contextlib import ExitStack

import concourse.bass as bass
from concourse import mybir

F32 = mybir.dt.float32
I32 = mybir.dt.int32
BF16 = mybir.dt.bfloat16
ALU = mybir.AluOpType
ACT = mybir.ActivationFunctionType
AX = mybir.AxisListType

P = 128
NODES, D = 625, 512
NB = 5
EDGES = 10000
EP, EC = 125, 80
NT = EDGES // P + 1 + NB
U = 4
NI = NT // U
IS = 6
SLOTS = NT * P
PAD_NODE = NODES
RS = 24
RW = RS + 128
F_SRC, F_DST, F_W, F_TYPE, F_A4, F_A8, F_A8N = 0, 1, 2, 3, 4, 8, 16
SEG = SLOTS // P
BIG = 1.0e30
EPS = 1e-5
ACC = NB * D


class Env:
    pass


def hold(eng, *waits):
    waits = [(sem, value) for sem, value in waits if not (isinstance(value, int) and value <= 0)]
    for sem, value in waits:
        eng.wait_ge(sem, value)
    if waits:
        eng.nop(nofuse=True)


def turns(eng, n, body):
    body(0)
    with eng.Fori(1, n) as it:
        body(it)


class Steps:

    def __init__(self, eng, sem, base=0):
        self.eng, self.sem, self.base, self.n = eng, sem, base, 0

    def __call__(self, ins):
        ins.then_inc(self.sem, 1)
        self.n += 1

    def settle(self):
        hold(self.eng, (self.sem, self.base + self.n))



def ln_vector(v, e, s, src):
    for b in range(NB):
        v.bn_stats(e.stats[:, b, :], src[:, b, :]).then_inc(s.stats, 1)
    for b in range(NB):
        v.wait_ge(s.stats, b + 1)
        v.bn_aggr(e.mv[:, b, :], e.stats[:, b, :]).then_inc(s.aggr, 1)
    v.wait_ge(s.aggr, NB)
    v.tensor_scalar(e.vare[:, :], e.mv[:, :, 1], EPS, None, ALU.add).then_inc(s.vare, 1)
    v.wait_ge(s.sd, 1)
    v.reciprocal(e.rstd[:, :], e.sd[:, :]).then_inc(s.rstd, 1)
    v.wait_ge(s.rstd, 1)
    v.scalar_tensor_tensor(out=e.nbias[:, :], in0=e.mv[:, :, 0], scalar=-1.0, in1=e.rstd[:, :],
                           op0=ALU.mult, op1=ALU.mult).then_inc(s.norm, 1)


def ln_scalar(a, e, s, src, dst, func):
    a.wait_ge(s.vare, 1)
    a.activation(e.sd[:, :], e.vare[:, :], ACT.Sqrt).then_inc(s.sd, 1)
    a.wait_ge(s.norm, 1)
    for b in range(NB):
        a.activation(dst[:, b, :], src[:, b, :], func, bias=e.nbias[:, b:b + 1],
                     scale=e.rstd[:, b:b + 1]).then_inc(s.normed, 1)


def ln_sems(e, name):
    s = Env()
    s.stats, s.aggr, s.vare, s.sd = e.sem(f"{name}_stats"), e.sem(f"{name}_aggr"), e.sem(f"{name}_vare"), e.sem(f"{name}_sd")
    s.rstd, s.norm, s.normed = e.sem(f"{name}_rstd"), e.sem(f"{name}_norm"), e.sem(f"{name}_normed")
    return s


def node_ln(e, name, src, dst, func):
    s = ln_sems(e, name)
    with e.nc.Block() as block:
        @block.vector
        def _(v):
            ln_vector(v, e, s, src)

        @block.scalar
        def _(a):
            ln_scalar(a, e, s, src, dst, func)


def node_linear(e, name, srcs, dstT, gb, funcT, lin, evac, ln=None):
    nc = e.nc
    s = ln_sems(e, name) if ln else None
    turned, copied = e.sem(f"{name}_turned"), e.sem(f"{name}_copied")
    summed, taken = e.sem(f"{name}_summed"), e.sem(f"{name}_taken")
    chunks = [(t, c) for t in srcs for c in range(4)]
    KC = len(chunks)
    G = KC // 4
    R = 4
    with nc.Block() as block:
        @block.vector
        def _(v):
            if ln:
                ln_vector(v, e, s, ln[0])
            g = 0
            for b in range(NB):
                for n in range(len(lin)):
                    v.wait_ge(summed, g + 1)
                    evac(v, b, n, e.ps[2 + g % R]).then_inc(taken, 1)
                    g += 1

        @block.scalar
        def _(a):
            if ln:
                ln_scalar(a, e, s, ln[0], ln[1], ACT.Identity)
            for b in range(NB):
                for q in range(G):
                    k = b * G + q
                    a.wait_ge(turned, k + 1)
                    ps = e.ps[k % 2].rearrange("p (c n) -> p c n", c=4)
                    if gb is None:
                        a.activation(dstT[:, 4 * q:4 * q + 4, b * P:(b + 1) * P], ps[:, :, :],
                                     funcT).then_inc(copied, 1)
                    else:
                        for c in range(4):
                            i = a.activation(dstT[:, 4 * q + c, b * P:(b + 1) * P], ps[:, c, :], funcT,
                                             scale=gb[0][:, c:c + 1], bias=gb[1][:, c:c + 1])
                        i.then_inc(copied, 1)

        @block.tensor
        def _(pe):
            def turn(b):
                for q in range(G):
                    k = b * G + q
                    if ln and q == 0:
                        pe.wait_ge(s.normed, b + 1)
                    if k >= 2:
                        pe.wait_ge(copied, k - 1)
                    for c in range(4):
                        t, cc = chunks[4 * q + c]
                        i = pe.transpose(e.ps[k % 2][:, c * P:(c + 1) * P], t[:, b, cc * P:(cc + 1) * P],
                                         e.ident[:, :])
                    i.then_inc(turned, 1)
            turn(0)
            g = 0
            for b in range(NB):
                if b + 1 < NB:
                    turn(b + 1)
                pe.wait_ge(copied, (b + 1) * G)
                for n, (w, bias) in enumerate(lin):
                    if g >= R:
                        pe.wait_ge(taken, g - R + 1)
                    ps = e.ps[2 + g % R]
                    for k in range(KC):
                        i = pe.matmul(ps[:, :], dstT[:, k, b * P:(b + 1) * P], w[:, k, :],
                                      start=(k == 0), stop=(k == KC - 1 and bias is None))
                    if bias is not None:
                        i = pe.matmul(ps[:, :], e.ones[0:1, :], bias, start=False, stop=True)
                    i.then_inc(summed, 1)
                    g += 1


def store_table(e, name, pairs):
    done = e.sem(f"{name}_stored")
    with e.nc.Block() as block:
        @block.sync
        def _(sp):
            for table, tile in pairs:
                sp.dma_start(table.rearrange("(b p) n -> p b n", p=P), tile).then_inc(done, 16)
            sp.wait_ge(done, 16 * len(pairs))



def prepare(e, i):
    nc = e.nc
    built, loaded, filled = e.sem("built"), e.sem("loaded"), e.sem("filled")
    ph_ready = e.sem("phantom_ready")
    with nc.Block() as block:
        @block.gpsimd
        def _(g):
            g.memset(e.ident[:, :], 0.0).then_inc(built, 1)
            g.memset(e.lower[:, :], 0.0).then_inc(built, 1)
            g.memset(e.window[:, :], 1.0).then_inc(built, 1)
            g.memset(e.x[:, NB - 1, :], 0.0).then_inc(built, 1)
            g.wait_ge(built, 4)
            g.affine_select(out=e.ident[:, :], in_=e.ident[:, :], compare_op=ALU.not_equal, fill=1.0,
                            base=0, pattern=[[-1, P]], channel_multiplier=1).then_inc(built, 1)
            g.affine_select(out=e.lower[:, :], in_=e.lower[:, :], compare_op=ALU.is_ge, fill=1.0,
                            base=0, pattern=[[-1, P]], channel_multiplier=1).then_inc(built, 1)
            g.affine_select(out=e.window[:, :], in_=e.window[:, :], compare_op=ALU.is_ge, fill=0.0,
                            base=EC - 1, pattern=[[-1, 2 * EC]], channel_multiplier=0).then_inc(built, 1)
            g.iota(e.nodeno[:, :], pattern=[[1, NB * P]], base=0, channel_multiplier=0,
                   allow_small_or_imprecise_dtypes=True).then_inc(built, 1)
            g.iota(e.lane[:, :], pattern=[[1, P]], base=0, channel_multiplier=0,
                   allow_small_or_imprecise_dtypes=True).then_inc(built, 1)
            g.iota(e.laneP[:, :], pattern=[[0, 1]], base=0, channel_multiplier=1,
                   allow_small_or_imprecise_dtypes=True).then_inc(built, 1)
            g.iota(e.tile_at[:, :], pattern=[[P, NT]], base=0, channel_multiplier=0,
                   allow_small_or_imprecise_dtypes=True).then_inc(built, 1)
            g.wait_ge(built, 11)

        @block.vector
        def _(v):
            steps = Steps(v, e.sem("prep_steps"))
            steps(v.memset(e.phantom[:, :, :], 0.0))
            steps(v.memset(e.ones[:, :], 1.0))
            steps(v.memset(e.zeros[:, :], 0.0))
            steps(v.memset(e.onesb[:, :], 1.0))
            steps(v.memset(e.zerosb[:, :], 0.0))
            steps.settle()
            v.memset(e.phantom[:, :, F_DST:F_DST + 1], float(PAD_NODE)).then_inc(ph_ready, 1)

        @block.sync
        def _(sp):
            sp.wait_ge(ph_ready, 1)
            view = e.rec.rearrange("(p j k) f -> p j (k f)", p=P, k=e.PK)
            for j in range(SEG // e.PK):
                sp.dma_start(view[:, j, :], e.phantom.rearrange("p k f -> p (k f)")).then_inc(filled, 16)
            sp.wait_ge(filled, 16 * (SEG // e.PK))

        @block.scalar
        def _(a):
            a.wait_ge(built, 4)
            a.dma_start(e.x[:, 0:NB - 1, :], i["x"][0:(NB - 1) * P, :].rearrange("(b p) n -> p b n", p=P)).then_inc(loaded, 16)
            a.dma_start(e.x[0:NODES - (NB - 1) * P, NB - 1, :], i["x"][(NB - 1) * P:NODES, :]).then_inc(loaded, 16)
            for tile, src in ((e.srcs, i["src"]), (e.dsts, i["dst"]), (e.kinds, i["edge_type_8"]), (e.weights, i["edge_weight"])):
                a.dma_start(tile[:, :], src.rearrange("(p c) -> p c", c=EC)).then_inc(loaded, 16)
            for tile, src in ((e.a4, i["edge_attr_4"]), (e.a8, i["edge_attr_8"]), (e.a8n, i["edge_attr_8_n2"]),
                              (e.a128, i["edge_attr_128"])):
                a.dma_start(tile[:, :, :], src.rearrange("(p c) f -> p c f", c=EC)).then_inc(loaded, 16)
            for tile, src in e.loads0:
                a.dma_start(tile, src).then_inc(loaded, 16)
            a.wait_ge(loaded, 16 * (10 + len(e.loads0)))


def count_edges(e):
    nc = e.nc
    fields = e.sem("fields")
    marked, used, cleared = e.sem("cnt_marked"), e.sem("cnt_used"), e.sem("cnt_cleared")
    with nc.Block() as block:
        @block.vector
        def _(v):
            for at, n, src in ((F_SRC, 1, e.srcs), (F_DST, 1, e.dsts), (F_TYPE, 1, e.kinds), (F_W, 1, e.weights)):
                v.tensor_copy(e.small[:, :, at:at + 1], src[:, :, None]).then_inc(fields, 1)
            for at, n, src in ((F_A4, 4, e.a4), (F_A8, 8, e.a8), (F_A8N, 8, e.a8n)):
                v.tensor_copy(e.small[:, :, at:at + n], src[:, :, :]).then_inc(fields, 1)
            v.tensor_copy(e.dstf[:, :], e.dsts[:, :]).then_inc(fields, 1)
            v.wait_ge(fields, 8)
            def turn(it):
                for u in range(U):
                    hold(v, (used, it * U + (u + 1)))
                    v.tensor_scalar(e.mark[:, u, :], e.nodeno[0:EP, :], e.dstf[:, bass.ds(it * U + u, 1)], None,
                                    ALU.is_equal).then_inc(marked, 1)
            turns(v, EC // U, turn)

        @block.tensor
        def _(pe):
            outs = ((e.ps[0][:, :], e.ps[2][:, :], 0, 512), (e.ps[1][:, 0:P], e.ps[3][:, 0:P], 512, 640))
            for cnt, pre, a, b in outs:
                pe.matmul(cnt, e.zerosb[:, 0:P], e.zerosb[:, 0:b - a], start=True, stop=True)
                pe.matmul(pre, e.zerosb[:, 0:P], e.zerosb[:, 0:b - a], start=True, stop=True)
            pe.sem_inc(used, U)
            def turn(it):
                for u in range(U):
                    hold(pe, (marked, it * U + (u + 1)))
                    for cnt, pre, a, b in outs:
                        pe.matmul(cnt, e.onesb[0:EP, 0:P], e.mark[:, u, a:b], start=False, stop=True,
                                  skip_group_check=True)
                        i = pe.matmul(pre, e.lowerb[0:EP, :], e.mark[:, u, a:b], start=False, stop=True,
                                      skip_group_check=True)
                    i.then_inc(used, 1)
            turns(pe, EC // U, turn)

def place_edges(e):
    nc = e.nc
    with nc.Block() as block:
        @block.vector
        def _(v):
            steps = Steps(v, e.sem("place_steps"))
            steps(v.tensor_copy(e.cnt[:, 0:512], e.ps[0][:, :]))
            steps(v.tensor_copy(e.cnt[:, 512:640], e.ps[1][:, 0:P]))
            steps(v.memset(e.blk[:, :], 0.0))
            steps.settle()
            steps(v.tensor_reduce(e.bsum[:, :], e.cnt.rearrange("p (b n) -> p b n", b=NB), AX.X, ALU.add))
            steps.settle()
            steps(v.tensor_scalar(e.bsumi[:, :], e.bsum[:, :], float(P - 1), None, ALU.add))
            steps.settle()
            steps(v.tensor_scalar(e.btile[:, :], e.bsumi[:, :], 7, 7, ALU.arith_shift_right, ALU.logical_shift_left))
            steps.settle()
            steps(v.tensor_copy(e.bsize[:, :], e.btile[:, :]))
            steps.settle()
            steps(v.tensor_tensor_scan(e.bend[:, :], e.zeros[:, 0:NB], e.bsize[:, :], 0.0, ALU.add, ALU.add))
            steps.settle()
            steps(v.tensor_tensor(e.bstart[:, :], e.bend[:, :], e.bsize[:, :], ALU.subtract))
            steps.settle()
            for b in range(NB):
                steps(v.tensor_tensor_scan(e.base[:, b * P:(b + 1) * P], e.zeros[:, 0:P],
                                           e.cnt[:, b * P:(b + 1) * P], e.bstart[:, b:b + 1], ALU.add, ALU.add))
            for b in range(1, NB):
                steps.settle()
                steps(v.scalar_tensor_tensor(out=e.blk[:, :], in0=e.tile_at[:, :], scalar=e.bstart[:, b:b + 1],
                                             in1=e.blk[:, :], op0=ALU.is_ge, op1=ALU.add))
            steps.settle()
            steps(v.tensor_copy(e.blki[:, :], e.blk[:, :]))
            steps(v.tensor_tensor(e.base[:, :], e.base[:, :], e.cnt[:, :], ALU.subtract))
            steps.settle()
            steps(v.tensor_tensor(e.base[:, 0:512], e.base[:, 0:512], e.ps[2][:, :], ALU.add))
            steps(v.tensor_tensor(e.base[:, 512:640], e.base[:, 512:640], e.ps[3][:, 0:P], ALU.add))
            steps.settle()
            rank = e.sem("rank")
            def turn(it):
                for u in range(U):
                    c = it * U + u
                    hold(v, (rank, it * (2 * U) + 2 * u))
                    v.scalar_tensor_tensor(out=e.junk[:, 0, :], in0=e.nodeno[0:EP, :],
                                           scalar=e.dstf[:, bass.ds(c, 1)], in1=e.base[0:EP, :], op0=ALU.is_equal,
                                           op1=ALU.mult, accum_out=e.slota[:, bass.ds(c, 1)]).then_inc(rank, 1)
                    v.scalar_tensor_tensor(out=e.junk[:, 1, 0:EC], in0=e.dstf[:, :],
                                           scalar=e.dstf[:, bass.ds(c, 1)], in1=e.window[0:EP, bass.ds(EC - c, EC)],
                                           op0=ALU.is_equal, op1=ALU.mult,
                                           accum_out=e.slotb[:, bass.ds(c, 1)]).then_inc(rank, 1)
            turns(v, EC // U, turn)
            v.wait_ge(rank, 2 * EC)
            v.tensor_tensor(e.sloti[:, :], e.slota[:, :], e.slotb[:, :], ALU.add).then_inc(rank, 1)
            v.wait_ge(rank, 2 * EC + 1)


def scatter_records(e):
    nc = e.nc
    staged = e.sem("rec_staged")
    written = e.landed()
    cols, gone = e.sem("rec_cols"), e.sem("rec_gone")
    with nc.Block() as block:
        @block.scalar
        def _(a):
            def turn(it):
                for u in range(U):
                    hold(a, (written[u], it * 16))
                    a.activation(e.recbuf[:, u, 0:RS], e.small[:, bass.ds(it * U + u, 1), :].rearrange("p a f -> p (a f)"), ACT.Copy).then_inc(staged, 1)
                    a.activation(e.recbuf[:, u, RS:RW], e.a128[:, bass.ds(it * U + u, 1), :].rearrange("p a f -> p (a f)"), ACT.Copy).then_inc(staged, 1)
            turns(a, EC // U, turn)

        @block.gpsimd
        def _(g):
            def turn(it):
                hold(g, *[(written[u], it * 16) for u in range(U)])
                g.tensor_copy(e.slotbuf[:, :], e.sloti[:, bass.ds(it * U, U)]).then_inc(cols, 1)
                hold(g, (cols, it + 1))
                for u in range(U):
                    hold(g, (staged, it * (2 * U) + 2 * (u + 1)))
                    g.indirect_dma_start(e.rec[:, :], bass.IndirectOffsetOnAxis(ap=e.slotbuf[:, u:u + 1], axis=0),
                                         e.recbuf[:, u, :], None).then_inc(written[u], 16)
            turns(g, EC // U, turn)
            for u in range(U):
                g.wait_ge(written[u], 16 * (EC // U))


def turned_marks(e):
    out, back, sv, read = e.sem("oht_out"), [e.sem(f"oht_back{k}") for k in range(2)], e.sem("oht_steps"), e.sem("oht_read")
    C = SLOTS // 6
    flat = e.dlocd.rearrange("t p -> (t p)").rearrange("(a n) -> a n", a=1)
    with e.nc.Block() as block:
        @block.tensor
        def _(pe):
            pe.transpose(e.ps[0][0:NT, 0:P], e.dloc[:, :], e.ident[:, :]).then_inc(sv, 1)

        @block.vector
        def _(v):
            v.wait_ge(sv, 1)
            v.tensor_copy(e.dstT[0:NT, :], e.ps[0][0:NT, 0:P]).then_inc(out, 1)
            for c in range(6):
                v.wait_ge(back[c % 2], 16 * (c // 2 + 1))
                v.tensor_scalar(e.ohT[:, c * C:(c + 1) * C], e.spread[:, c % 2, :], e.laneP[:, 0:1], None,
                                ALU.is_equal).then_inc(read, 1)

        @block.sync
        def _(sp):
            sp.wait_ge(out, 1)
            sp.dma_start(e.dlocd[:, :], e.dstT[0:NT, :]).then_inc(e.oht_st, 16)
            sp.wait_ge(e.oht_st, 16)
            for c in range(6):
                if c >= 2:
                    sp.wait_ge(read, c - 1)
                sp.dma_start(e.spread[:, c % 2, :], flat[:, c * C:(c + 1) * C].to_broadcast([P, C])).then_inc(back[c % 2], 16)


def load_sorted(e):
    nc = e.nc
    ld, dt, dd = e.sem("srt_loaded"), e.sem("srt_turned"), e.sem("srt_dst")
    sv, emb = e.sem("srt_steps"), e.sem("srt_row")
    with nc.Block() as block:
        @block.sync
        def _(sp):
            sp.dma_start(e.srt[:, :, :], e.rec[:, 0:RS].rearrange("(t p) f -> p t f", p=P)).then_inc(ld, 16)
            sp.wait_ge(sv, 2)
            sp.dma_start(e.dstd[1:1 + SLOTS, :].rearrange("(t p) a -> t (p a)", p=P), e.dstT[0:NT, :]).then_inc(dd, 16)
            sp.dma_start(e.dstd[0:1, :], e.guard[0:1, 0:1]).then_inc(dd, 16)
            sp.dma_start(e.dstd[SLOTS + 1:SLOTS + 2, :], e.guard[0:1, 1:2]).then_inc(dd, 16)
            sp.wait_ge(dd, 48)
            for k in range(3):
                sp.dma_start(e.seg3[:, k, :], e.dstd[k:k + SLOTS, :].rearrange("(p j) a -> p (j a)", p=P)).then_inc(dd, 16)

        @block.tensor
        def _(pe):
            pe.wait_ge(ld, 16)
            pe.transpose(e.ps[0][0:NT, 0:P], e.srt[:, :, F_DST], e.ident[:, :]).then_inc(dt, 1)
            pe.wait_ge(sv, e.ROWS_AT)
            for k in range(2):
                i = pe.matmul(e.ps[1][0:16, k * P:(k + 1) * P], e.whole[:, k:k + 1].to_broadcast([P, 16]), e.ident[:, :],
                              start=True, stop=True)
            i.then_inc(emb, 1)

        @block.vector
        def _(v):
            st = Steps(v, sv)
            v.wait_ge(dt, 1)
            st(v.tensor_copy(e.dstT[0:NT, :], e.ps[0][0:NT, 0:P]))
            st(v.memset(e.guard[0:1, :], -7.0))
            v.wait_ge(ld, 16)
            st(v.tensor_copy(e.srcI[:, :], e.srt[:, :, F_SRC]))
            st(v.tensor_copy(e.dstI[:, :], e.srt[:, :, F_DST]))
            st(v.scalar_tensor_tensor(out=e.dloc[:, :], in0=e.blk[:, :], scalar=-float(P), in1=e.srt[:, :, F_DST],
                                      op0=ALU.mult, op1=ALU.add))
            st(v.tensor_tensor(e.asum[:, :, :], e.srt[:, :, F_A8:F_A8 + 8], e.srt[:, :, F_A8N:F_A8N + 8], ALU.add))
            v.wait_ge(dd, 96)
            st(v.tensor_tensor(e.pen[:, 0, :], e.seg3[:, 1, :], e.seg3[:, 0, :], ALU.is_equal))
            st(v.tensor_tensor(e.pen[:, 1, :], e.seg3[:, 1, :], e.seg3[:, 2, :], ALU.is_equal))
            st.settle()
            st(v.tensor_scalar(e.pen[:, :, :], e.pen[:, :, :], -1.0, BIG, ALU.add, ALU.mult))
            st.settle()
            st(v.tensor_reduce(e.whole[:, :], e.pen[:, :, :], AX.X, ALU.min))
            for h in range(16):
                st(v.tensor_copy(e.penF[:, h, :], e.pen[:, 0, :]))
                st(v.tensor_copy(e.penB[:, h, :], e.pen[:, 1, :]))
            st.settle()
            st(v.memset(e.penF[:, :, 0:1], -BIG))
            st(v.memset(e.penB[:, :, SEG - 1:SEG], -BIG))
            assert st.n >= e.ROWS_AT
            v.wait_ge(emb, 1)
            st(v.tensor_copy(e.wrow[0:16, :], e.ps[1][0:16, 0:2 * P]))
            st(v.memset(e.fac[:, :, :], 1.0))
            st.settle()
            for k in range(8):
                st(v.scalar_tensor_tensor(out=e.fack[:, :, :], in0=e.srt[:, :, F_TYPE:F_TYPE + 1].to_broadcast([P, NT, 8]),
                                          scalar=float(k), in1=e.emb[:, k:k + 1, :].to_broadcast([P, NT, 8]),
                                          op0=ALU.is_equal, op1=ALU.mult))
                st.settle()
                st(v.tensor_tensor(e.fac[:, :, :], e.fac[:, :, :], e.fack[:, :, :], ALU.add))
                st.settle()
            st(v.tensor_tensor(e.fac[:, :, :], e.fac[:, :, :], e.srt[:, :, F_W:F_W + 1].to_broadcast([P, NT, 8]), ALU.mult))
            st.settle()



def segment_softmax(e, name, H, floor_zero):
    nc = e.nc
    io, sv = e.sem(f"{name}_io"), e.sem(f"{name}_steps")
    turned, ex = e.sem(f"{name}_turned"), e.sem(f"{name}_exp")
    W = H * SEG
    A = e.segA[:, 0:W]
    Fw = e.segF[:, 0:W]
    A3 = A.rearrange("p (h j) -> p h j", h=H)
    F3 = Fw.rearrange("p (h j) -> p h j", h=H)
    penF = e.penF[:, 0:H, :].rearrange("p h j -> p (h j)")
    penB = e.penB[:, 0:H, :].rearrange("p h j -> p (h j)")
    marks = {}
    with nc.Block() as block:
        @block.vector
        def _(v):
            st = Steps(v, sv)
            v.wait_ge(io, 16)
            st(v.tensor_copy(e.edge0[:, 0:H], A3[:, :, 0]))
            st(v.tensor_tensor_scan(Fw, penF, A, -BIG, ALU.add, ALU.max))
            st.settle()
            st(v.tensor_copy(e.ends[:, 0:H], F3[:, :, SEG - 1]))
            marks["f"] = st.n
            st(v.memset(e.carry[0:H, 0:1], -BIG))
            v.wait_ge(turned, 1)
            st(v.tensor_tensor_scan(e.carry[0:H, 1:P + 1], e.wrow[0:H, 0:P], e.ps[0][0:H, 0:P], -BIG, ALU.add, ALU.max))
            marks["fc"] = st.n
            v.wait_ge(turned, 2)
            st(v.scalar_tensor_tensor(out=A3[:, :, 0], in0=e.ps[1][:, 0:H], scalar=e.pen[:, 0, 0:1], in1=e.edge0[:, 0:H],
                                      op0=ALU.add, op1=ALU.max))
            st.settle()
            st(v.tensor_tensor_scan(Fw, penF, A, -BIG, ALU.add, ALU.max))
            st.settle()
            st(v.tensor_copy(A3[:, :, 0], e.edge0[:, 0:H]))
            st(v.tensor_tensor_scan(e.segB[:, 0:W][:, ::-1], penB[:, ::-1], Fw[:, ::-1], -BIG, ALU.add, ALU.max))
            st.settle()
            st(v.tensor_copy(e.ends[:, 0:H], e.segB[:, 0:W].rearrange("p (h j) -> p h j", h=H)[:, :, 0]))
            marks["b"] = st.n
            st(v.memset(e.carry[0:H, P:P + 1], -BIG))
            v.wait_ge(turned, 3)
            st(v.tensor_tensor_scan(e.carry[0:H, 0:P][:, ::-1], e.wrow[0:H, P:2 * P][:, ::-1],
                                    e.ps[0][0:H, 0:P][:, ::-1], -BIG, ALU.add, ALU.max))
            marks["bc"] = st.n
            v.wait_ge(turned, 4)
            st(v.scalar_tensor_tensor(out=F3[:, :, SEG - 1], in0=e.ps[1][:, 0:H], scalar=e.pen[:, 1, SEG - 1:SEG],
                                      in1=F3[:, :, SEG - 1], op0=ALU.add, op1=ALU.max))
            st.settle()
            st(v.tensor_tensor_scan(e.segB[:, 0:W][:, ::-1], penB[:, ::-1], Fw[:, ::-1], -BIG, ALU.add, ALU.max))
            st.settle()
            if floor_zero:
                st(v.tensor_scalar(e.segB[:, 0:W], e.segB[:, 0:W], 0.0, None, ALU.max))
                st.settle()
            v.tensor_tensor(A, A, e.segB[:, 0:W], ALU.subtract).then_inc(ex, 1)

        @block.tensor
        def _(pe):
            for k, m in enumerate(("f", "fc", "b", "bc")):
                pe.wait_ge(sv, marks[m])
                if k % 2 == 0:
                    i = pe.transpose(e.ps[0][0:H, 0:P], e.ends[:, 0:H], e.ident[:, :])
                else:
                    a = 0 if k == 1 else 1
                    i = pe.transpose(e.ps[1][:, 0:H], e.carry[0:H, a:a + P], e.ident[0:H, 0:H])
                i.then_inc(turned, 1)

        @block.scalar
        def _(a):
            a.wait_ge(ex, 1)
            a.activation(A, A, ACT.Exp).then_inc(ex, 1)

        @block.sync
        def _(sp):
            sp.dma_start(A3, e.rowd[0:H, 0:SLOTS].rearrange("h (p j) -> p h j", p=P)).then_inc(io, 16)
            sp.wait_ge(ex, 2)
            sp.dma_start(e.rowd2[0:H, 0:SLOTS].rearrange("h (p j) -> p h j", p=P), A3).then_inc(io, 16)
            sp.wait_ge(io, 32)


def gather_loop(g, e, name, fetches, free, got, extra=None):
    cols = e.sem(f"{name}_cols")
    K, S = len(fetches), IS

    def turn(it):
        for half in range(2):
            first = it * (2 * S) + half * S
            for k, (index, table, buf) in enumerate(fetches):
                g.tensor_copy(e.idx[:, k, half, :], index[:, bass.ds(first, S)]).then_inc(cols, 1)
            hold(g, (cols, it * (2 * K) + (half + 1) * K))
            for j in range(S):
                u = (half * S + j) % U
                hold(g, (free, first + (j + 1)))
                for k, (index, table, buf) in enumerate(fetches):
                    g.indirect_dma_start(buf[:, u, :], None, table[:, :],
                                         bass.IndirectOffsetOnAxis(ap=e.idx[:, k, half, j:j + 1], axis=0)).then_inc(got[k][u], 16)
                if extra:
                    extra(g, first + j, u)
    turns(g, NT // (2 * S), turn)


def gather_sems(e, name, n):
    return [e.landed() for k in range(n)]


def row_transposes(pe, e, it, lg, H, lg_ready, ps, row_free, turned):
    hold(pe, (lg_ready, it + 1), (row_free, it))
    for u in range(U):
        i = pe.transpose(ps[0:H, u * P:(u + 1) * P], lg[:, u, 0:H], e.ident[:, :])
    i.then_inc(turned, 1)


def split3(v, st, e, dst, src, width):
    for k in range(3):
        for b in range(NB):
            st(v.tensor_copy(dst[:, b, k, 0:width], (src if k == 0 else e.rest)[:, b, 0:width]))
        st.settle()
        if k < 2:
            for b in range(NB):
                st(v.tensor_tensor(e.rest[:, b, 0:width], (src if k == 0 else e.rest)[:, b, 0:width], dst[:, b, k, 0:width],
                                   ALU.subtract))
            st.settle()


def split_table(e, name, dst, src, width):
    with e.nc.Block() as block:
        @block.vector
        def _(v):
            split3(v, Steps(v, e.sem(f"{name}_split")), e, dst, src, width)


def at_destination(pe, e, ps, t, table, a, b):
    blk = pe.value_load(e.blki[0:1, bass.ds(t, 1)], min_val=0, max_val=NB - 1)
    for k in range(3):
        i = pe.matmul(ps, e.ohT[:, bass.ds(t * P, P)], table[:, bass.ds(blk, 1), k, a:b].rearrange("p a n -> p (a n)"),
                      start=(k == 0), stop=(k == 2))
    return i


def logits_l0(e):
    H = 8
    nc = e.nc
    got = gather_sems(e, "a0", 1)
    free, turned, rows, keys = e.sem("a0_free"), e.sem("a0_turned"), e.sem("a0_rows"), e.sem("a0_keys")
    stored = e.sem("a0_stored")
    ready, summed, multiplied = e.sem("a0_ready"), e.sem("a0_summed"), e.sem("a0_multiplied")
    with nc.Block() as block:
        @block.gpsimd
        def _(g):
            gather_loop(g, e, "a0", [(e.srcI, e.tq, e.gb0)], free, got)

        @block.vector
        def _(v):
            v.sem_inc(free, U)

            def turn(it):
                for u in range(U):
                    hold(v, (got[0][u], it * 16 + 16), (keys, it * U + (u + 1)), (summed, it))
                    v.tensor_tensor(e.gb2[:, u, :], e.gb0[:, u, :], e.ps[1 + u][:, :], ALU.mult).then_inc(multiplied, 1)
                    hold(v, (multiplied, it * U + (u + 1)))
                    v.sem_inc(free, 1)
                hold(v, (turned, it))
                v.tensor_reduce(e.lg[:, :, 0:H], e.gb2[:, :, :].rearrange("p u (h d) -> p u h d", h=H), AX.X,
                                ALU.add).then_inc(summed, 1)
                hold(v, (summed, it + 1))
                v.tensor_tensor(e.lg[:, :, 0:H], e.lg[:, :, 0:H], e.asum[:, bass.ds(it * U, U), :], ALU.add).then_inc(ready, 1)
            turns(v, NI, turn)

        @block.tensor
        def _(pe):
            def keys_of(it):
                for u in range(U):
                    hold(pe, (multiplied, it * U - (U - 1 - u)))
                    at_destination(pe, e, e.ps[1 + u][:, :], it * U + u, e.tk3, 0, D).then_inc(keys, 1)

            def turn(it):
                keys_of(it + 1)
                row_transposes(pe, e, it, e.lg, H, ready, e.ps[0], rows, turned)
            keys_of(0)
            turns(pe, NI - 1, turn)
            row_transposes(pe, e, NI - 1, e.lg, H, ready, e.ps[0], rows, turned)

        @block.scalar
        def _(a):
            def turn(it):
                hold(a, (turned, it + 1), (stored, it * 16))
                a.activation(e.rowb[0:H, :], e.ps[0][0:H, :], ACT.Copy).then_inc(rows, 1)
            turns(a, NI, turn)

        @block.sync
        def _(sp):
            def turn(it):
                hold(sp, (rows, it + 1))
                sp.dma_start(e.rowd[0:H, bass.ds(it * (U * P), U * P)], e.rowb[0:H, :]).then_inc(stored, 16)
            turns(sp, NI, turn)
            sp.wait_ge(stored, 16 * NI)


def weighted_sums(e, name, H, table):
    DH = D // H
    nc = e.nc
    got = gather_sems(e, name, 1) if table is not None else [[e.sem(f"{name}_got{u}") for u in range(U)]]
    free, rowin, wts = e.sem(f"{name}_free"), e.sem(f"{name}_rowin"), e.sem(f"{name}_weights")
    turned, oh, msg = e.sem(f"{name}_turned"), e.sem(f"{name}_marks"), e.sem(f"{name}_msgs")
    with nc.Block() as block:
        if table is not None:
            @block.gpsimd
            def _(g):
                gather_loop(g, e, name, [(e.srcI, table, e.gb0)], free, got)
        else:
            @block.sync
            def _(sp):
                def turn(it):
                    for u in range(U):
                        hold(sp, (free, it * U + (u + 1)))
                        sp.dma_start(e.gb0[:, u, :], e.vd[bass.ds((it * U + u) * P, P), :]).then_inc(got[0][u], 16)
                turns(sp, NI, turn)

        @block.scalar
        def _(a):
            def turn(it):
                hold(a, (turned, it))
                a.dma_start(e.rowb[0:H, :], e.rowd2[0:H, bass.ds(it * (U * P), U * P)]).then_inc(rowin, 16)
                hold(a, (turned, it + 1))
                a.activation(e.wt[:, bass.ds(it * U, U), 0:H], e.ps[7][:, 0:U * H].rearrange("p (u h) -> p u h", u=U),
                             ACT.Copy).then_inc(wts, 1)
            turns(a, NI, turn)

        @block.vector
        def _(v):
            def turn(it):
                hold(v, (wts, it + 1))
                for u in range(U):
                    hold(v, (got[0][u], it * 16 + 16), (free, it * U + (u + 1)))
                    v.tensor_scalar(e.oh[:, u, :], e.lane[:, :], e.dloc[:, bass.ds(it * U + u, 1)], None,
                                    ALU.is_equal).then_inc(oh, 1)
                    v.tensor_tensor(e.gb2[:, u, :].rearrange("p (h d) -> p h d", h=H),
                                    e.gb0[:, u, :].rearrange("p (h d) -> p h d", h=H),
                                    e.wt[:, bass.ds(it * U + u, 1), 0:H].rearrange("p a h -> p h a").to_broadcast([P, H, DH]),
                                    ALU.mult).then_inc(msg, 1)
            turns(v, NI, turn)

        @block.tensor
        def _(pe):
            for b in range(NB):
                pe.matmul(e.acc[:, b * D:(b + 1) * D], e.zeros[:, 0:P], e.zeros[:, :], start=True, stop=True)
            pe.matmul(e.ps[6][:, :], e.zeros[:, 0:P], e.zeros[:, :], start=True, stop=True)
            pe.sem_inc(free, U)
            def weights(it):
                hold(pe, (rowin, it * 16 + 16), (wts, it))
                for u in range(U):
                    i = pe.transpose(e.ps[7][:, u * H:(u + 1) * H], e.rowb[0:H, u * P:(u + 1) * P], e.ident[0:H, 0:H])
                i.then_inc(turned, 1)

            def sums(it):
                for u in range(U):
                    blk = pe.value_load(e.blki[0:1, bass.ds(it * U + u, 1)], min_val=0, max_val=NB - 1)
                    hold(pe, (oh, it * U + (u + 1)), (msg, it * U + (u + 1)))
                    pe.matmul(e.ps[6][:, bass.ds(blk * 16, H)], e.oh[:, u, :],
                              e.wt[:, bass.ds(it * U + u, 1), 0:H].rearrange("p a h -> p (a h)"), start=False, stop=True,
                              skip_group_check=True)
                    pe.matmul(e.acc[:, bass.ds(blk * D, D)], e.oh[:, u, :], e.gb2[:, u, :], start=False, stop=True,
                              skip_group_check=True).then_inc(free, 1)

            def turn(it):
                weights(it + 1)
                sums(it)
            weights(0)
            turns(pe, NI - 1, turn)
            sums(NI - 1)

def divide_sums(e, name, H, guard, bias=None):
    DH = D // H
    den = e.ps[6][:, 0:NB * 16].rearrange("p (b h) -> p b h", b=NB)[:, :, 0:H]
    with e.nc.Block() as block:
        @block.vector
        def _(v):
            st = Steps(v, e.sem(f"{name}_steps"))
            if guard == "add":
                st(v.tensor_scalar(e.rden[:, :, 0:H], den, 1e-10, None, ALU.add))
            else:
                st(v.tensor_scalar(e.rden[:, :, 0:H], den, 0.5, None, ALU.max))
            st(v.tensor_scalar(e.some[:, :], den[:, :, 0], 0.0, None, ALU.is_gt))
            st.settle()
            st(v.reciprocal(e.rden[:, :, 0:H], e.rden[:, :, 0:H]))
            st.settle()
            for b in range(NB):
                st(v.tensor_tensor(e.t0[:, b, :].rearrange("p (h d) -> p h d", h=H),
                                   e.acc[:, b * D:(b + 1) * D].rearrange("p (h d) -> p h d", h=H),
                                   e.rden[:, b, 0:H, None].to_broadcast([P, H, DH]), ALU.mult))
            st.settle()
            if bias is not None:
                for b in range(NB):
                    st(v.scalar_tensor_tensor(out=e.t0[:, b, :], in0=bias, scalar=e.some[:, b:b + 1], in1=e.t0[:, b, :],
                                              op0=ALU.mult, op1=ALU.add))
                st.settle()


def ffn(e):
    nc = e.nc
    M = 4 * D // P
    up, gel, down, got = e.sem("f_up"), e.sem("f_gelu"), e.sem("f_down"), e.sem("f_got")
    parts = ((0, 512), (512, NB * P))
    R = 3
    with nc.Block() as block:
        @block.tensor
        def _(pe):
            pe.wait_ge(e.W1_in, 16)
            pe.wait_ge(e.W2_in, 32)

            def hidden(m):
                for q, (a, b) in enumerate(parts):
                    k = 2 * m + q
                    if k >= R:
                        pe.wait_ge(gel, k - R + 1)
                    for c in range(4):
                        i = pe.matmul(e.ps[NB + k % R][:, 0:b - a], e.W1[:, c, m * P:(m + 1) * P], e.hT[:, c, a:b],
                                      start=(c == 0), stop=(c == 3))
                    i.then_inc(up, 1)

            hidden(0)
            for m in range(M):
                if m + 1 < M:
                    hidden(m + 1)
                pe.wait_ge(gel, 2 * m + 2)
                for b in range(NB):
                    i = pe.matmul(e.ps[b][:, :], e.uT[:, m % 4, b * P:(b + 1) * P], e.W2[:, m, :], start=(m == 0), stop=False,
                                  skip_group_check=True)
                i.then_inc(down, 1)
            for b in range(NB):
                pe.matmul(e.ps[b][:, :], e.ones[0:1, :], e.b2r[0:1, :], start=False, stop=True,
                          skip_group_check=True).then_inc(got, 1)

        @block.scalar
        def _(a_):
            for m in range(M):
                if m >= 4:
                    a_.wait_ge(down, m - 3)
                for q, (a, b) in enumerate(parts):
                    k = 2 * m + q
                    a_.wait_ge(up, k + 1)
                    a_.activation(e.uT[:, m % 4, a:b], e.ps[NB + k % R][:, 0:b - a], ACT.Gelu,
                                  bias=e.b1c[:, m:m + 1]).then_inc(gel, 1)

        @block.vector
        def _(v):
            st = Steps(v, e.sem("f_steps"))
            for b in range(NB):
                st(v.tensor_tensor(e.x[:, b, :], e.x[:, b, :], e.h1[:, b, :], ALU.add))
            st.settle()
            for b in range(NB):
                v.wait_ge(got, b + 1)
                st(v.tensor_tensor(e.x[:, b, :], e.ps[b][:, :], e.x[:, b, :], ALU.add))



def l1_table(e):
    nc = e.nc
    turned, copied, summed, taken = (e.sem(f"u_{f}") for f in ("turned", "copied", "summed", "taken"))
    scale = 1.0 / math.sqrt(P) * SILU_2MOM / math.sqrt(64.0)
    with nc.Block() as block:
        @block.tensor
        def _(pe):
            for b in range(NB):
                if b >= 2:
                    pe.wait_ge(copied, b - 1)
                for c in range(4):
                    src = e.h[:, b, 0:P] if c == 0 else e.h[:, b, P:D].rearrange("p (u m) -> p m u", m=3)[:, c - 1, :]
                    i = pe.transpose(e.ps[b % 2][:, c * P:(c + 1) * P], src, e.ident[:, :])
                i.then_inc(turned, 1)
            for b in range(NB):
                pe.wait_ge(copied, b + 1)
                if b >= 2:
                    pe.wait_ge(taken, b - 1)
                for c in range(4):
                    i = pe.matmul(e.ps[2 + b % 2][:, c * P:(c + 1) * P], e.hT[:, c, b * P:(b + 1) * P],
                                  (e.Wup0 if c == 0 else e.Wup1)[:, :], start=True, stop=True)
                i.then_inc(summed, 1)

        @block.scalar
        def _(a):
            for b in range(NB):
                a.wait_ge(turned, b + 1)
                a.activation(e.hT[:, 0:4, b * P:(b + 1) * P], e.ps[b % 2].rearrange("p (c n) -> p c n", c=4),
                             ACT.Copy).then_inc(copied, 1)

        @block.vector
        def _(v):
            for b in range(NB):
                v.wait_ge(summed, b + 1)
                v.tensor_scalar(e.t0[:, b, :], e.ps[2 + b % 2][:, :], scale, None, ALU.mult).then_inc(taken, 1)


SILU_2MOM = 1.679177


def l1_mlp(e):
    nc = e.nc
    stored = e.sem("m_stored")
    sems = {f: e.sem(f"m_{f}") for f in ("fin", "ft", "ftc", "mm1", "a1", "mm2", "a2", "mm3", "a3")}
    with nc.Block() as block:
        @block.scalar
        def _(a):
            def turn(it):
                hold(a, (sems["ft"], it))
                a.activation(e.fin[:, :, :], e.srt[:, bass.ds(it * U, U), F_A8:F_A8 + 8], ACT.Copy).then_inc(sems["fin"], 1)
                hold(a, (sems["ft"], it + 1), (sems["mm1"], it))
                a.activation(e.fT[0:8, :], e.ps[0][0:8, :], ACT.Copy).then_inc(sems["ftc"], 1)
                hold(a, (sems["mm1"], it + 1), (sems["mm2"], it))
                a.activation(e.hh1[0:64, :], e.ps[1][0:64, :], ACT.Silu, scale=1.0 / math.sqrt(8.0)).then_inc(sems["a1"], 1)
                hold(a, (sems["mm2"], it + 1), (sems["mm3"], it))
                a.activation(e.hh2[0:64, :], e.ps[2][0:64, :], ACT.Silu, scale=SILU_2MOM / 8.0).then_inc(sems["a2"], 1)
                hold(a, (sems["mm3"], it + 1), (stored, it * 16))
                a.activation(e.h3[0:64, :], e.ps[3][0:64, :], ACT.Silu, scale=SILU_2MOM / 8.0).then_inc(sems["a3"], 1)
            turns(a, NI, turn)

        @block.sync
        def _(sp):
            def turn(it):
                hold(sp, (sems["a3"], it + 1))
                sp.dma_start(e.h3d[:, bass.ds(it * (U * P), U * P)], e.h3[0:64, :]).then_inc(stored, 16)
            turns(sp, NI, turn)
            sp.wait_ge(stored, 16 * NI)

        @block.tensor
        def _(pe):
            def turn(it):
                hold(pe, (sems["fin"], it + 1), (sems["ftc"], it))
                for u in range(U):
                    i = pe.transpose(e.ps[0][0:8, u * P:(u + 1) * P], e.fin[:, u, :], e.ident[:, :])
                i.then_inc(sems["ft"], 1)
                hold(pe, (sems["ftc"], it + 1), (sems["a1"], it))
                pe.matmul(e.ps[1][0:64, :], e.Wm1[0:8, :], e.fT[0:8, :], start=True, stop=True).then_inc(sems["mm1"], 1)
                hold(pe, (sems["a1"], it + 1), (sems["a2"], it))
                pe.matmul(e.ps[2][0:64, :], e.Wm2[0:64, :], e.hh1[0:64, :], start=True, stop=True).then_inc(sems["mm2"], 1)
                hold(pe, (sems["a2"], it + 1), (sems["a3"], it))
                pe.matmul(e.ps[3][0:64, :], e.Wm3[0:64, :], e.hh2[0:64, :], start=True, stop=True).then_inc(sems["mm3"], 1)
            turns(pe, NI, turn)

def l1_pass(e, name, second):
    nc = e.nc
    got = gather_sems(e, name, 1)
    free, w, msg = (e.sem(f"{name}_{f}") for f in ("free", "w", "msg"))
    hr = [e.sem(f"{name}_hid{u}") for u in range(U)]
    scaled = e.sem(f"{name}_scaled")
    W4 = e.Wm4[0:64, :].rearrange("p (a b n) -> p a b n", a=2, b=2)[:, :, 1 if second else 0, :]
    K = 6 if second else 3

    def y(t, m):
        return e.srt[:, bass.ds(t, 1), F_A4 + m:F_A4 + m + 1].rearrange("p a f -> p (a f)")

    with nc.Block() as block:
        @block.gpsimd
        def _(g):
            gather_loop(g, e, name, [(e.srcI, e.ts, e.gb0)], free, got)

        @block.sync
        def _(sp):
            def turn(it):
                for u in range(U):
                    hold(sp, (free, it * U + (u + 1)))
                    sp.dma_start(e.h3r[0:64, u, :], e.h3d[:, bass.ds((it * U + u) * P, P)]).then_inc(hr[u], 16)
            turns(sp, NI, turn)

        @block.scalar
        def _(a):
            if second:
                def turn(it):
                    for u in range(U):
                        hold(a, (msg, it * (K * U) + (K * u + 2)))
                        for m in range(3):
                            i = a.activation(e.gb2[:, u, m * P:(m + 1) * P], e.t2[:, u, :], ACT.Copy,
                                             scale=y(it * U + u, m + 1))
                        i.then_inc(scaled, 1)
                turns(a, NI, turn)

        @block.vector
        def _(v):
            def turn(it):
                for u in range(U):
                    t = it * U + u
                    at = it * (K * U) + K * u
                    hold(v, (got[0][u], it * 16 + 16), (free, it * U + (u + 1)), (w, it * U + (u + 1)))
                    ps = e.ps[5 + u % 3]
                    s0, s1 = e.gb0[:, u, 0:P], e.gb0[:, u, P:D]
                    if not second:
                        v.tensor_scalar(e.oh[:, u, :], e.lane[:, :], e.dloc[:, bass.ds(t, 1)], y(t, 0), ALU.is_equal,
                                        ALU.mult).then_inc(msg, 1)
                        v.tensor_tensor(e.gb2[:, u, 0:P], s0, ps[:, 0:P], ALU.mult).then_inc(msg, 1)
                        v.tensor_tensor(e.gb2[:, u, P:D].rearrange("p (m n) -> p m n", m=3),
                                        s1.rearrange("p (m n) -> p m n", m=3),
                                        ps[:, None, P:2 * P].to_broadcast([P, 3, P]), ALU.mult).then_inc(msg, 1)
                    else:
                        v.tensor_scalar(e.oh[:, u, :], e.lane[:, :], e.dloc[:, bass.ds(t, 1)], None,
                                        ALU.is_equal).then_inc(msg, 1)
                        v.tensor_tensor(e.t2[:, u, :], s0, ps[:, 0:P], ALU.mult).then_inc(msg, 1)
                        v.tensor_scalar(e.dot[:, 0, :], s1[:, 0:P], y(t, 1), None, ALU.mult).then_inc(msg, 1)
                        hold(v, (msg, at + 3))
                        v.scalar_tensor_tensor(out=e.dot[:, 1, :], in0=s1[:, P:2 * P], scalar=y(t, 2), in1=e.dot[:, 0, :],
                                               op0=ALU.mult, op1=ALU.add).then_inc(msg, 1)
                        hold(v, (msg, at + 4))
                        v.scalar_tensor_tensor(out=e.dot[:, 2, :], in0=s1[:, 2 * P:3 * P], scalar=y(t, 3), in1=e.dot[:, 1, :],
                                               op0=ALU.mult, op1=ALU.add).then_inc(msg, 1)
                        hold(v, (msg, at + 5))
                        v.scalar_tensor_tensor(out=e.gb2[:, u, 3 * P:D], in0=e.dot[:, 2, :], scalar=1.0 / math.sqrt(3.0),
                                               in1=ps[:, P:2 * P], op0=ALU.mult, op1=ALU.mult).then_inc(msg, 1)
            turns(v, NI, turn)

        @block.tensor
        def _(pe):
            for b in range(NB):
                pe.matmul(e.acc[:, b * D:(b + 1) * D], e.zeros[:, 0:P], e.zeros[:, :], start=True, stop=True)
            pe.sem_inc(free, U)
            def turn(it):
                def radial(u):
                    hold(pe, (hr[u], it * 16 + 16), (msg, it * (K * U) + (K if u == 3 else 0)))
                    pe.matmul(e.ps[5 + u % 3][:, 0:2 * P], e.h3r[0:64, u, :], W4, start=True, stop=True).then_inc(w, 1)
                for u in range(3):
                    radial(u)
                for u in range(U):
                    blk = pe.value_load(e.blki[0:1, bass.ds(it * U + u, 1)], min_val=0, max_val=NB - 1)
                    hold(pe, (msg, it * (K * U) + K * (u + 1)), *([(scaled, it * U + (u + 1))] if second else []))
                    pe.matmul(e.acc[:, bass.ds(blk * D, D)], e.oh[:, u, :], e.gb2[:, u, :], start=False, stop=True,
                              skip_group_check=True).then_inc(free, 1)
                    if u == 0:
                        radial(3)
            turns(pe, NI, turn)

def take_sums(e, name, dst):
    taken = e.sem(f"{name}_taken")
    with e.nc.Block() as block:
        @block.vector
        def _(v):
            for b in range(NB):
                v.tensor_copy(dst[:, b, :], e.acc[:, b * D:(b + 1) * D]).then_inc(taken, 1)
            v.wait_ge(taken, NB)


def l1_out(e, first, second):
    nc = e.nc
    turned, copied, summed, taken = (e.sem(f"o_{f}") for f in ("turned", "copied", "summed", "taken"))
    scale = 1.0 / math.sqrt(2.0 * P) / 10.0
    with nc.Block() as block:
        @block.tensor
        def _(pe):
            for b in range(NB):
                for q, t in enumerate((first, second)):
                    k = 2 * b + q
                    if k >= 2:
                        pe.wait_ge(copied, k - 1)
                    for c in range(4):
                        i = pe.transpose(e.ps[k % 2][:, c * P:(c + 1) * P], t[:, b, c * P:(c + 1) * P], e.ident[:, :])
                    i.then_inc(turned, 1)
            for b in range(NB):
                pe.wait_ge(copied, 2 * b + 2)
                if b >= 2:
                    pe.wait_ge(taken, 2 * b - 2)
                ps = e.ps[2 + b % 2]
                for c, (k0, k1, W) in enumerate(((0, 7, e.Wo0), (4, 1, e.Wo1), (5, 2, e.Wo1), (6, 3, e.Wo1))):
                    pe.matmul(ps[:, c * P:(c + 1) * P], e.dT[:, k0, b * P:(b + 1) * P], W[:, 0, :], start=True, stop=False)
                    i = pe.matmul(ps[:, c * P:(c + 1) * P], e.dT[:, k1, b * P:(b + 1) * P], W[:, 1, :], start=False, stop=True)
                i.then_inc(summed, 1)

        @block.scalar
        def _(a):
            for b in range(NB):
                for q in range(2):
                    k = 2 * b + q
                    a.wait_ge(turned, k + 1)
                    a.activation(e.dT[:, 4 * q:4 * q + 4, b * P:(b + 1) * P], e.ps[k % 2].rearrange("p (c n) -> p c n", c=4),
                                 ACT.Copy).then_inc(copied, 1)

        @block.vector
        def _(v):
            for b in range(NB):
                v.wait_ge(summed, b + 1)
                ps = e.ps[2 + b % 2]
                v.scalar_tensor_tensor(out=e.x[:, b, 0:P], in0=ps[:, 0:P], scalar=scale, in1=e.x[:, b, 0:P],
                                       op0=ALU.mult, op1=ALU.add).then_inc(taken, 1)
                xv = e.x[:, b, P:D].rearrange("p (n m) -> p m n", m=3)
                v.scalar_tensor_tensor(out=xv, in0=ps[:, P:D].rearrange("p (m n) -> p m n", m=3), scalar=scale, in1=xv,
                                       op0=ALU.mult, op1=ALU.add).then_inc(taken, 1)



def l2_edges(e):
    H, HD = 16, 32
    nc = e.nc
    name = "e2"
    got = gather_sems(e, name, 2)
    egot = e.landed()
    vst = [e.sem(f"{name}_vst{u}") for u in range(U)]
    rst = [e.sem(f"{name}_rst{u}") for u in range(U)]
    (free, ta, eac, m1, added, st, vare, sdr, norm, xnr, tx, rl, m2k, m2v, vo, lgr, rt, rc) = (
        e.sem(f"{name}_{f}") for f in ("free", "ta", "eac", "m1", "added", "steps", "vare", "sd", "norm", "xn", "tx",
                                       "relu", "m2k", "m2v", "vout", "logits", "rowt", "rowc"))
    M1 = e.psum[:, 512:1536]
    LN = 10
    PR = 2
    qd, qt = e.sem("e2_qd"), e.sem("e2_qt")

    class T:

        def __init__(self, it, off):
            self.n, self.u, self.turn = it * U + off, off % U, it + off // U
            self.r = off % 2

    def steps_loop(eng, head, body, tail):
        head()
        def turn(it):
            for u in range(U):
                body(T(it, u + 2), T(it, u + 1), T(it, u), T(it, u + 3))
        turns(eng, (NT - 4) // U, turn)
        for s in (NT - 3, NT - 2):
            body(T(0, s + 1), T(0, s), T(0, s - 1), T(0, s + 2) if s + 2 < NT else None)
        tail(T(0, NT - 1), T(0, NT - 2))

    with nc.Block() as block:
        @block.gpsimd
        def _(g):
            def attr(g, t, u):
                g.dma_start(e.ea[:, u, :], e.rec[bass.ds(t * P, P), RS:RW]).then_inc(egot[u], 16)
            gather_loop(g, e, name, [(e.srcI, e.tkv, e.gkv), (e.dstI, e.tq2, e.qg)], free, got, attr)

        @block.sync
        def _(sp):
            def turn(it):
                for u in range(U):
                    hold(sp, (vo, it * U + (u + 1)))
                    sp.dma_start(e.vd[bass.ds((it * U + u) * P, P), :], e.vout[:, u, :]).then_inc(vst[u], 16)
                    hold(sp, (rc, it * U + (u + 1)))
                    sp.dma_start(e.rowd[0:H, bass.ds((it * U + u) * P, P)], e.rowb[0:H, u * P:(u + 1) * P]).then_inc(rst[u], 16)
            turns(sp, NI, turn)
            for u in range(U):
                sp.wait_ge(vst[u], 16 * NI)
                sp.wait_ge(rst[u], 16 * NI)

        @block.tensor
        def _(pe):
            def attributes(t):
                hold(pe, (egot[t.u], t.turn * 16 + 16), (eac, t.n))
                pe.transpose(e.ps[0][:, t.u * P:(t.u + 1) * P], e.ea[:, t.u, :], e.ident[:, :]).then_inc(ta, 1)

            def first(t):
                hold(pe, (eac, t.n + 1), (added, t.n))
                pe.matmul(e.ps[1][:, :], e.eaT[:, t.u, :], e.hkW1e[:, :], start=True, stop=True)
                pe.matmul(e.ps[2][:, :], e.eaT[:, t.u, :], e.hvW1e[:, :], start=True, stop=True).then_inc(m1, 1)

            def hidden(t):
                for k in range(2):
                    hold(pe, (xnr, 2 * t.n + k + 1), (rl, 2 * t.n))
                    for c in range(4 * k, 4 * k + 4):
                        i = pe.transpose(e.ps[3 + k][:, c % 4 * P:(c % 4 + 1) * P], e.hid[:, t.r, c * P:(c + 1) * P], e.ident[:, :])
                    i.then_inc(tx, 1)

            def second(t):
                hold(pe, (rl, 2 * t.n + 1), (lgr, t.n * (PR + 1)))
                for c in range(4):
                    i = pe.matmul(e.ps[5][:, :], e.hTe[:, t.r, c * P:(c + 1) * P], e.hkW2[:, c, :], start=(c == 0), stop=(c == 3))
                i.then_inc(m2k, 1)
                hold(pe, (rl, 2 * t.n + 2), (vo, t.n))
                for c in range(4):
                    i = pe.matmul(e.ps[6][:, :], e.hTe[:, t.r, (4 + c) * P:(5 + c) * P], e.hvW2[:, c, :], start=(c == 0), stop=(c == 3))
                i.then_inc(m2v, 1)

            def row(t):
                hold(pe, (lgr, t.n * (PR + 1) + (PR + 1)), (rc, t.n))
                pe.transpose(e.ps[7][0:H, t.u * P:(t.u + 1) * P], e.lg[:, t.u, 0:H], e.ident[:, :]).then_inc(rt, 1)

            pe.sem_inc(tx, 4)

            def head():
                attributes(T(0, 0))
                first(T(0, 0))
                attributes(T(0, 1))
                hidden(T(0, 0))
                first(T(0, 1))
                attributes(T(0, 2))
                second(T(0, 0))

            def body(t1, t0, tb, t2):
                hidden(t0)
                first(t1)
                if t2:
                    attributes(t2)
                second(t0)
                row(tb)

            def tail(t0, tb):
                hidden(t0)
                second(t0)
                row(tb)
                row(t0)
            steps_loop(pe, head, body, tail)

        @block.scalar
        def _(a):
            def turned_in(t):
                hold(a, (ta, t.n + 1))
                a.activation(e.eaT[:, t.u, :], e.ps[0][:, t.u * P:(t.u + 1) * P], ACT.Copy).then_inc(eac, 1)

            def root(t):
                hold(a, (vare, t.n + 1))
                a.activation(e.sd2[:, t.r, :], e.va2[:, t.r, :], ACT.Sqrt).then_inc(sdr, 1)

            def relu_in(t):
                for k in range(2):
                    hold(a, (tx, 2 * t.n + 5 + k))
                    a.activation(e.hTe[:, t.r, k * D:(k + 1) * D], e.ps[3 + k][:, :], ACT.Relu).then_inc(rl, 1)

            def value_out(t):
                hold(a, (m2v, t.n + 1), (vst[t.u], t.turn * 16))
                a.activation(e.vout[:, t.u, :], e.ps[6][:, :], ACT.Copy).then_inc(vo, 1)

            def row_out(t):
                hold(a, (rt, t.n + 1), (rst[t.u], t.turn * 16))
                a.activation(e.rowb[0:H, t.u * P:(t.u + 1) * P], e.ps[7][0:H, t.u * P:(t.u + 1) * P], ACT.Copy).then_inc(rc, 1)

            def head():
                turned_in(T(0, 0))
                turned_in(T(0, 1))
                root(T(0, 0))
                relu_in(T(0, 0))
                turned_in(T(0, 2))
                root(T(0, 1))
                value_out(T(0, 0))

            def body(t1, t0, tb, t2):
                relu_in(t0)
                if t2:
                    turned_in(t2)
                root(t1)
                value_out(t0)
                row_out(tb)

            def tail(t0, tb):
                relu_in(t0)
                value_out(t0)
                row_out(tb)
                row_out(t0)
            steps_loop(a, head, body, tail)

        @block.vector
        def _(v):
            def norms(t):
                at = t.n * LN
                hold(v, (m1, t.n + 1), (got[0][t.u], t.turn * 16 + 16), (tx, 2 * t.n + 2))
                hid = e.hid[:, t.r, :]
                v.tensor_tensor(hid, M1, e.gkv[:, t.u, :], ALU.add).then_inc(added, 1)
                hold(v, (added, t.n + 1))
                for k in range(2):
                    v.bn_stats(e.st2[:, t.r, k, :], hid[:, k * D:(k + 1) * D]).then_inc(st, 1)
                hold(v, (st, at + 2))
                for k in range(2):
                    v.bn_aggr(e.mv2[:, t.r, k, :], e.st2[:, t.r, k, :]).then_inc(st, 1)
                hold(v, (st, at + 4))
                v.tensor_scalar(e.va2[:, t.r, :], e.mv2[:, t.r, :, 1], EPS, None, ALU.add).then_inc(vare, 1)
                for k in range(2):
                    v.scalar_tensor_tensor(out=hid[:, k * D:(k + 1) * D], in0=hid[:, k * D:(k + 1) * D],
                                           scalar=e.mv2[:, t.r, k, 0:1], in1=e.gkvr[:, k * D:(k + 1) * D],
                                           op0=ALU.subtract, op1=ALU.mult).then_inc(st, 1)
                hold(v, (sdr, t.n + 1))
                v.reciprocal(e.rs2[:, t.r, :], e.sd2[:, t.r, :]).then_inc(st, 4)
                hold(v, (st, at + 10))
                for k in range(2):
                    v.scalar_tensor_tensor(out=hid[:, k * D:(k + 1) * D], in0=hid[:, k * D:(k + 1) * D],
                                           scalar=e.rs2[:, t.r, k:k + 1], in1=e.bkvr[:, k * D:(k + 1) * D],
                                           op0=ALU.mult, op1=ALU.add).then_inc(xnr, 1)

            def product(t):
                at = t.n * (PR + 1)
                hold(v, (m2k, t.n + 1), (got[1][t.u], t.turn * 16 + 16), (rt, t.turn * U))
                v.tensor_tensor(e.prod[:, :], e.ps[5][:, :], e.qg[:, t.u, 0:D], ALU.mult).then_inc(lgr, 1)
                hold(v, (lgr, at + 1))
                v.tensor_reduce(e.lg[:, t.u, 0:H], e.prod.rearrange("p (h d) -> p h d", h=H), AX.X, ALU.add).then_inc(lgr, 1)
                hold(v, (lgr, at + 2))
                v.tensor_tensor(e.lg[:, t.u, 0:H], e.lg[:, t.u, 0:H], e.qg[:, t.u, D:D + H], ALU.add).then_inc(lgr, 1)
                hold(v, (lgr, at + 3))
                v.sem_inc(free, 1)

            v.sem_inc(free, U)

            def head():
                norms(T(0, 0))
                norms(T(0, 1))
                product(T(0, 0))

            def body(t1, t0, tb, t2):
                norms(t1)
                product(t0)

            def tail(t0, tb):
                product(t0)
            steps_loop(v, head, body, tail)


def logits_l3(e):
    H = 8
    nc = e.nc
    got = gather_sems(e, "a3", 1)
    stored = e.sem("a3_stored")
    free, turned, rows, ready, st, dests = (e.sem(f"a3_{f}") for f in ("free", "turned", "rows", "ready", "steps", "dests"))
    with nc.Block() as block:
        @block.gpsimd
        def _(g):
            gather_loop(g, e, "a3", [(e.srcI, e.tes, e.sg)], free, got)

        @block.vector
        def _(v):
            v.sem_inc(free, U)

            def turn(it):
                for u in range(U):
                    hold(v, (got[0][u], it * 16 + 16), (dests, it + 1), (turned, it))
                    v.tensor_tensor(e.lg2[:, u, :], e.sg[:, u, :], e.ps[1][:, u * H:(u + 1) * H], ALU.add).then_inc(st, 1)
                    hold(v, (st, it * 5 + (u + 1)))
                    v.sem_inc(free, 1)
                v.scalar_tensor_tensor(out=e.lg3[:, :, :], in0=e.lg2[:, :, :], scalar=0.2, in1=e.lg2[:, :, :],
                                       op0=ALU.mult, op1=ALU.max).then_inc(st, 1)
                hold(v, (st, it * 5 + 5))
                v.tensor_tensor(e.lg[:, :, 0:H], e.lg3[:, :, :], e.fac[:, bass.ds(it * U, U), :], ALU.mult).then_inc(ready, 1)
            turns(v, NI, turn)

        @block.tensor
        def _(pe):
            def turn(it):
                hold(pe, (st, it * 5))
                for u in range(U):
                    i = at_destination(pe, e, e.ps[1][:, u * H:(u + 1) * H], it * U + u, e.ted3, 0, H)
                i.then_inc(dests, 1)
                row_transposes(pe, e, it, e.lg, H, ready, e.ps[0], rows, turned)
            turns(pe, NI, turn)

        @block.scalar
        def _(a):
            def turn(it):
                hold(a, (turned, it + 1), (stored, it * 16))
                a.activation(e.rowb[0:H, :], e.ps[0][0:H, :], ACT.Copy).then_inc(rows, 1)
            turns(a, NI, turn)

        @block.sync
        def _(sp):
            def turn(it):
                hold(sp, (rows, it + 1))
                sp.dma_start(e.rowd[0:H, bass.ds(it * (U * P), U * P)], e.rowb[0:H, :]).then_inc(stored, 16)
            turns(sp, NI, turn)
            sp.wait_ge(stored, 16 * NI)


def load(e, name, pairs, later=()):
    done = e.sem(f"{name}_loaded")
    with e.nc.Block() as block:
        @block.sync
        def _(sp):
            for tile, src in pairs:
                sp.dma_start(tile, src, allow_slow_non_contiguous=True).then_inc(done, 16)
            for sem, tile, src in later:
                sp.dma_start(tile, src).then_inc(sem, 16)
            sp.wait_ge(done, 16 * len(pairs))


def rows(w):
    return w.rearrange("(c p) n -> p c n", p=P)


def column(b):
    return b.rearrange("(c p) -> p c", p=P)


def line(b):
    return b.rearrange("(a n) -> a n", a=1)


def spread(b):
    return line(b).to_broadcast([P, b.shape[0]])


def program(nc, i, out):
    ctx = ExitStack()
    e = Env()
    e.nc = nc
    with ctx:
        uses = {}

        def sb(name, shape, dt=F32, scope=ctx):
            uses[name] = uses.get(name, 0) + 1
            t = scope.enter_context(nc.sbuf_tensor(f"{name}_{uses[name]}", shape, dt))
            return t

        sems = Env()
        sems.scope, sems.held = ctx.enter_context(ExitStack()), []

        def sem(name):
            handle = sems.scope.enter_context(nc.semaphore(name))
            sems.held.append(handle)
            return handle
        e.sem = sem
        sems.landed = [ctx.enter_context(nc.semaphore(f"landed{k}")) for k in range(12 * U)]
        sems.lent = 0

        def landed():
            sems.lent += U
            return sems.landed[sems.lent - U:sems.lent]
        e.landed = landed

        def renew():
            with nc.Block() as block:
                @block.gpsimd
                def _(g):
                    for handle in sems.held:
                        g.sem_clear(handle)
            sems.scope.close()
            sems.held.clear()

        def table(name, n, w):
            return nc.dram_tensor(f"d_{name}", [n, w], F32).ap()

        NN = NB * P
        e.rec = table("rec", SLOTS, RW)
        e.h3d = table("h3d", 64, SLOTS)
        e.dstd = table("dstd", SLOTS + 2, 1)
        e.rowd = table("rowd", 16, SLOTS)
        e.rowd2 = table("rowd2", 16, SLOTS)
        e.vd = table("vd", SLOTS, D)
        e.tq = table("tq", NN, D)
        e.tv = table("tv", NN, D)
        e.ts = table("ts", NN, D)
        e.th = table("th", NN, D)
        e.tkv = table("tkv", NN, 2 * D)
        e.tq2 = table("tq2", NN, D + 16)
        e.tes = table("tes", NN, 8)
        e.dlocd = table("dlocd", NT, P)

        e.psum = ctx.enter_context(nc.psum_tensor("psum", [P, 8 * 512], F32))
        e.ps = [e.psum[:, k * 512:(k + 1) * 512] for k in range(8)]
        e.acc = e.psum[:, 0:ACC]

        e.x = sb("x", [P, NB, D])
        e.h = sb("h", [P, NB, D])
        e.t0 = sb("t0", [P, NB, D])
        e.hT = sb("hT", [P, 4, NB * P])
        e.ident = sb("ident", [P, P])
        e.ones = sb("ones", [P, P])
        e.zeros = sb("zeros", [P, 512])
        e.lane = sb("lane", [P, P])
        e.srcI = sb("srcI", [P, NT], I32)
        e.dstI = sb("dstI", [P, NT], I32)
        e.blki = sb("blki", [P, NT], I32)
        e.dloc = sb("dloc", [P, NT])
        e.ohT = sb("ohT", [P, SLOTS], BF16)
        e.laneP = sb("laneP", [P, 1])
        e.asum = sb("asum", [P, NT, 8])
        e.fac = sb("fac", [P, NT, 8])
        e.srt = sb("srt", [P, NT, RS])
        e.pen = sb("pen", [P, 2, SEG])
        e.penF = sb("penF", [P, 16, SEG])
        e.penB = sb("penB", [P, 16, SEG])
        e.wrow = sb("wrow", [16, 2 * P])
        e.stats = sb("stats", [P, NB, 6])
        e.mv = sb("mv", [P, NB, 2])
        e.vare = sb("vare", [P, NB])
        e.sd = sb("sd", [P, NB])
        e.rstd = sb("rstd", [P, NB])
        e.nbias = sb("nbias", [P, NB])
        e.rden = sb("rden", [P, NB, 16])
        e.some = sb("some", [P, NB])
        e.idx = sb("idx", [P, 2, 2, IS], I32)
        e.lg = sb("lg", [P, U, 16])
        e.oh = sb("oh", [P, U, P])
        e.rowb = sb("rowb", [16, U * P])
        e.edge0 = sb("edge0", [P, 16])
        e.ends = sb("ends", [P, 16])
        e.carry = sb("carry", [16, P + 1])

        with ExitStack() as sc:
            e.PK = 12
            e.lower = sb("lower", [P, P], F32, sc)
            e.lowerb = sb("lowerb", [P, P], BF16, sc)
            e.window = sb("window", [P, 2 * EC], F32, sc)
            e.nodeno = sb("nodeno", [P, NB * P], F32, sc)
            e.tile_at = sb("tile_at", [P, NT], F32, sc)
            e.onesb = sb("onesb", [P, P], BF16, sc)
            e.zerosb = sb("zerosb", [P, 512], BF16, sc)
            e.phantom = sb("phantom", [P, e.PK, RW], F32, sc)
            e.srcs = sb("srcs", [EP, EC], I32, sc)
            e.dsts = sb("dsts", [EP, EC], I32, sc)
            e.kinds = sb("kinds", [EP, EC], I32, sc)
            e.weights = sb("weights", [EP, EC], F32, sc)
            e.a4 = sb("a4", [EP, EC, 4], F32, sc)
            e.a8 = sb("a8", [EP, EC, 8], F32, sc)
            e.a8n = sb("a8n", [EP, EC, 8], F32, sc)
            e.a128 = sb("a128", [EP, EC, P], F32, sc)
            e.small = sb("small", [EP, EC, RS], F32, sc)
            e.dstf = sb("dstf", [EP, EC], F32, sc)
            e.mark = sb("mark", [EP, U, NB * P], BF16, sc)
            e.cnt = sb("cnt", [P, NB * P], F32, sc)
            e.base = sb("base", [P, NB * P], F32, sc)
            e.bsum = sb("bsum", [P, NB], F32, sc)
            e.bsumi = sb("bsumi", [P, NB], I32, sc)
            e.btile = sb("btile", [P, NB], I32, sc)
            e.bsize = sb("bsize", [P, NB], F32, sc)
            e.bend = sb("bend", [P, NB], F32, sc)
            e.bstart = sb("bstart", [P, NB], F32, sc)
            e.blk = sb("blk", [P, NT], F32, sc)
            e.junk = sb("junk", [EP, 2, NB * P], F32, sc)
            e.slota = sb("slota", [EP, EC], F32, sc)
            e.slotb = sb("slotb", [EP, EC], F32, sc)
            e.sloti = sb("sloti", [EP, EC], I32, sc)
            e.recbuf = sb("recbuf", [EP, U, RW], F32, sc)
            e.slotbuf = sb("slotbuf", [EP, U], I32, sc)
            e.dstT = sb("dstT", [P, P], F32, sc)
            e.guard = sb("guard", [1, 2], F32, sc)
            e.seg3 = sb("seg3", [P, 3, SEG], F32, sc)
            e.whole = sb("whole", [P, 2], F32, sc)
            e.fack = sb("fack", [P, NT, 8], F32, sc)
            e.emb = sb("emb", [P, 8, 8], F32, sc)
            e.loads0 = [(e.emb.rearrange("p k h -> p (k h)"),
                         i["L3_gnn_et_emb"].rearrange("k (h a) -> a (k h)", a=1).to_broadcast([P, 64]))]
            e.ROWS_AT = 42
            prepare(e, i)
            lowb = e.sem("lowb")
            with nc.Block() as block:
                @block.vector
                def _(v):
                    v.tensor_copy(e.lowerb[:, :], e.lower[:, :]).then_inc(lowb, 1)
                    v.wait_ge(lowb, 1)
            count_edges(e)
            place_edges(e)
            scatter_records(e)
            load_sorted(e)
            e.oht_st = e.sem("oht_stored")
            with ExitStack() as s2:
                e.spread = sb("spread", [P, 2, SLOTS // 6], F32, s2)
                turned_marks(e)

        renew()
        with ExitStack() as sc:
            e.h1 = sb("h1", [P, NB, D], F32, sc)
            e.g1c = sb("g1c", [P, 4], F32, sc)
            e.b1lc = sb("b1lc", [P, 4], F32, sc)
            e.g2c = sb("g2c", [P, 4], F32, sc)
            e.b2lc = sb("b2lc", [P, 4], F32, sc)
            s1 = ExitStack()
            e.tk3 = sb("tk3", [P, NB, 3, D], BF16, s1)
            with ExitStack() as s2:
                e.rest = sb("rest", [P, NB, D], F32, s2)
                e.Wqkv = sb("Wqkv", [P, 4, 3 * D], F32, s2)
                e.bqkv = sb("bqkv", [1, 3 * D], F32, s2)
                e.tq_ = sb("tq_", [P, NB, D], F32, s2)
                e.tk_ = sb("tk_", [P, NB, D], F32, s2)
                e.tv_ = sb("tv_", [P, NB, D], F32, s2)
                load(e, "w0a", [(e.Wqkv[:, :, :], rows(i["L0_gnn_Wqkv"])), (e.bqkv[:, :], line(i["L0_gnn_bqkv"])),
                                (e.g1c[:, :], column(i["L0_gnn_ln1_g"])), (e.b1lc[:, :], column(i["L0_gnn_ln1_b"])),
                                (e.g2c[:, :], column(i["L0_gnn_ln2_g"])), (e.b2lc[:, :], column(i["L0_gnn_ln2_b"]))])
                node_ln(e, "n0", e.x, e.h, ACT.Relu)

                def evac0(v, b, n, ps):
                    if n == 0:
                        return v.tensor_scalar(e.tq_[:, b, :], ps[:, :], float(D) ** -0.5, None, ALU.mult)
                    return v.tensor_copy((e.tk_, e.tv_)[n - 1][:, b, :], ps[:, :])
                node_linear(e, "qkv", [e.t0], e.hT, (e.g1c, e.b1lc), ACT.Identity,
                            [(e.Wqkv[:, :, n * D:(n + 1) * D], e.bqkv[0:1, n * D:(n + 1) * D]) for n in range(3)],
                            evac0, ln=(e.h, e.t0))
                split_table(e, "tk", e.tk3, e.tk_, D)
                store_table(e, "t0", [(e.tq, e.tq_[:, :, :]), (e.tv, e.tv_[:, :, :])])
            with ExitStack() as s2:
                edge_buffers(e, sb, s2)
                logits_l0(e)
                segment_softmax(e, "s0", 8, False)
                weighted_sums(e, "b0", 8, e.tv)
                divide_sums(e, "d0", 8, "max")
            s1.close()
            with ExitStack() as s2:
                e.Wo = sb("Wo", [P, 4, D], F32, s2)
                e.bor = sb("bor", [1, D], F32, s2)
                e.W1 = sb("W1", [P, 4, 4 * D], F32, s2)
                e.b1c = sb("b1c", [P, 16], F32, s2)
                e.W2 = sb("W2", [P, 16, D], F32, s2)
                e.b2r = sb("b2r", [1, D], F32, s2)
                e.uT = sb("uT", [P, 4, NB * P], F32, s2)
                e.W1_in, e.W2_in = e.sem("W1_in"), e.sem("W2_in")
                load(e, "w0b", [(e.Wo[:, :, :], rows(i["L0_gnn_Wo"])), (e.bor[:, :], line(i["L0_gnn_bo"])),
                                (e.b1c[:, :], column(i["L0_gnn_b1"]))],
                     [(e.W1_in, e.W1[:, :, :], rows(i["L0_gnn_W1"])), (e.W2_in, e.W2[:, :, :], rows(i["L0_gnn_W2"])),
                      (e.W2_in, e.b2r[:, :], line(i["L0_gnn_b2"]))])
                node_linear(e, "wo", [e.t0], e.hT, None, ACT.Copy, [(e.Wo[:, :, :], e.bor[0:1, :])],
                            lambda v, b, n, ps: v.tensor_tensor(e.h1[:, b, :], ps[:, :], e.h[:, b, :], ALU.add))
                node_linear(e, "ln2", [e.t0], e.hT, (e.g2c, e.b2lc), ACT.Identity, [], None, ln=(e.h1, e.t0))
                ffn(e)

        renew()
        with ExitStack() as sc:
            edge_buffers(e, sb, sc, rows_too=False)
            e.Wup0 = sb("Wup0", [P, P], F32, sc)
            e.Wup1 = sb("Wup1", [P, P], F32, sc)
            e.Wm1 = sb("Wm1", [8, 64], F32, sc)
            e.Wm2 = sb("Wm2", [64, 64], F32, sc)
            e.Wm3 = sb("Wm3", [64, 64], F32, sc)
            e.Wm4 = sb("Wm4", [64, 512], F32, sc)
            e.Wo0 = sb("Wo0", [P, 2, P], F32, sc)
            e.Wo1 = sb("Wo1", [P, 2, P], F32, sc)
            e.fin = sb("fin", [P, U, 8], F32, sc)
            e.fT = sb("fT", [8, 512], F32, sc)
            e.hh1 = sb("hh1", [64, 512], F32, sc)
            e.hh2 = sb("hh2", [64, 512], F32, sc)
            e.h3 = sb("h3", [64, U * P], F32, sc)
            e.h3r = sb("h3r", [64, U, P], F32, sc)
            e.t2 = sb("t2", [P, U, P], F32, sc)
            e.dot = sb("dot", [P, 3, P], F32, sc)
            e.dT = sb("dT", [P, 8, NB * P], F32, sc)
            load(e, "w1", [(e.Wup0[:, :], i["L1_gnn_W_up0"]), (e.Wup1[:, :], i["L1_gnn_W_up1"]), (e.Wm1[:, :], i["L1_gnn_W_mlp1"]),
                           (e.Wm2[:, :], i["L1_gnn_W_mlp2"]), (e.Wm3[:, :], i["L1_gnn_W_mlp3"]), (e.Wm4[:, :], i["L1_gnn_W_mlp4"]),
                           (e.Wo0[:, :, :], rows(i["L1_gnn_W_out0"])), (e.Wo1[:, :, :], rows(i["L1_gnn_W_out1"]))])
            node_ln(e, "n1", e.x, e.h, ACT.Relu)
            l1_table(e)
            store_table(e, "t1", [(e.ts, e.t0[:, :, :])])
            l1_mlp(e)
            l1_pass(e, "p1", False)
            take_sums(e, "p1", e.h)
            l1_pass(e, "p2", True)
            take_sums(e, "p2", e.t0)
            l1_out(e, e.h, e.t0)

        renew()
        with ExitStack() as sc:
            e.hvb2 = sb("hvb2", [P, D], F32, sc)
            with ExitStack() as s2:
                e.hkW1e = sb("hkW1e", [P, D], F32, s2)
                e.hvW1e = sb("hvW1e", [P, D], F32, s2)
                e.hkW2 = sb("hkW2", [P, 4, D], F32, s2)
                e.hvW2 = sb("hvW2", [P, 4, D], F32, s2)
                e.gkvr = sb("gkvr", [P, 2 * D], F32, s2)
                e.bkvr = sb("bkvr", [P, 2 * D], F32, s2)
                with ExitStack() as s3:
                    e.hkW1 = sb("hkW1", [P, 4, D], F32, s3)
                    e.hvW1 = sb("hvW1", [P, 4, D], F32, s3)
                    e.hqW1 = sb("hqW1", [P, 4, D], F32, s3)
                    e.hqW2 = sb("hqW2", [P, 4, D], F32, s3)
                    e.hkb1 = sb("hkb1", [1, D], F32, s3)
                    e.hvb1 = sb("hvb1", [1, D], F32, s3)
                    e.hqb1 = sb("hqb1", [1, D], F32, s3)
                    e.hqb2 = sb("hqb2", [1, D], F32, s3)
                    e.gqc = sb("gqc", [P, 4], F32, s3)
                    e.bqc = sb("bqc", [P, 4], F32, s3)
                    e.hkb2 = sb("hkb2", [P, D], F32, s3)
                    e.tkv_ = sb("tkv_", [P, NB, 2 * D], F32, s3)
                    e.tq2_ = sb("tq2_", [P, NB, D + 16], F32, s3)
                    load(e, "w2a", [(e.hkW1[:, :, :], rows(i["L2_gnn_hk_W1"][0:D, :])), (e.hkW1e[:, :], i["L2_gnn_hk_W1"][D:D + P, :]),
                                    (e.hvW1[:, :, :], rows(i["L2_gnn_hv_W1"][0:D, :])), (e.hvW1e[:, :], i["L2_gnn_hv_W1"][D:D + P, :]),
                                    (e.hkW2[:, :, :], rows(i["L2_gnn_hk_W2"])), (e.hvW2[:, :, :], rows(i["L2_gnn_hv_W2"])),
                                    (e.hqW1[:, :, :], rows(i["L2_gnn_hq_W1"])), (e.hqW2[:, :, :], rows(i["L2_gnn_hq_W2"])),
                                    (e.hkb1[:, :], line(i["L2_gnn_hk_b1"])), (e.hvb1[:, :], line(i["L2_gnn_hv_b1"])),
                                    (e.hqb1[:, :], line(i["L2_gnn_hq_b1"])), (e.hqb2[:, :], line(i["L2_gnn_hq_b2"])),
                                    (e.gkvr[:, 0:D], spread(i["L2_gnn_hk_g"])), (e.gkvr[:, D:2 * D], spread(i["L2_gnn_hv_g"])),
                                    (e.bkvr[:, 0:D], spread(i["L2_gnn_hk_be"])), (e.bkvr[:, D:2 * D], spread(i["L2_gnn_hv_be"])),
                                    (e.gqc[:, :], column(i["L2_gnn_hq_g"])), (e.bqc[:, :], column(i["L2_gnn_hq_be"])),
                                    (e.hkb2[:, :], spread(i["L2_gnn_hk_b2"])), (e.hvb2[:, :], spread(i["L2_gnn_hv_b2"]))])
                    node_ln(e, "n2", e.x, e.h, ACT.Relu)

                    def evac2(v, b, n, ps):
                        if n < 2:
                            return v.tensor_copy(e.tkv_[:, b, n * D:(n + 1) * D], ps[:, :])
                        return v.tensor_copy(e.t0[:, b, :], ps[:, :])
                    node_linear(e, "kv1", [e.h], e.hT, None, ACT.Copy,
                                [(e.hkW1[:, :, :], e.hkb1[0:1, :]), (e.hvW1[:, :, :], e.hvb1[0:1, :]),
                                 (e.hqW1[:, :, :], e.hqb1[0:1, :])], evac2)
                    node_linear(e, "q2", [e.t0], e.hT, (e.gqc, e.bqc), ACT.Relu, [(e.hqW2[:, :, :], e.hqb2[0:1, :])],
                                lambda v, b, n, ps: v.tensor_scalar(e.tq2_[:, b, 0:D], ps[:, :], 1.0 / math.sqrt(32.0), None, ALU.mult),
                                ln=(e.t0, e.t0))
                    dots = e.sem("qb2")
                    with nc.Block() as block:
                        @block.vector
                        def _(v):
                            for b in range(NB):
                                v.tensor_tensor(e.t0[:, b, :], e.tq2_[:, b, 0:D], e.hkb2[:, :], ALU.mult).then_inc(dots, 1)
                            v.wait_ge(dots, NB)
                            for b in range(NB):
                                v.tensor_reduce(e.tq2_[:, b, D:D + 16], e.t0[:, b, :].rearrange("p (h d) -> p h d", h=16),
                                                AX.X, ALU.add).then_inc(dots, 1)
                            v.wait_ge(dots, 2 * NB)
                    store_table(e, "t2", [(e.tkv, e.tkv_[:, :, :]), (e.tq2, e.tq2_[:, :, :])])
                with ExitStack() as s3:
                    e.ea = sb("ea", [P, U, P], F32, s3)
                    e.eaT = sb("eaT", [P, U, P], F32, s3)
                    e.gkv = sb("gkv", [P, U, 2 * D], F32, s3)
                    e.qg = sb("qg", [P, U, D + 16], F32, s3)
                    e.hid = sb("hid", [P, 2, 2 * D], F32, s3)
                    e.hTe = sb("hTe", [P, 2, 2 * D], F32, s3)
                    e.prod = sb("prod", [P, D], F32, s3)
                    e.vout = sb("vout", [P, U, D], F32, s3)
                    e.st2 = sb("st2", [P, 2, 2, 6], F32, s3)
                    e.mv2 = sb("mv2", [P, 2, 2, 2], F32, s3)
                    e.va2 = sb("va2", [P, 2, 2], F32, s3)
                    e.sd2 = sb("sd2", [P, 2, 2], F32, s3)
                    e.rs2 = sb("rs2", [P, 2, 2], F32, s3)
                    e.nb2 = sb("nb2", [P, 2, 2], F32, s3)
                    l2_edges(e)
                edge_buffers(e, sb, s2)
                segment_softmax(e, "s2", 16, False)
                weighted_sums(e, "b2", 16, None)
                divide_sums(e, "d2", 16, "max", bias=e.hvb2[:, :])
            with ExitStack() as s2:
                e.noW1 = sb("noW1", [P, 8, D], F32, s2)
                e.noW2 = sb("noW2", [P, 4, D], F32, s2)
                e.nob1 = sb("nob1", [1, D], F32, s2)
                e.nob2 = sb("nob2", [1, D], F32, s2)
                e.gnc = sb("gnc", [P, 4], F32, s2)
                e.bnc = sb("bnc", [P, 4], F32, s2)
                e.catT = sb("catT", [P, 8, NB * P], F32, s2)
                e.t1 = sb("t1", [P, NB, D], F32, s2)
                load(e, "w2b", [(e.noW1[:, :, :], rows(i["L2_gnn_no_W1"])), (e.noW2[:, :, :], rows(i["L2_gnn_no_W2"])),
                                (e.nob1[:, :], line(i["L2_gnn_no_b1"])), (e.nob2[:, :], line(i["L2_gnn_no_b2"])),
                                (e.gnc[:, :], column(i["L2_gnn_no_g"])), (e.bnc[:, :], column(i["L2_gnn_no_be"]))])
                node_linear(e, "no1", [e.t0, e.h], e.catT, None, ACT.Copy, [(e.noW1[:, :, :], e.nob1[0:1, :])],
                            lambda v, b, n, ps: v.tensor_tensor(e.t1[:, b, :], ps[:, :], e.zeros[:, :], ALU.add))
                xh = e.sem("xh")
                with nc.Block() as block:
                    @block.vector
                    def _(v):
                        for b in range(NB):
                            v.tensor_tensor(e.x[:, b, :], e.x[:, b, :], e.h[:, b, :], ALU.add).then_inc(xh, 1)
                        v.wait_ge(xh, NB)
                node_linear(e, "no2", [e.t1], e.hT, (e.gnc, e.bnc), ACT.Relu, [(e.noW2[:, :, :], e.nob2[0:1, :])],
                            lambda v, b, n, ps: v.tensor_tensor(e.x[:, b, :], ps[:, :], e.x[:, b, :], ALU.add),
                            ln=(e.t1, e.t1))

        renew()
        with ExitStack() as sc:
            edge_buffers(e, sb, sc)
            e.W3 = sb("W3", [P, 4, D], F32, sc)
            e.W3T = sb("W3T", [P, 4, D], F32, sc)
            e.asrc = sb("asrc", [P, D], F32, sc)
            e.adst = sb("adst", [P, D], F32, sc)
            e.gamma = sb("gamma", [P, D], F32, sc)
            e.beta = sb("beta", [P, D], F32, sc)
            e.tes_ = sb("tes_", [P, NB, 8], F32, sc)
            e.ted_ = sb("ted_", [P, NB, 8], F32, sc)
            e.t1 = sb("t1", [P, NB, D], F32, sc)
            e.ted3 = sb("ted3", [P, NB, 3, 8], BF16, sc)
            e.rest = sb("rest", [P, NB, 8], F32, sc)
            e.sg = sb("sg", [P, U, 8], F32, sc)
            e.dg = sb("dg", [P, U, 8], F32, sc)
            e.lg2 = sb("lg2", [P, U, 8], F32, sc)
            e.lg3 = sb("lg3", [P, U, 8], F32, sc)
            load(e, "w3", [(e.W3[:, :, :], rows(i["L3_gnn_W"])),
                           (e.asrc[:, :], spread(i["L3_gnn_a_src"].rearrange("h d -> (h d)"))),
                           (e.adst[:, :], spread(i["L3_gnn_a_dst"].rearrange("h d -> (h d)"))),
                           (e.gamma[:, :], spread(i["L3_gnn_ln_gamma"])), (e.beta[:, :], spread(i["L3_gnn_ln_beta"]))])
            node_ln(e, "n3", e.x, e.h, ACT.Relu)
            wt_, wc_ = e.sem("w3_turned"), e.sem("w3_copied")
            with nc.Block() as block:
                @block.tensor
                def _(pe):
                    for c in range(4):
                        for r in range(4):
                            k = pe.transpose(e.ps[c][:, r * P:(r + 1) * P], e.W3[:, r, c * P:(c + 1) * P], e.ident[:, :])
                        k.then_inc(wt_, 1)

                @block.vector
                def _(v):
                    for c in range(4):
                        v.wait_ge(wt_, c + 1)
                        v.tensor_copy(e.W3T[:, c, :], e.ps[c][:, :]).then_inc(wc_, 1)
            node_linear(e, "l3", [e.h], e.hT, None, ACT.Copy, [(e.W3T[:, :, :], None)],
                        lambda v, b, n, ps: v.tensor_copy(e.t0[:, b, :], ps[:, :]))
            dots3 = e.sem("dots3")
            with nc.Block() as block:
                @block.vector
                def _(v):
                    st = Steps(v, dots3)
                    for vec, dst in ((e.asrc, e.tes_), (e.adst, e.ted_)):
                        for b in range(NB):
                            st(v.tensor_tensor(e.t1[:, b, :], e.t0[:, b, :], vec[:, :], ALU.mult))
                        st.settle()
                        for b in range(NB):
                            st(v.tensor_reduce(dst[:, b, :], e.t1[:, b, :].rearrange("p (h d) -> p h d", h=8), AX.X, ALU.add))
                        st.settle()
            split_table(e, "ted", e.ted3, e.ted_, 8)
            store_table(e, "t3", [(e.th, e.t0[:, :, :]), (e.tes, e.tes_[:, :, :])])
            logits_l3(e)
            segment_softmax(e, "s3", 8, True)
            weighted_sums(e, "b3", 8, e.th)
            divide_sums(e, "d3", 8, "add")
            fin = e.sem("fin")
            with nc.Block() as block:
                @block.vector
                def _(v):
                    for b in range(NB):
                        v.tensor_tensor(e.t0[:, b, :], e.t0[:, b, :], e.h[:, b, :], ALU.add).then_inc(fin, 1)
                    v.wait_ge(fin, NB)
            node_ln(e, "n4", e.t0, e.t1, ACT.Identity)
            stored = e.sem("stored")
            with nc.Block() as block:
                @block.vector
                def _(v):
                    st = Steps(v, fin, NB)
                    for op, vec in ((ALU.mult, e.gamma), (ALU.add, e.beta)):
                        for b in range(NB):
                            st(v.tensor_tensor(e.t1[:, b, :], e.t1[:, b, :], vec[:, :], op))
                        st.settle()
                    for b in range(NB):
                        st(v.tensor_tensor(e.x[:, b, :], e.t1[:, b, :], e.x[:, b, :], ALU.add))
                    st.settle()

                @block.sync
                def _(sp):
                    sp.wait_ge(fin, 4 * NB)
                    sp.dma_start(out[0:(NB - 1) * P, :].rearrange("(b p) n -> p b n", p=P), e.x[:, 0:NB - 1, :]).then_inc(stored, 16)
                    sp.dma_start(out[(NB - 1) * P:NODES, :], e.x[0:NODES - (NB - 1) * P, NB - 1, :]).then_inc(stored, 16)
                    sp.wait_ge(stored, 32)


def edge_buffers(e, sb, scope, rows_too=True):
    e.gb0 = sb("gb0", [P, U, D], F32, scope)
    e.gb2 = sb("gb2", [P, U, D], F32, scope)
    if rows_too:
        e.wt = sb("wt", [P, NT, 16], F32, scope)
        e.segA = sb("segA", [P, 16 * SEG], F32, scope)
        e.segF = sb("segF", [P, 16 * SEG], F32, scope)
        e.segB = sb("segB", [P, 16 * SEG], F32, scope)


def kernel(**inputs):
    import numpy as _np
    import concourse.bacc as _bacc
    from concourse import mybir as _mybir
    from concourse.bass_utils import run_bass_kernel_spmd as _run

    nc = _bacc.Bacc("TRN2", target_bir_lowering=False, num_devices=1)
    arrays, args = {}, {}
    for name, a in inputs.items():
        a = _np.ascontiguousarray(a)
        arrays[f"in_{name}"] = a
        args[name] = nc.dram_tensor(f"in_{name}", a.shape, _mybir.dt.from_np(a.dtype), kind="ExternalInput").ap()
    out = nc.dram_tensor("out_0", (NODES, D), _mybir.dt.float32, kind="ExternalOutput").ap()
    program(nc, args, out)
    r = _run(nc, [arrays], core_ids=[0])
    return r.results[0]["out_0"]
```

```python
import math
from contextlib import ExitStack

import concourse.bass as bass
from concourse import mybir

F32 = mybir.dt.float32
I32 = mybir.dt.int32
BF16 = mybir.dt.bfloat16
F32R = mybir.dt.float32r
ALU = mybir.AluOpType
ACT = mybir.ActivationFunctionType
AX = mybir.AxisListType

P = 128
NODES, D = 625, 512
NB = 5
EDGES = 10000
EP, EC = 125, 80
NT = EDGES // P + 1 + NB
U = 4
NI = NT // U
IS = 6
RING = 2 * IS
RT = RING // U
SC = 8
PAIRS = RING // 2
PAIR_BANKS = 3
SLOTS = NT * P
PAD_NODE = NODES
F_SRC, F_DST, F_W, F_TYPE, F_A4, F_A8, F_A8N, F_ID = 0, 1, 2, 3, 4, 8, 16, 24
RS = 25
SEG = SLOTS // P
BIG = 1.0e30
EPS = 1e-5
ACC = NB * D


class Env:
    pass


def hold(eng, *waits):
    waits = [(sem, value) for sem, value in waits if not (isinstance(value, int) and value <= 0)]
    for sem, value in waits:
        eng.wait_ge(sem, value)
    if waits:
        eng.nop(nofuse=True)


def turns(eng, n, body):
    body(0)
    with eng.Fori(1, n) as it:
        body(it)


def ring_turns(eng, body, between=None):
    for r in range(RT):
        body(r, r, 0)
    if between:
        between()
    with eng.Fori(1, NI // RT) as big:
        for r in range(RT):
            body(big * RT + r, r, big)


class Steps:

    def __init__(self, eng, sem, base=0):
        self.eng, self.sem, self.base, self.n = eng, sem, base, 0

    def __call__(self, ins):
        ins.then_inc(self.sem, 1)
        self.n += 1

    def settle(self):
        hold(self.eng, (self.sem, self.base + self.n))



def ln_vector(v, e, s, src):
    for b in range(NB):
        v.bn_stats(e.stats[:, b, :], src[:, b, :]).then_inc(s.stats, 1)
    for b in range(NB):
        v.wait_ge(s.stats, b + 1)
        v.bn_aggr(e.mv[:, b, :], e.stats[:, b, :]).then_inc(s.aggr, 1)
    v.wait_ge(s.aggr, NB)
    v.tensor_scalar(e.vare[:, :], e.mv[:, :, 1], EPS, None, ALU.add).then_inc(s.vare, 1)
    v.wait_ge(s.sd, 1)
    v.reciprocal(e.rstd[:, :], e.sd[:, :]).then_inc(s.rstd, 1)
    v.wait_ge(s.rstd, 1)
    v.scalar_tensor_tensor(out=e.nbias[:, :], in0=e.mv[:, :, 0], scalar=-1.0, in1=e.rstd[:, :],
                           op0=ALU.mult, op1=ALU.mult).then_inc(s.norm, 1)


def ln_scalar(a, e, s, src, dst, func):
    a.wait_ge(s.vare, 1)
    a.activation(e.sd[:, :], e.vare[:, :], ACT.Sqrt).then_inc(s.sd, 1)
    a.wait_ge(s.norm, 1)
    for b in range(NB):
        a.activation(dst[:, b, :], src[:, b, :], func, bias=e.nbias[:, b:b + 1],
                     scale=e.rstd[:, b:b + 1]).then_inc(s.normed, 1)


def ln_sems(e, name):
    s = Env()
    s.stats, s.aggr, s.vare, s.sd = e.sem(f"{name}_stats"), e.sem(f"{name}_aggr"), e.sem(f"{name}_vare"), e.sem(f"{name}_sd")
    s.rstd, s.norm, s.normed = e.sem(f"{name}_rstd"), e.sem(f"{name}_norm"), e.sem(f"{name}_normed")
    return s


def node_ln(e, name, src, dst, func):
    s = ln_sems(e, name)
    with e.nc.Block() as block:
        @block.vector
        def _(v):
            ln_vector(v, e, s, src)

        @block.scalar
        def _(a):
            ln_scalar(a, e, s, src, dst, func)


def node_linear(e, name, srcs, dstT, gb, funcT, lin, evac, ln=None, needs=(), before=None):
    nc = e.nc
    s = ln_sems(e, name) if ln else None
    turned, copied = e.sem(f"{name}_turned"), e.sem(f"{name}_copied")
    summed, taken = e.sem(f"{name}_summed"), e.sem(f"{name}_taken")
    chunks = [(t, c) for t in srcs for c in range(4)]
    KC = len(chunks)
    G = KC // 4
    R = 4
    with nc.Block() as block:
        @block.vector
        def _(v):
            if ln:
                ln_vector(v, e, s, ln[0])
            hold(v, *needs)
            if before:
                steps = Steps(v, e.sem(f"{name}_before"))
                before(v, steps)
                steps.settle()
            g = 0
            for b in range(NB):
                for n in range(len(lin)):
                    v.wait_ge(summed, g + 1)
                    evac(v, b, n, e.ps[2 + g % R]).then_inc(taken, 1)
                    g += 1

        @block.scalar
        def _(a):
            if ln:
                ln_scalar(a, e, s, ln[0], ln[1], ACT.Identity)
            if gb is not None:
                hold(a, *needs)
            for b in range(NB):
                for q in range(G):
                    k = b * G + q
                    a.wait_ge(turned, k + 1)
                    ps = e.ps[k % 2].rearrange("p (c n) -> p c n", c=4)
                    if gb is None:
                        a.activation(dstT[:, 4 * q:4 * q + 4, b * P:(b + 1) * P], ps[:, :, :],
                                     funcT).then_inc(copied, 1)
                    else:
                        for c in range(4):
                            i = a.activation(dstT[:, 4 * q + c, b * P:(b + 1) * P], ps[:, c, :], funcT,
                                             scale=gb[0][:, c:c + 1], bias=gb[1][:, c:c + 1])
                        i.then_inc(copied, 1)

        @block.tensor
        def _(pe):
            def turn(b):
                for q in range(G):
                    k = b * G + q
                    if ln and q == 0:
                        pe.wait_ge(s.normed, b + 1)
                    if k >= 2:
                        pe.wait_ge(copied, k - 1)
                    for c in range(4):
                        t, cc = chunks[4 * q + c]
                        i = pe.transpose(e.ps[k % 2][:, c * P:(c + 1) * P], t[:, b, cc * P:(cc + 1) * P],
                                         e.ident[:, :])
                    i.then_inc(turned, 1)
            turn(0)
            hold(pe, *needs)
            g = 0
            for b in range(NB):
                if b + 1 < NB:
                    turn(b + 1)
                pe.wait_ge(copied, (b + 1) * G)
                for n, (w, bias) in enumerate(lin):
                    if g >= R:
                        pe.wait_ge(taken, g - R + 1)
                    ps = e.ps[2 + g % R]
                    for k in range(KC):
                        i = pe.matmul(ps[:, :], dstT[:, k, b * P:(b + 1) * P], w[:, k, :],
                                      start=(k == 0), stop=(k == KC - 1 and bias is None))
                    if bias is not None:
                        i = pe.matmul(ps[:, :], e.ones[0:1, :], bias, start=False, stop=True)
                    i.then_inc(summed, 1)
                    g += 1


def store_table(e, name, pairs):
    done = e.sem(f"{name}_stored")
    with e.nc.Block() as block:
        @block.sync
        def _(sp):
            for table, tile in pairs:
                sp.dma_start(table.rearrange("(b p) n -> p b n", p=P), tile).then_inc(done, 16)
            sp.wait_ge(done, 16 * len(pairs))



def prepare(e, i):
    nc = e.nc
    built, loaded, filled = e.sem("built"), e.sem("loaded"), e.sem("filled")
    ph_ready = e.sem("phantom_ready")
    with nc.Block() as block:
        @block.gpsimd
        def _(g):
            g.memset(e.ident[:, :], 0.0).then_inc(built, 1)
            g.memset(e.lower[:, :], 0.0).then_inc(built, 1)
            g.memset(e.window[:, :], 1.0).then_inc(built, 1)
            g.memset(e.x[:, NB - 1, :], 0.0).then_inc(built, 1)
            g.wait_ge(built, 4)
            g.affine_select(out=e.ident[:, :], in_=e.ident[:, :], compare_op=ALU.not_equal, fill=1.0,
                            base=0, pattern=[[-1, P]], channel_multiplier=1).then_inc(built, 1)
            g.affine_select(out=e.lower[:, :], in_=e.lower[:, :], compare_op=ALU.is_ge, fill=1.0,
                            base=0, pattern=[[-1, P]], channel_multiplier=1).then_inc(built, 1)
            g.affine_select(out=e.window[:, :], in_=e.window[:, :], compare_op=ALU.is_ge, fill=0.0,
                            base=EC - 1, pattern=[[-1, 2 * EC]], channel_multiplier=0).then_inc(built, 1)
            g.iota(e.nodeno[:, :], pattern=[[1, NB * P]], base=0, channel_multiplier=0,
                   allow_small_or_imprecise_dtypes=True).then_inc(built, 1)
            g.iota(e.lane[:, :], pattern=[[1, P]], base=0, channel_multiplier=0,
                   allow_small_or_imprecise_dtypes=True).then_inc(built, 1)
            g.iota(e.laneP[:, :], pattern=[[0, 1]], base=0, channel_multiplier=1,
                   allow_small_or_imprecise_dtypes=True).then_inc(built, 1)
            g.iota(e.tile_at[:, :], pattern=[[P, NT]], base=0, channel_multiplier=0,
                   allow_small_or_imprecise_dtypes=True).then_inc(built, 1)
            g.iota(e.small[:, :, F_ID:F_ID + 1], pattern=[[1, EC], [0, 1]], base=0, channel_multiplier=EC,
                   allow_small_or_imprecise_dtypes=True).then_inc(built, 1)
            g.wait_ge(built, 12)

        @block.vector
        def _(v):
            steps = Steps(v, e.sem("prep_steps"))
            steps(v.memset(e.phantom[:, :, :], 0.0))
            steps(v.memset(e.ones[:, :], 1.0))
            steps(v.memset(e.zeros[:, :], 0.0))
            steps(v.memset(e.onesb[:, :], 1.0))
            steps(v.memset(e.zerosb[:, :], 0.0))
            steps.settle()
            v.memset(e.phantom[:, :, F_DST:F_DST + 1], float(PAD_NODE)).then_inc(ph_ready, 1)

        @block.sync
        def _(sp):
            sp.wait_ge(ph_ready, 1)
            sp.dma_start(e.rec.rearrange("(p j) f -> p (j f)", p=P), e.phantom.rearrange("p j f -> p (j f)")).then_inc(filled, 16)
            sp.wait_ge(filled, 16)

        @block.scalar
        def _(a):
            a.wait_ge(built, 4)
            a.dma_start(e.x[:, 0:NB - 1, :], i["x"][0:(NB - 1) * P, :].rearrange("(b p) n -> p b n", p=P)).then_inc(loaded, 16)
            a.dma_start(e.x[0:NODES - (NB - 1) * P, NB - 1, :], i["x"][(NB - 1) * P:NODES, :]).then_inc(loaded, 16)
            for tile, src in ((e.srcs, i["src"]), (e.dsts, i["dst"]), (e.kinds, i["edge_type_8"]), (e.weights, i["edge_weight"])):
                a.dma_start(tile[:, :], src.rearrange("(p c) -> p c", c=EC)).then_inc(loaded, 16)
            for tile, src in ((e.a4, i["edge_attr_4"]), (e.a8, i["edge_attr_8"]), (e.a8n, i["edge_attr_8_n2"])):
                a.dma_start(tile[:, :, :], src.rearrange("(p c) f -> p c f", c=EC)).then_inc(loaded, 16)
            for tile, src in e.loads0:
                a.dma_start(tile, src).then_inc(loaded, 16)
            a.wait_ge(loaded, 16 * (9 + len(e.loads0)))


def count_edges(e):
    nc = e.nc
    fields = e.sem("fields")
    marked, used, cleared = e.sem("cnt_marked"), e.sem("cnt_used"), e.sem("cnt_cleared")
    with nc.Block() as block:
        @block.vector
        def _(v):
            for at, n, src in ((F_SRC, 1, e.srcs), (F_DST, 1, e.dsts), (F_TYPE, 1, e.kinds), (F_W, 1, e.weights)):
                v.tensor_copy(e.small[:, :, at:at + 1], src[:, :, None]).then_inc(fields, 1)
            for at, n, src in ((F_A4, 4, e.a4), (F_A8, 8, e.a8), (F_A8N, 8, e.a8n)):
                v.tensor_copy(e.small[:, :, at:at + n], src[:, :, :]).then_inc(fields, 1)
            v.tensor_copy(e.dstf[:, :], e.dsts[:, :]).then_inc(fields, 1)
            v.wait_ge(fields, 8)
            def turn(it):
                for u in range(U):
                    hold(v, (used, it * U + (u + 1)))
                    v.tensor_scalar(e.mark[:, u, :], e.nodeno[0:EP, :], e.dstf[:, bass.ds(it * U + u, 1)], None,
                                    ALU.is_equal).then_inc(marked, 1)
            turns(v, EC // U, turn)

        @block.tensor
        def _(pe):
            outs = ((e.ps[0][:, :], e.ps[2][:, :], 0, 512), (e.ps[1][:, 0:P], e.ps[3][:, 0:P], 512, 640))
            for cnt, pre, a, b in outs:
                pe.matmul(cnt, e.zerosb[:, 0:P], e.zerosb[:, 0:b - a], start=True, stop=True)
                pe.matmul(pre, e.zerosb[:, 0:P], e.zerosb[:, 0:b - a], start=True, stop=True)
            pe.sem_inc(used, U)
            def turn(it):
                for u in range(U):
                    hold(pe, (marked, it * U + (u + 1)))
                    for cnt, pre, a, b in outs:
                        pe.matmul(cnt, e.onesb[0:EP, 0:P], e.mark[:, u, a:b], start=False, stop=True,
                                  skip_group_check=True)
                        i = pe.matmul(pre, e.lowerb[0:EP, :], e.mark[:, u, a:b], start=False, stop=True,
                                      skip_group_check=True)
                    i.then_inc(used, 1)
            turns(pe, EC // U, turn)

def place_edges(e):
    nc = e.nc
    with nc.Block() as block:
        @block.vector
        def _(v):
            steps = Steps(v, e.sem("place_steps"))
            steps(v.tensor_copy(e.cnt[:, 0:512], e.ps[0][:, :]))
            steps(v.tensor_copy(e.cnt[:, 512:640], e.ps[1][:, 0:P]))
            steps(v.memset(e.blk[:, :], 0.0))
            steps.settle()
            steps(v.tensor_reduce(e.bsum[:, :], e.cnt.rearrange("p (b n) -> p b n", b=NB), AX.X, ALU.add))
            steps.settle()
            steps(v.tensor_scalar(e.bsumi[:, :], e.bsum[:, :], float(P - 1), None, ALU.add))
            steps.settle()
            steps(v.tensor_scalar(e.btile[:, :], e.bsumi[:, :], 7, 7, ALU.arith_shift_right, ALU.logical_shift_left))
            steps.settle()
            steps(v.tensor_copy(e.bsize[:, :], e.btile[:, :]))
            steps.settle()
            steps(v.tensor_tensor_scan(e.bend[:, :], e.zeros[:, 0:NB], e.bsize[:, :], 0.0, ALU.add, ALU.add))
            steps.settle()
            steps(v.tensor_tensor(e.bstart[:, :], e.bend[:, :], e.bsize[:, :], ALU.subtract))
            steps.settle()
            for b in range(NB):
                steps(v.tensor_tensor_scan(e.base[:, b * P:(b + 1) * P], e.zeros[:, 0:P],
                                           e.cnt[:, b * P:(b + 1) * P], e.bstart[:, b:b + 1], ALU.add, ALU.add))
            for b in range(1, NB):
                steps.settle()
                steps(v.scalar_tensor_tensor(out=e.blk[:, :], in0=e.tile_at[:, :], scalar=e.bstart[:, b:b + 1],
                                             in1=e.blk[:, :], op0=ALU.is_ge, op1=ALU.add))
            steps.settle()
            steps(v.tensor_copy(e.blki[:, :], e.blk[:, :]))
            steps(v.tensor_tensor(e.base[:, :], e.base[:, :], e.cnt[:, :], ALU.subtract))
            steps.settle()
            steps(v.tensor_tensor(e.base[:, 0:512], e.base[:, 0:512], e.ps[2][:, :], ALU.add))
            steps(v.tensor_tensor(e.base[:, 512:640], e.base[:, 512:640], e.ps[3][:, 0:P], ALU.add))
            steps.settle()


class QueriesKeysValues:
    SLOTS = 4
    BANKS = 4

    def __init__(self, e):
        self.e = e
        self.ln = ln_sems(e, "qkv")
        self.turned, self.copied, self.summed, self.taken = (
            e.sem(f"qkv_{f}") for f in ("turned", "copied", "summed", "taken"))
        self.stored = [e.sem(f"qkv_stored{k}") for k in range(self.SLOTS)]

    def vector(self, v):
        ln_vector(v, self.e, self.ln, self.e.h)

    def keys_in_parts(self, v):
        e = self.e
        v.wait_ge(self.taken, 3 * NB)
        split3(v, Steps(v, e.sem("tk_split")), e, e.tk3, e.tk_, D)

    def scalar(self, a):
        e = self.e
        ln_scalar(a, e, self.ln, e.h, e.t0, ACT.Identity)

        def turn(b):
            a.wait_ge(self.turned, b + 1)
            for c in range(4):
                i = a.activation(e.hT[:, c, b * P:(b + 1) * P], e.ps[b % 2][:, c * P:(c + 1) * P], ACT.Identity,
                                 scale=e.g1c[:, c:c + 1], bias=e.b1lc[:, c:c + 1])
            i.then_inc(self.copied, 1)

        turn(0)
        for b in range(NB):
            if b + 1 < NB:
                turn(b + 1)
            for n in range(3):
                a.wait_ge(self.summed, 3 * b + n + 1)
                ps = e.ps[2 + (3 * b + n) % self.BANKS]
                if n == 1:
                    a.activation(e.tk_[:, b, :], ps[:, :], ACT.Copy).then_inc(self.taken, 1)
                    continue
                k = 2 * b + n // 2
                if k >= self.SLOTS:
                    a.wait_ge(self.stored[k % self.SLOTS], 16 * (k // self.SLOTS))
                a.activation(e.tout[:, k % self.SLOTS, :], ps[:, :], ACT.Copy,
                             scale=float(D) ** -0.5 if n == 0 else 1.0).then_inc(self.taken, 1)

    def tensor(self, pe):
        e = self.e

        def turn(b):
            pe.wait_ge(self.ln.normed, b + 1)
            if b >= 2:
                pe.wait_ge(self.copied, b - 1)
            for c in range(4):
                i = pe.transpose(e.ps[b % 2][:, c * P:(c + 1) * P], e.t0[:, b, c * P:(c + 1) * P], e.ident[:, :])
            i.then_inc(self.turned, 1)

        turn(0)
        pe.wait_ge(e.Wqkv_in, 32)
        for b in range(NB):
            if b + 1 < NB:
                turn(b + 1)
            pe.wait_ge(self.copied, b + 1)
            for n in range(3):
                g = 3 * b + n
                if g >= self.BANKS:
                    pe.wait_ge(self.taken, g - self.BANKS + 1)
                ps = e.ps[2 + g % self.BANKS]
                for k in range(4):
                    pe.matmul(ps[:, :], e.hT[:, k, b * P:(b + 1) * P], e.Wqkv[:, k, n * D:(n + 1) * D],
                              start=(k == 0), stop=False)
                pe.matmul(ps[:, :], e.ones[0:1, :], e.bqkv[0:1, n * D:(n + 1) * D], start=False,
                          stop=True).then_inc(self.summed, 1)

    def sync(self, sp):
        e = self.e
        for k in range(2 * NB):
            b, n = k // 2, k % 2 * 2
            sp.wait_ge(self.taken, 3 * b + n + 1)
            sp.dma_start((e.tq if n == 0 else e.tv)[b * P:(b + 1) * P, :], e.tout[:, k % self.SLOTS, :]
                         ).then_inc(self.stored[k % self.SLOTS], 16)
        for k in range(self.SLOTS):
            sp.wait_ge(self.stored[k], 16 * len(range(k, 2 * NB, self.SLOTS)))


def scatter_records(e, nodes):
    nc = e.nc
    rank, slots, staged = e.sem("rank"), e.sem("rec_slots"), e.sem("rec_staged")
    written = [e.landed() + e.landed() for half in range(2)]
    with nc.Block() as block:
        def column_turns(eng, body):
            for half in range(2):
                body(half, half, 0)
            with eng.Fori(1, EC // SC // 2) as k:
                for half in range(2):
                    body(k * 2 + half, half, k)

        @block.tensor
        def _(pe):
            nodes.tensor(pe)

        @block.scalar
        def _(a):
            nodes.scalar(a)

        @block.sync
        def _(sp):
            nodes.sync(sp)

        @block.vector
        def _(v):
            nodes.vector(v)

            def turn(it, half, k):
                hold(v, (slots, it))
                for j in range(SC):
                    c = it * SC + j
                    if j == SC // 2:
                        hold(v, (rank, it * (2 * SC) + SC))
                    v.scalar_tensor_tensor(out=e.junk[:, j % (SC // 2), :], in0=e.nodeno[0:EP, :],
                                           scalar=e.dstf[:, bass.ds(c, 1)], in1=e.base[0:EP, :], op0=ALU.is_equal,
                                           op1=ALU.mult, accum_out=e.slota[:, j:j + 1]).then_inc(rank, 1)
                    v.scalar_tensor_tensor(out=e.junkw[:, j % (SC // 2), :], in0=e.dstf[:, :],
                                           scalar=e.dstf[:, bass.ds(c, 1)], in1=e.window[0:EP, bass.ds(EC - c, EC)],
                                           op0=ALU.is_equal, op1=ALU.mult,
                                           accum_out=e.slotb[:, j:j + 1]).then_inc(rank, 1)
                hold(v, (rank, it * (2 * SC) + 2 * SC), *[(sem, k * 16) for sem in written[half]])
                v.tensor_tensor(e.slotbuf[:, half, :], e.slota[:, :], e.slotb[:, :], ALU.add).then_inc(slots, 1)
            column_turns(v, turn)
            nodes.keys_in_parts(v)

        @block.gpsimd
        def _(g):
            def turn(it, half, k):
                hold(g, *[(sem, k * 16) for sem in written[half]])
                g.tensor_copy(e.recbuf[:, half, :, :], e.small[:, bass.ds(it * SC, SC), :]).then_inc(staged, 1)
                hold(g, (slots, it + 1), (staged, it + 1))
                for j in range(SC):
                    g.indirect_dma_start(e.rec[:, :], bass.IndirectOffsetOnAxis(ap=e.slotbuf[:, half, j:j + 1], axis=0),
                                         e.recbuf[:, half, j, :], None).then_inc(written[half][j], 16)
            column_turns(g, turn)
            for half in range(2):
                for sem in written[half]:
                    g.wait_ge(sem, 16 * (EC // SC // 2))


def load_sorted(e):
    nc = e.nc
    local, out, back = e.sem("oht_local"), e.sem("oht_out"), [e.sem(f"oht_back{k}") for k in range(2)]
    stored, read = e.sem("oht_stored"), e.sem("oht_read")
    C = SLOTS // 6
    flat = e.dlocd.rearrange("t p -> (t p)").rearrange("(a n) -> a n", a=1)
    ld, dt, dd = e.sem("srt_loaded"), e.sem("srt_turned"), e.sem("srt_dst")
    sv, emb = e.sem("srt_steps"), e.sem("srt_row")
    with nc.Block() as block:
        @block.sync
        def _(sp):
            sp.dma_start(e.srt[:, :, :], e.rec.rearrange("(t p) f -> p t f", p=P)).then_inc(ld, 16)
            sp.wait_ge(sv, 2)
            sp.dma_start(e.dstd[1:1 + SLOTS, :].rearrange("(t p) a -> t (p a)", p=P), e.dstT[0:NT, :]).then_inc(dd, 16)
            sp.dma_start(e.dstd[0:1, :], e.guard[0:1, 0:1]).then_inc(dd, 16)
            sp.dma_start(e.dstd[SLOTS + 1:SLOTS + 2, :], e.guard[0:1, 1:2]).then_inc(dd, 16)
            sp.wait_ge(dd, 48)
            for k in range(3):
                sp.dma_start(e.seg3[:, k, :], e.dstd[k:k + SLOTS, :].rearrange("(p j) a -> p (j a)", p=P)).then_inc(dd, 16)
            sp.wait_ge(out, 1)
            sp.dma_start(e.dlocd[:, :], e.dlocT[0:NT, :]).then_inc(stored, 16)
            sp.wait_ge(stored, 16)
            for c in range(6):
                if c >= 2:
                    sp.wait_ge(read, c - 1)
                sp.dma_start(e.spread[:, c % 2, :], flat[:, c * C:(c + 1) * C].to_broadcast([P, C])).then_inc(back[c % 2], 16)

        @block.tensor
        def _(pe):
            pe.wait_ge(ld, 16)
            pe.transpose(e.ps[0][0:NT, 0:P], e.srt[:, :, F_DST], e.ident[:, :]).then_inc(dt, 1)
            pe.wait_ge(sv, 6)
            pe.transpose(e.ps[2][0:NT, 0:P], e.dloc[:, :], e.ident[:, :]).then_inc(local, 1)
            pe.wait_ge(sv, e.ROWS_AT)
            for k in range(2):
                i = pe.matmul(e.ps[1][0:16, k * P:(k + 1) * P], e.whole[:, k:k + 1].to_broadcast([P, 16]), e.ident[:, :],
                              start=True, stop=True)
            i.then_inc(emb, 1)

        @block.vector
        def _(v):
            st = Steps(v, sv)
            v.wait_ge(dt, 1)
            st(v.tensor_copy(e.dstT[0:NT, :], e.ps[0][0:NT, 0:P]))
            st(v.memset(e.guard[0:1, :], -7.0))
            v.wait_ge(ld, 16)
            st(v.tensor_copy(e.srcI[:, :], e.srt[:, :, F_SRC]))
            st(v.tensor_copy(e.dstI[:, :], e.srt[:, :, F_DST]))
            st(v.tensor_copy(e.idI[:, :], e.srt[:, :, F_ID]))
            st(v.scalar_tensor_tensor(out=e.dloc[:, :], in0=e.blk[:, :], scalar=-float(P), in1=e.srt[:, :, F_DST],
                                      op0=ALU.mult, op1=ALU.add))
            st(v.tensor_tensor(e.asum[:, :, :], e.srt[:, :, F_A8:F_A8 + 8], e.srt[:, :, F_A8N:F_A8N + 8], ALU.add))
            v.wait_ge(local, 1)
            v.tensor_copy(e.dlocT[0:NT, :], e.ps[2][0:NT, 0:P]).then_inc(out, 1)
            v.wait_ge(dd, 96)
            st(v.tensor_tensor(e.pen[:, 0, :], e.seg3[:, 1, :], e.seg3[:, 0, :], ALU.is_equal))
            st(v.tensor_tensor(e.pen[:, 1, :], e.seg3[:, 1, :], e.seg3[:, 2, :], ALU.is_equal))
            st.settle()
            st(v.tensor_scalar(e.pen[:, :, :], e.pen[:, :, :], -1.0, BIG, ALU.add, ALU.mult))
            st.settle()
            st(v.tensor_reduce(e.whole[:, :], e.pen[:, :, :], AX.X, ALU.min))
            for h in range(16):
                st(v.tensor_copy(e.penF[:, h, :], e.pen[:, 0, :]))
                st(v.tensor_copy(e.penB[:, h, :], e.pen[:, 1, :]))
            st.settle()
            st(v.memset(e.penF[:, :, 0:1], -BIG))
            st(v.memset(e.penB[:, :, SEG - 1:SEG], -BIG))
            assert st.n >= e.ROWS_AT
            v.wait_ge(emb, 1)
            st(v.tensor_copy(e.wrow[0:16, :], e.ps[1][0:16, 0:2 * P]))
            st(v.memset(e.fac[:, :, :], 1.0))
            st.settle()
            for k in range(8):
                st(v.scalar_tensor_tensor(out=e.fack[:, :, :], in0=e.srt[:, :, F_TYPE:F_TYPE + 1].to_broadcast([P, NT, 8]),
                                          scalar=float(k), in1=e.emb[:, k:k + 1, :].to_broadcast([P, NT, 8]),
                                          op0=ALU.is_equal, op1=ALU.mult))
                st.settle()
                st(v.tensor_tensor(e.fac[:, :, :], e.fac[:, :, :], e.fack[:, :, :], ALU.add))
                st.settle()
            st(v.tensor_tensor(e.fac[:, :, :], e.fac[:, :, :], e.srt[:, :, F_W:F_W + 1].to_broadcast([P, NT, 8]), ALU.mult))
            st.settle()
            for c in range(6):
                v.wait_ge(back[c % 2], 16 * (c // 2 + 1))
                v.tensor_scalar(e.ohT[:, c * C:(c + 1) * C], e.spread[:, c % 2, :], e.laneP[:, 0:1], None,
                                ALU.is_equal).then_inc(read, 1)



def segment_softmax(e, name, H, floor_zero):
    nc = e.nc
    io, sv = e.sem(f"{name}_io"), e.sem(f"{name}_steps")
    turned, ex = e.sem(f"{name}_turned"), e.sem(f"{name}_exp")
    W = H * SEG
    A = e.segA[:, 0:W]
    Fw = e.segF[:, 0:W]
    A3 = A.rearrange("p (h j) -> p h j", h=H)
    F3 = Fw.rearrange("p (h j) -> p h j", h=H)
    penF = e.penF[:, 0:H, :].rearrange("p h j -> p (h j)")
    penB = e.penB[:, 0:H, :].rearrange("p h j -> p (h j)")
    marks = {}
    with nc.Block() as block:
        @block.vector
        def _(v):
            st = Steps(v, sv)
            v.wait_ge(io, 16)
            st(v.tensor_copy(e.edge0[:, 0:H], A3[:, :, 0]))
            st(v.tensor_tensor_scan(Fw, penF, A, -BIG, ALU.add, ALU.max))
            st.settle()
            st(v.tensor_copy(e.ends[:, 0:H], F3[:, :, SEG - 1]))
            marks["f"] = st.n
            st(v.memset(e.carry[0:H, 0:1], -BIG))
            v.wait_ge(turned, 1)
            st(v.tensor_tensor_scan(e.carry[0:H, 1:P + 1], e.wrow[0:H, 0:P], e.ps[0][0:H, 0:P], -BIG, ALU.add, ALU.max))
            marks["fc"] = st.n
            v.wait_ge(turned, 2)
            st(v.scalar_tensor_tensor(out=A3[:, :, 0], in0=e.ps[1][:, 0:H], scalar=e.pen[:, 0, 0:1], in1=e.edge0[:, 0:H],
                                      op0=ALU.add, op1=ALU.max))
            st.settle()
            st(v.tensor_tensor_scan(Fw, penF, A, -BIG, ALU.add, ALU.max))
            st.settle()
            st(v.tensor_copy(A3[:, :, 0], e.edge0[:, 0:H]))
            st(v.tensor_tensor_scan(e.segB[:, 0:W][:, ::-1], penB[:, ::-1], Fw[:, ::-1], -BIG, ALU.add, ALU.max))
            st.settle()
            st(v.tensor_copy(e.ends[:, 0:H], e.segB[:, 0:W].rearrange("p (h j) -> p h j", h=H)[:, :, 0]))
            marks["b"] = st.n
            st(v.memset(e.carry[0:H, P:P + 1], -BIG))
            v.wait_ge(turned, 3)
            st(v.tensor_tensor_scan(e.carry[0:H, 0:P][:, ::-1], e.wrow[0:H, P:2 * P][:, ::-1],
                                    e.ps[0][0:H, 0:P][:, ::-1], -BIG, ALU.add, ALU.max))
            marks["bc"] = st.n
            v.wait_ge(turned, 4)
            st(v.scalar_tensor_tensor(out=F3[:, :, SEG - 1], in0=e.ps[1][:, 0:H], scalar=e.pen[:, 1, SEG - 1:SEG],
                                      in1=F3[:, :, SEG - 1], op0=ALU.add, op1=ALU.max))
            st.settle()
            st(v.tensor_tensor_scan(e.segB[:, 0:W][:, ::-1], penB[:, ::-1], Fw[:, ::-1], -BIG, ALU.add, ALU.max))
            st.settle()
            if floor_zero:
                st(v.tensor_scalar(e.segB[:, 0:W], e.segB[:, 0:W], 0.0, None, ALU.max))
                st.settle()
            v.tensor_tensor(A, A, e.segB[:, 0:W], ALU.subtract).then_inc(ex, 1)

        @block.tensor
        def _(pe):
            for k, m in enumerate(("f", "fc", "b", "bc")):
                pe.wait_ge(sv, marks[m])
                if k % 2 == 0:
                    i = pe.transpose(e.ps[0][0:H, 0:P], e.ends[:, 0:H], e.ident[:, :])
                else:
                    a = 0 if k == 1 else 1
                    i = pe.transpose(e.ps[1][:, 0:H], e.carry[0:H, a:a + P], e.ident[0:H, 0:H])
                i.then_inc(turned, 1)

        @block.scalar
        def _(a):
            a.wait_ge(ex, 1)
            a.activation(A, A, ACT.Exp).then_inc(ex, 1)

        @block.sync
        def _(sp):
            sp.dma_start(A3, e.rowd[0:H, 0:SLOTS].rearrange("h (p j) -> p h j", p=P)).then_inc(io, 16)
            sp.wait_ge(ex, 2)
            sp.dma_start(e.rowd2[0:H, 0:SLOTS].rearrange("h (p j) -> p h j", p=P), A3).then_inc(io, 16)
            sp.wait_ge(io, 32)


def gather_loop(g, e, name, fetches, free, got, extra=None, ring=RING, K=1):
    cols = e.sem(f"{name}_cols")
    F, S = len(fetches), IS

    def turn(it):
        for half in range(2):
            first = it * (2 * S) + half * S
            hold(g, (free, first * K - S * K))
            for k, (index, table, buf) in enumerate(fetches):
                g.tensor_copy(e.idx[:, k, half, :], index[:, bass.ds(first, S)]).then_inc(cols, 1)
            hold(g, (cols, it * (2 * F) + (half + 1) * F))
            for j in range(S):
                u = (half * S + j) % ring
                hold(g, (free, first * K + (j + 1 - ring) * K))
                for k, (index, table, buf) in enumerate(fetches):
                    g.indirect_dma_start(buf[:, u, :], None, table[:, :],
                                         bass.IndirectOffsetOnAxis(ap=e.idx[:, k, half, j:j + 1], axis=0)).then_inc(got[k][u], 16)
                if extra:
                    extra(g, first + j, u)
    turns(g, NT // (2 * S), turn)


class RingRows:

    def __init__(self, e):
        self.sems, self.base = e.ring_landed, e.ring_base.count
        e.ring_base.count += 16 * (NT // RING)

    def of_turn(self, r, big):
        return [self.of_tile(r * U + u, big) for u in range(U)]

    def of_tile(self, slot, big):
        return (self.sems[slot], big * 16 + (self.base + 16))


def row_transposes(pe, e, it, lg, H, lg_ready, ps, row_free, turned):
    hold(pe, (lg_ready, it + 1), (row_free, it))
    for u in range(U):
        i = pe.transpose(ps[0:H, u * P:(u + 1) * P], lg[:, u, 0:H], e.ident[:, :])
    i.then_inc(turned, 1)


def split3(v, st, e, dst, src, width):
    for k in range(3):
        left = src if k == 0 else e.rest
        st(v.tensor_copy(dst[:, :, k, 0:width], left[:, :, 0:width]))
        st.settle()
        if k < 2:
            st(v.tensor_tensor(e.rest[:, :, 0:width], left[:, :, 0:width], dst[:, :, k, 0:width], ALU.subtract))
            st.settle()


def split_table(e, name, dst, src, width):
    with e.nc.Block() as block:
        @block.vector
        def _(v):
            split3(v, Steps(v, e.sem(f"{name}_split")), e, dst, src, width)


def node_blocks(e, t, n):
    loads, blocks = e.nc.values_load_multi_w_load_instructions(
        e.blki[0:1, bass.ds(t, n)], engines=[mybir.EngineType.PE], min_val=0, max_val=NB - 1)
    return blocks


def at_destination(pe, e, ps, t, blk, table, a, b):
    for k in range(3):
        i = pe.matmul(ps, e.ohT[:, bass.ds(t * P, P)], table[:, bass.ds(blk, 1), k, a:b].rearrange("p a n -> p (a n)"),
                      start=(k == 0), stop=(k == 2))
    return i


def logits_l0(e, mlp):
    H, BANKS = 8, 3
    nc = e.nc
    got = RingRows(e)
    turned, rows, keys, stored = e.sem("a0_turned"), e.sem("a0_rows"), e.sem("a0_keys"), e.sem("a0_stored")
    ready, summed, multiplied = e.sem("a0_ready"), e.sem("a0_summed"), e.sem("a0_multiplied")

    def bank(r, u):
        return e.ps[1 + (r * U + u) % BANKS]

    with nc.Block() as block:
        @block.gpsimd
        def _(g):
            gather_loop(g, e, "a0", [(e.srcI, e.tq, e.gb0)], multiplied, [got.sems])

        @block.vector
        def _(v):
            def turn(it, r, big):
                for u in range(U):
                    hold(v, got.of_tile(r * U + u, big), (keys, it * U + (u + 1)), *([(summed, it)] if u == 0 else []))
                    v.tensor_tensor(e.gb2[:, u, :], e.gb0[:, r * U + u, :], bank(r, u)[:, :], ALU.mult).then_inc(multiplied, 1)
                hold(v, (multiplied, it * U + U), (turned, it))
                v.tensor_reduce(e.lg[:, :, 0:H], e.gb2[:, :, :].rearrange("p u (h d) -> p u h d", h=H), AX.X,
                                ALU.add).then_inc(summed, 1)
                hold(v, (summed, it + 1))
                v.tensor_tensor(e.lg[:, :, 0:H], e.lg[:, :, 0:H], e.asum[:, bass.ds(it * U, U), :], ALU.add).then_inc(ready, 1)
            ring_turns(v, turn)

        @block.tensor
        def _(pe):
            def key(it, r, u, blk):
                hold(pe, (multiplied, it * U + (u + 1 - BANKS)))
                at_destination(pe, e, bank(r, u)[:, :], it * U + u, blk, e.tk3, 0, D).then_inc(keys, 1)

            def turn(it, r, peeled):
                more = not (peeled and it == NI - 1)
                layers = mlp.tensor(pe, it, peeled)
                blks = node_blocks(e, (it + 1) * U, U) if more else None
                for u in range(U):
                    if more:
                        key(it + 1, (r + 1) % RT, u, blks[u])
                    if u < len(layers):
                        layers[u]()
                row_transposes(pe, e, it, e.lg, H, ready, e.ps[0], rows, turned)

            for u, blk in enumerate(node_blocks(e, 0, U)):
                key(0, 0, u, blk)
            for r in range(2 * RT):
                turn(r, r % RT, True)
            with pe.Fori(2, NI // RT - 1) as big:
                for r in range(RT):
                    turn(big * RT + r, r, False)
            for r in range(RT):
                turn(NI - RT + r, r, True)
            for s in range(NI, NI + mlp.LEAD):
                for layer in mlp.tensor(pe, s, True):
                    layer()

        @block.scalar
        def _(a):
            def turn(it, peeled):
                for layer in mlp.scalar(a, it, peeled):
                    layer()
                hold(a, (turned, it + 1), (stored, it * 16))
                a.activation(e.rowb[0:H, :], e.ps[0][0:H, :], ACT.Copy).then_inc(rows, 1)

            for it in range(2 * RT):
                turn(it, True)
            with a.Fori(2 * RT, NI - RT) as it:
                turn(it, False)
            for it in range(NI - RT, NI):
                turn(it, True)
            for s in range(NI, NI + mlp.LEAD):
                for layer in mlp.scalar(a, s, True):
                    layer()

        @block.sync
        def _(sp):
            def turn(it):
                mlp.sync(sp, it - mlp.LEAD)
                hold(sp, (rows, it + 1))
                sp.dma_start(e.rowd[0:H, bass.ds(it * (U * P), U * P)], e.rowb[0:H, :]).then_inc(stored, 16)

            for it in range(mlp.LEAD + 1):
                turn(it)
            with sp.Fori(mlp.LEAD + 1, NI) as it:
                turn(it)
            for s in range(NI, NI + mlp.LEAD):
                mlp.sync(sp, s - mlp.LEAD)
            sp.wait_ge(stored, 16 * NI)
            sp.wait_ge(mlp.stored, 16 * NI)


SILU_2MOM = 1.679177


class RadialLayers:
    LEAD = 4

    def __init__(self, e):
        self.e = e
        (self.stored, self.fin, self.ft, self.ftc, self.mm1, self.a1, self.mm2, self.a2, self.mm3, self.a3) = (
            e.sem(f"m_{f}") for f in ("stored", "fields", "turned", "copied", "mm1", "a1", "mm2", "a2", "mm3", "a3"))

    def stages(self, s, peeled, stages):
        def bind(stage, t):
            return lambda: stage(t)
        return [bind(stage, s - behind) for behind, stage in stages if not peeled or 0 <= s - behind < NI]

    def scalar(self, a, s, peeled):
        e = self.e

        def fields(t):
            hold(a, (self.ft, t))
            a.activation(e.fin[:, :, :], e.srt[:, bass.ds(t * U, U), F_A8:F_A8 + 8], ACT.Copy).then_inc(self.fin, 1)

        def turned(t):
            hold(a, (self.ft, t + 1), (self.mm1, t))
            a.activation(e.fT[0:8, :], e.ps[4][0:8, :], ACT.Copy).then_inc(self.ftc, 1)

        def silu(t, done, used, ps, dst, by, signal):
            hold(a, (done, t + 1), used)
            a.activation(dst[0:64, :], ps[0:64, :], ACT.Silu, scale=by).then_inc(signal, 1)

        return self.stages(s, peeled, [
            (4, lambda t: silu(t, self.mm3, (self.stored, t * 16), e.ps[7], e.h3, SILU_2MOM / 8.0, self.a3)),
            (3, lambda t: silu(t, self.mm2, (self.mm3, t), e.ps[6], e.hh2, SILU_2MOM / 8.0, self.a2)),
            (2, lambda t: silu(t, self.mm1, (self.mm2, t), e.ps[5], e.hh1, 1.0 / math.sqrt(8.0), self.a1)),
            (1, turned), (0, fields)])

    def tensor(self, pe, s, peeled):
        e = self.e

        def turn_fields(t):
            hold(pe, (self.fin, t + 1), (self.ftc, t))
            for u in range(U):
                i = pe.transpose(e.ps[4][0:8, u * P:(u + 1) * P], e.fin[:, u, :], e.ident[:, :])
            i.then_inc(self.ft, 1)

        def layer(t, units, taken, ps, w, src, signal):
            hold(pe, (units, t + 1), (taken, t))
            pe.matmul(ps[0:64, :], w, src, start=True, stop=True).then_inc(signal, 1)

        return self.stages(s, peeled, [
            (4, lambda t: layer(t, self.a2, self.a3, e.ps[7], e.Wm3[0:64, :], e.hh2[0:64, :], self.mm3)),
            (3, lambda t: layer(t, self.a1, self.a2, e.ps[6], e.Wm2[0:64, :], e.hh1[0:64, :], self.mm2)),
            (2, lambda t: layer(t, self.ftc, self.a1, e.ps[5], e.Wm1[0:8, :], e.fT[0:8, :], self.mm1)),
            (1, turn_fields)])

    def sync(self, sp, t):
        e = self.e
        if not (isinstance(t, int) and t < 0):
            hold(sp, (self.a3, t + 1))
            sp.dma_start(e.h3d[:, bass.ds(t * (U * P), U * P)], e.h3[0:64, :]).then_inc(self.stored, 16)


def weighted_sums(e, name, H, table, prefetch=()):
    DH = D // H
    nc = e.nc
    got = RingRows(e) if table is not None else [e.sem(f"{name}_got{r}") for r in range(RT)]
    used, rowin, wts = e.sem(f"{name}_used"), e.sem(f"{name}_rowin"), e.sem(f"{name}_weights")
    turned, oh, msg = e.sem(f"{name}_turned"), e.sem(f"{name}_marks"), e.sem(f"{name}_msgs")
    with nc.Block() as block:
        if table is not None:
            @block.gpsimd
            def _(g):
                gather_loop(g, e, name, [(e.srcI, table, e.gb0)], msg, [got.sems])
        else:
            @block.sync
            def _(sp):
                def turn(it, r, big):
                    hold(sp, (msg, (it - RT + 1) * U))
                    sp.dma_start(e.gb0[:, r * U:(r + 1) * U, :],
                                 e.vd[bass.ds(it * (U * P), U * P), :].rearrange("(u p) n -> p u n", p=P)).then_inc(got[r], 16)

                def loads():
                    for sem, tile, src in prefetch:
                        sp.dma_start(tile, src, allow_slow_non_contiguous=True).then_inc(sem, 16)
                ring_turns(sp, turn, loads)

        @block.scalar
        def _(a):
            def turn(it):
                hold(a, (turned, it))
                a.dma_start(e.rowb[0:H, :], e.rowd2[0:H, bass.ds(it * (U * P), U * P)]).then_inc(rowin, 16)
                hold(a, (turned, it + 1))
                a.activation(e.wt[:, bass.ds(it * U, U), 0:H], e.ps[7][:, 0:U * H].rearrange("p (u h) -> p u h", u=U),
                             ACT.Copy).then_inc(wts, 1)
            turns(a, NI, turn)

        @block.vector
        def _(v):
            def turn(it, r, big):
                hold(v, (wts, it + 1), *([(got[r], big * 16 + 16)] if table is None else []))
                for u in range(U):
                    hold(v, *([got.of_tile(r * U + u, big)] if table is not None else []), (used, it * U + (u + 1 - U)))
                    v.tensor_scalar(e.oh[:, u, :], e.lane[:, :], e.dloc[:, bass.ds(it * U + u, 1)], None,
                                    ALU.is_equal).then_inc(oh, 1)
                    v.tensor_tensor(e.gb2[:, u, :].rearrange("p (h d) -> p h d", h=H),
                                    e.gb0[:, r * U + u, :].rearrange("p (h d) -> p h d", h=H),
                                    e.wt[:, bass.ds(it * U + u, 1), 0:H].rearrange("p a h -> p h a").to_broadcast([P, H, DH]),
                                    ALU.mult).then_inc(msg, 1)
            ring_turns(v, turn)

        @block.tensor
        def _(pe):
            for b in range(NB):
                pe.matmul(e.acc[:, b * D:(b + 1) * D], e.zeros[:, 0:P], e.zeros[:, :], start=True, stop=True)
            pe.matmul(e.ps[6][:, :], e.zeros[:, 0:P], e.zeros[:, :], start=True, stop=True)
            def weights(it):
                hold(pe, (rowin, it * 16 + 16), (wts, it))
                for u in range(U):
                    i = pe.transpose(e.ps[7][:, u * H:(u + 1) * H], e.rowb[0:H, u * P:(u + 1) * P], e.ident[0:H, 0:H])
                i.then_inc(turned, 1)

            def sums(it):
                for u, blk in enumerate(node_blocks(e, it * U, U)):
                    hold(pe, (oh, it * U + (u + 1)), (msg, it * U + (u + 1)))
                    pe.matmul(e.ps[6][:, bass.ds(blk * 16, H)], e.oh[:, u, :],
                              e.wt[:, bass.ds(it * U + u, 1), 0:H].rearrange("p a h -> p (a h)"), start=False, stop=True,
                              skip_group_check=True)
                    pe.matmul(e.acc[:, bass.ds(blk * D, D)], e.oh[:, u, :], e.gb2[:, u, :], start=False, stop=True,
                              skip_group_check=True).then_inc(used, 1)

            def turn(it):
                weights(it + 1)
                sums(it)
            weights(0)
            turns(pe, NI - 1, turn)
            sums(NI - 1)

def divide_sums(e, name, H, guard, bias=None):
    DH = D // H
    den = e.ps[6][:, 0:NB * 16].rearrange("p (b h) -> p b h", b=NB)[:, :, 0:H]
    with e.nc.Block() as block:
        @block.vector
        def _(v):
            st = Steps(v, e.sem(f"{name}_steps"))
            if guard == "add":
                st(v.tensor_scalar(e.rden[:, :, 0:H], den, 1e-10, None, ALU.add))
            else:
                st(v.tensor_scalar(e.rden[:, :, 0:H], den, 0.5, None, ALU.max))
            st(v.tensor_scalar(e.some[:, :], den[:, :, 0], 0.0, None, ALU.is_gt))
            st.settle()
            st(v.reciprocal(e.rden[:, :, 0:H], e.rden[:, :, 0:H]))
            st.settle()
            for b in range(NB):
                st(v.tensor_tensor(e.t0[:, b, :].rearrange("p (h d) -> p h d", h=H),
                                   e.acc[:, b * D:(b + 1) * D].rearrange("p (h d) -> p h d", h=H),
                                   e.rden[:, b, 0:H, None].to_broadcast([P, H, DH]), ALU.mult))
            st.settle()
            if bias is not None:
                for b in range(NB):
                    st(v.scalar_tensor_tensor(out=e.t0[:, b, :], in0=bias, scalar=e.some[:, b:b + 1], in1=e.t0[:, b, :],
                                              op0=ALU.mult, op1=ALU.add))
                st.settle()


def ffn(e):
    nc = e.nc
    M = 4 * D // P
    up, gel, down, got = e.sem("f_up"), e.sem("f_gelu"), e.sem("f_down"), e.sem("f_got")
    parts = ((0, 512), (512, NB * P))
    R = 3
    with nc.Block() as block:
        @block.tensor
        def _(pe):
            pe.wait_ge(e.W1_in, 16)
            pe.wait_ge(e.W2_in, 32)

            def hidden(m):
                for q, (a, b) in enumerate(parts):
                    k = 2 * m + q
                    if k >= R:
                        pe.wait_ge(gel, k - R + 1)
                    for c in range(4):
                        i = pe.matmul(e.ps[NB + k % R][:, 0:b - a], e.W1[:, c, m * P:(m + 1) * P], e.hT[:, c, a:b],
                                      start=(c == 0), stop=(c == 3))
                    i.then_inc(up, 1)

            hidden(0)
            for m in range(M):
                if m + 1 < M:
                    hidden(m + 1)
                pe.wait_ge(gel, 2 * m + 2)
                for b in range(NB):
                    i = pe.matmul(e.ps[b][:, :], e.uT[:, m % 4, b * P:(b + 1) * P], e.W2[:, m, :], start=(m == 0),
                                  stop=(m == M - 1), skip_group_check=True)
                    if m == M - 1:
                        i.then_inc(got, 1)
                if m < M - 1:
                    i.then_inc(down, 1)

        @block.scalar
        def _(a_):
            for m in range(M):
                if m >= 4:
                    a_.wait_ge(down, m - 3)
                for q, (a, b) in enumerate(parts):
                    k = 2 * m + q
                    a_.wait_ge(up, k + 1)
                    a_.activation(e.uT[:, m % 4, a:b], e.ps[NB + k % R][:, 0:b - a], ACT.Gelu,
                                  bias=e.b1c[:, m:m + 1]).then_inc(gel, 1)

        @block.vector
        def _(v):
            st = Steps(v, e.sem("f_steps"))
            for b in range(NB):
                st(v.tensor_tensor(e.x[:, b, :], e.x[:, b, :], e.h1[:, b, :], ALU.add))
            st.settle()
            v.wait_ge(e.W2_in, 32)
            for b in range(NB):
                st(v.tensor_tensor(e.x[:, b, :], e.x[:, b, :], e.b2r[:, :], ALU.add))
            st.settle()
            for b in range(NB):
                v.wait_ge(got, b + 1)
                st(v.tensor_tensor(e.x[:, b, :], e.ps[b][:, :], e.x[:, b, :], ALU.add))



def l1_table(e):
    nc = e.nc
    turned, copied, summed, taken = (e.sem(f"u_{f}") for f in ("turned", "copied", "summed", "taken"))
    scale = 1.0 / math.sqrt(P) * SILU_2MOM / math.sqrt(64.0)
    with nc.Block() as block:
        @block.tensor
        def _(pe):
            for b in range(NB):
                if b >= 2:
                    pe.wait_ge(copied, b - 1)
                for c in range(4):
                    src = e.h[:, b, 0:P] if c == 0 else e.h[:, b, P:D].rearrange("p (u m) -> p m u", m=3)[:, c - 1, :]
                    i = pe.transpose(e.ps[b % 2][:, c * P:(c + 1) * P], src, e.ident[:, :])
                i.then_inc(turned, 1)
            for b in range(NB):
                pe.wait_ge(copied, b + 1)
                if b >= 2:
                    pe.wait_ge(taken, b - 1)
                for c in range(4):
                    i = pe.matmul(e.ps[2 + b % 2][:, c * P:(c + 1) * P], e.hT[:, c, b * P:(b + 1) * P],
                                  (e.Wup0 if c == 0 else e.Wup1)[:, :], start=True, stop=True)
                i.then_inc(summed, 1)

        @block.scalar
        def _(a):
            for b in range(NB):
                a.wait_ge(turned, b + 1)
                a.activation(e.hT[:, 0:4, b * P:(b + 1) * P], e.ps[b % 2].rearrange("p (c n) -> p c n", c=4),
                             ACT.Copy).then_inc(copied, 1)

        @block.vector
        def _(v):
            for b in range(NB):
                v.wait_ge(summed, b + 1)
                v.tensor_scalar(e.t0[:, b, :], e.ps[2 + b % 2][:, :], scale, None, ALU.mult).then_inc(taken, 1)

class Pair:

    def __init__(self, e, big, k):
        big, k = big + k // PAIRS, k % PAIRS
        self.big, self.k, self.n, self.t = big, k, big * PAIRS + k, big * RING + 2 * k
        self.slots = slice(2 * k, 2 * k + 2)
        self.radial = e.ps[5 + k % PAIR_BANKS].rearrange("p (t n) -> p t n", t=2)


def pair_turns(eng, e, lead, body):
    last = NT // RING - 1

    def turn(big):
        for k in range(PAIRS):
            body(Pair(e, big, k), Pair(e, big, k + lead) if big is not last or k + lead < PAIRS else None)
    turn(0)
    with eng.Fori(1, last) as big:
        turn(big)
    turn(last)


def l1_pass(e, name, second):
    got = RingRows(e)
    w, marked, w2s0, d0, d1, d2, msg, scaled, used = (
        e.sem(f"{name}_{f}") for f in ("w", "marked", "w2s0", "dot0", "dot1", "dot2", "msg", "scaled", "used"))
    hidden = [e.sem(f"{name}_hidden{k}") for k in range(PAIRS)]
    W4 = e.Wm4[0:64, :].rearrange("p (a b n) -> p a b n", a=2, b=2)[:, :, 1 if second else 0, :]

    def y(t, m):
        return e.srt[:, bass.ds(t, 1), F_A4 + m:F_A4 + m + 1].rearrange("p a f -> p (a f)")

    with e.nc.Block() as block:
        @block.gpsimd
        def _(g):
            gather_loop(g, e, name, [(e.srcI, e.ts, e.gb0)], d2 if second else msg, [got.sems])

        @block.sync
        def _(sp):
            def load_units(p, ahead):
                hold(sp, (w, p.n + (1 - PAIRS)))
                sp.dma_start(e.h3r[0:64, p.slots, :],
                             e.h3d[:, bass.ds(p.t * P, 2 * P)].rearrange("c (t p) -> c t p", p=P)).then_inc(hidden[p.k], 16)
            pair_turns(sp, e, 0, load_units)

        if second:
            @block.scalar
            def _(a):
                def scale(p, ahead):
                    hold(a, (w2s0, p.n + 1), (used, p.t + (2 - RING)))
                    for j in range(2):
                        for m in range(3):
                            i = a.activation(e.msgs[:, 2 * p.k + j, m * P:(m + 1) * P], e.t2[:, 2 * p.k + j, :], ACT.Copy,
                                             scale=y(p.t + j, m + 1))
                    i.then_inc(scaled, 2)
                pair_turns(a, e, 0, scale)

        @block.vector
        def _(v):
            def first_messages(p, ahead):
                hold(v, (w, p.n + 1), (used, p.t + (2 - RING)), got.of_tile(2 * p.k, p.big), got.of_tile(2 * p.k + 1, p.big))
                for j in range(2):
                    u = 2 * p.k + j
                    v.tensor_scalar(e.marks[:, u, :], e.lane[:, :], e.dloc[:, bass.ds(p.t + j, 1)], y(p.t + j, 0),
                                    ALU.is_equal, ALU.mult).then_inc(marked, 1)
                v.tensor_tensor(e.msgs[:, p.slots, 0:P], e.gb0[:, p.slots, 0:P], p.radial[:, :, 0:P], ALU.mult).then_inc(w2s0, 1)
                for j in range(2):
                    u = 2 * p.k + j
                    v.tensor_tensor(e.msgs[:, u, P:D].rearrange("p (m n) -> p m n", m=3),
                                    e.gb0[:, u, P:D].rearrange("p (m n) -> p m n", m=3),
                                    p.radial[:, j:j + 1, P:2 * P].to_broadcast([P, 3, P]), ALU.mult).then_inc(msg, 1)

            def begin(p):
                hold(v, (w, p.n + 1), (used, p.t + (2 - RING)), (scaled, p.t + (2 - RING)),
                     got.of_tile(2 * p.k, p.big), got.of_tile(2 * p.k + 1, p.big))
                for j in range(2):
                    v.tensor_scalar(e.marks[:, 2 * p.k + j, :], e.lane[:, :], e.dloc[:, bass.ds(p.t + j, 1)], None,
                                    ALU.is_equal).then_inc(marked, 1)
                v.tensor_tensor(e.t2[:, p.slots, :], e.gb0[:, p.slots, 0:P], p.radial[:, :, 0:P], ALU.mult).then_inc(w2s0, 1)

            def dot(p, m, before, signal):
                hold(v, (before, p.t + 2) if m else (msg, p.t - 2))
                for j in range(2):
                    row, part = e.gb0[:, 2 * p.k + j, (m + 1) * P:(m + 2) * P], e.dot[:, 2 * (p.k % 2) + j, :, :]
                    if m == 0:
                        i = v.tensor_scalar(part[:, 0, :], row, y(p.t + j, 1), None, ALU.mult)
                    else:
                        i = v.scalar_tensor_tensor(out=part[:, m, :], in0=row, scalar=y(p.t + j, m + 1),
                                                   in1=part[:, m - 1, :], op0=ALU.mult, op1=ALU.add)
                    i.then_inc(signal, 1)

            def finish(p):
                hold(v, (d2, p.t + 2))
                v.scalar_tensor_tensor(out=e.msgs[:, p.slots, 3 * P:D], in0=e.dot[:, 2 * (p.k % 2):2 * (p.k % 2) + 2, 2, :],
                                       scalar=1.0 / math.sqrt(3.0), in1=p.radial[:, :, P:2 * P],
                                       op0=ALU.mult, op1=ALU.mult).then_inc(msg, 2)

            def second_messages(p, q):
                dot(p, 1, d0, d1)
                if q:
                    begin(q)
                dot(p, 2, d1, d2)
                if q:
                    dot(q, 0, None, d0)
                finish(p)

            if second:
                begin(Pair(e, 0, 0))
                dot(Pair(e, 0, 0), 0, None, d0)
                pair_turns(v, e, 1, second_messages)
            else:
                pair_turns(v, e, 0, first_messages)

        @block.tensor
        def _(pe):
            for b in range(NB):
                pe.matmul(e.acc[:, b * D:(b + 1) * D], e.zeros[:, 0:P], e.zeros[:, :], start=True, stop=True)

            def radial(p):
                hold(pe, (hidden[p.k], p.big * 16 + 16), (msg, p.t + (2 - 2 * PAIR_BANKS)))
                for j in range(2):
                    i = pe.matmul(p.radial[:, j, :], e.h3r[0:64, 2 * p.k + j, :], W4, start=True, stop=True)
                i.then_inc(w, 1)

            def sums(p, ahead):
                if ahead:
                    radial(ahead)
                blks = node_blocks(e, p.t, 2)
                hold(pe, (marked, p.t + 2), (msg, p.t + 2), *([(scaled, p.t + 2)] if second else [(w2s0, p.n + 1)]))
                for j, blk in enumerate(blks):
                    pe.matmul(e.acc[:, bass.ds(blk * D, D)], e.marks[:, 2 * p.k + j, :], e.msgs[:, 2 * p.k + j, :],
                              start=False, stop=True, skip_group_check=True).then_inc(used, 1)
            radial(Pair(e, 0, 0))
            radial(Pair(e, 0, 1))
            pair_turns(pe, e, 2, sums)


def take_sums(e, name, dst):
    taken = e.sem(f"{name}_taken")
    with e.nc.Block() as block:
        @block.vector
        def _(v):
            for b in range(NB):
                v.tensor_copy(dst[:, b, :], e.acc[:, b * D:(b + 1) * D]).then_inc(taken, 1)
            v.wait_ge(taken, NB)


def l1_out(e, first, second):
    nc = e.nc
    turned, copied, summed, taken = (e.sem(f"o_{f}") for f in ("turned", "copied", "summed", "taken"))
    scale = 1.0 / math.sqrt(2.0 * P) / 10.0
    with nc.Block() as block:
        @block.tensor
        def _(pe):
            for b in range(NB):
                for q, t in enumerate((first, second)):
                    k = 2 * b + q
                    if k >= 2:
                        pe.wait_ge(copied, k - 1)
                    for c in range(4):
                        i = pe.transpose(e.ps[k % 2][:, c * P:(c + 1) * P], t[:, b, c * P:(c + 1) * P], e.ident[:, :])
                    i.then_inc(turned, 1)
            for b in range(NB):
                pe.wait_ge(copied, 2 * b + 2)
                if b >= 2:
                    pe.wait_ge(taken, 2 * b - 2)
                ps = e.ps[2 + b % 2]
                for c, (k0, k1, W) in enumerate(((0, 7, e.Wo0), (4, 1, e.Wo1), (5, 2, e.Wo1), (6, 3, e.Wo1))):
                    pe.matmul(ps[:, c * P:(c + 1) * P], e.dT[:, k0, b * P:(b + 1) * P], W[:, 0, :], start=True, stop=False)
                    i = pe.matmul(ps[:, c * P:(c + 1) * P], e.dT[:, k1, b * P:(b + 1) * P], W[:, 1, :], start=False, stop=True)
                i.then_inc(summed, 1)

        @block.scalar
        def _(a):
            for b in range(NB):
                for q in range(2):
                    k = 2 * b + q
                    a.wait_ge(turned, k + 1)
                    a.activation(e.dT[:, 4 * q:4 * q + 4, b * P:(b + 1) * P], e.ps[k % 2].rearrange("p (c n) -> p c n", c=4),
                                 ACT.Copy).then_inc(copied, 1)

        @block.vector
        def _(v):
            for b in range(NB):
                v.wait_ge(summed, b + 1)
                ps = e.ps[2 + b % 2]
                v.scalar_tensor_tensor(out=e.x[:, b, 0:P], in0=ps[:, 0:P], scalar=scale, in1=e.x[:, b, 0:P],
                                       op0=ALU.mult, op1=ALU.add).then_inc(taken, 1)
                xv = e.x[:, b, P:D].rearrange("p (n m) -> p m n", m=3)
                v.scalar_tensor_tensor(out=xv, in0=ps[:, P:D].rearrange("p (m n) -> p m n", m=3), scalar=scale, in1=xv,
                                       op0=ALU.mult, op1=ALU.add).then_inc(taken, 1)



def split_weights(e, name, pairs, needs):
    high, low = e.sem(f"{name}_high"), e.sem(f"{name}_low")
    with e.nc.Block() as block:
        @block.scalar
        def _(a):
            hold(a, *needs)
            for w, h, l in pairs:
                a.activation(h, w, ACT.Copy).then_inc(high, 1)

        @block.vector
        def _(v):
            hold(v, *needs)
            for k, (w, h, l) in enumerate(pairs):
                v.wait_ge(high, k + 1)
                v.tensor_tensor(l, w, h, ALU.subtract).then_inc(low, 1)


def l2_edges(e):
    H = 16
    nc = e.nc
    name = "e2"
    got = [e.landed() for k in range(2)]
    egot = e.landed()
    vst = [e.sem(f"{name}_vst{r}") for r in range(2)]
    rst = [e.sem(f"{name}_rst{u}") for u in range(U)]
    (ta, eac, eal, m1, added, st, vare, sdr, norm, xnr, tx, rl, high, low, m2k, m2v, vo, lgr, rt, rc, cols) = (
        e.sem(f"{name}_{f}") for f in ("ta", "eac", "eal", "m1", "added", "steps", "vare", "sd", "norm", "xn", "tx",
                                       "relu", "high", "low", "m2k", "m2v", "vout", "logits", "rowt", "rowc", "cols"))
    M1 = e.psum[:, 512:1536]
    LN = 5
    PR = 3
    LAG = 2

    class T:

        def __init__(self, it, off):
            self.n, self.u, self.turn = it * U + off, off % U, it + off // U
            self.r = off % 2

    def steps(eng, stages):
        def ends(first, last):
            for s in range(first, last):
                for lead, stage in stages:
                    if 0 <= s + lead < NT:
                        stage(T(0, s + lead))
        ends(-max(lead for lead, stage in stages), U)
        with eng.Fori(1, NT // U - 1) as it:
            for u in range(U):
                for lead, stage in stages:
                    stage(T(it, u + lead))
        ends(NT - U, NT + 1)

    with nc.Block() as block:
        @block.gpsimd
        def _(g):
            def queries(half, j, n):
                hold(g, (lgr, n * PR + (1 - U) * PR))
                g.indirect_dma_start(e.qg[:, (half * IS + j - LAG) % U, :], None, e.tq2[:, :],
                                     bass.IndirectOffsetOnAxis(ap=e.idx[:, 1, half, j:j + 1], axis=0)
                                     ).then_inc(got[1][(half * IS + j - LAG) % U], 16)

            def turn(it):
                for half in range(2):
                    first = it * (2 * IS) + half * IS
                    at_start = isinstance(it, int) and half == 0
                    skip = LAG if at_start else 0
                    hold(g, (added, first - IS), (lgr, (first - IS - LAG) * PR))
                    g.tensor_copy(e.idx[:, 0, half, :], e.srcI[:, bass.ds(first, IS)]).then_inc(cols, 1)
                    g.tensor_copy(e.idx[:, 1, half, skip:IS], e.dstI[:, bass.ds(first + (skip - LAG), IS - skip)]).then_inc(cols, 1)
                    g.tensor_copy(e.idx[:, 2, half, :], e.idI[:, bass.ds(first, IS)]).then_inc(cols, 1)
                    hold(g, (cols, it * 6 + (half + 1) * 3))
                    for j in range(IS):
                        u = (half * IS + j) % U
                        hold(g, (added, first + (j + 1 - U)))
                        g.indirect_dma_start(e.ea[:, u, :], None, e.attributes,
                                             bass.IndirectOffsetOnAxis(ap=e.idx[:, 2, half, j:j + 1], axis=0)).then_inc(egot[u], 16)
                        g.indirect_dma_start(e.gkv[:, u, :], None, e.tkv[:, :],
                                             bass.IndirectOffsetOnAxis(ap=e.idx[:, 0, half, j:j + 1], axis=0)).then_inc(got[0][u], 16)
                        if j >= skip:
                            queries(half, j, first + (j - LAG))
            turns(g, NT // (2 * IS), turn)
            hold(g, (lgr, (NT - IS - LAG) * PR))
            g.tensor_copy(e.idx[:, 1, 0, 0:LAG], e.dstI[:, NT - LAG:NT]).then_inc(cols, 1)
            hold(g, (cols, NT // IS * 3 + 1))
            for j in range(LAG):
                queries(0, j, NT - LAG + j)

        @block.sync
        def _(sp):
            def turn(it):
                for u in range(U):
                    hold(sp, (vo, it * U + (u + 1)))
                    sp.dma_start(e.vd[bass.ds((it * U + u) * P, P), :], e.vout[:, u % 2, :]).then_inc(vst[u % 2], 16)
                    hold(sp, (rc, it * U + (u + 1)))
                    sp.dma_start(e.rowd[0:H, bass.ds((it * U + u) * P, P)], e.rowb[0:H, u * P:(u + 1) * P]).then_inc(rst[u], 16)
            turns(sp, NI, turn)
            for r in range(2):
                sp.wait_ge(vst[r], 16 * (NT // 2))
            for u in range(U):
                sp.wait_ge(rst[u], 16 * NI)

        @block.tensor
        def _(pe):
            def attributes(t):
                hold(pe, (egot[t.u], t.turn * 16 + 16), (eal, t.n))
                pe.transpose(e.ps[0][:, t.u * P:(t.u + 1) * P], e.ea[:, t.u, :], e.ident[:, :]).then_inc(ta, 1)

            def first(t):
                hold(pe, (eal, t.n + 1), (added, t.n))
                for ps, wh, wl in ((e.ps[1], e.kW1h, e.kW1l), (e.ps[2], e.vW1h, e.vW1l)):
                    pe.matmul(ps[:, :], e.eaTh[:, t.u, :], wh[:, :], start=True, stop=False)
                    pe.matmul(ps[:, :], e.eaTh[:, t.u, :], wl[:, :], start=False, stop=False)
                    i = pe.matmul(ps[:, :], e.eaTl[:, t.u, :], wh[:, :], start=False, stop=True)
                i.then_inc(m1, 1)

            def hidden(t):
                for k in range(2):
                    hold(pe, (xnr, 2 * t.n + k + 1), (rl, 2 * t.n))
                    for c in range(4 * k, 4 * k + 4):
                        i = pe.transpose(e.ps[3 + k][:, c % 4 * P:(c % 4 + 1) * P], e.hid[:, t.r, c * P:(c + 1) * P], e.ident[:, :])
                    i.then_inc(tx, 1)

            def second(t, k, ps, wh, wl, last_use, signal):
                hold(pe, (low, 2 * t.n + k + 1), last_use)
                for c in range(4):
                    chunk = slice((4 * k + c) * P, (4 * k + c + 1) * P)
                    pe.matmul(ps[:, :], e.hTh[:, t.r, chunk], wh[:, c, :], start=(c == 0), stop=False)
                    pe.matmul(ps[:, :], e.hTh[:, t.r, chunk], wl[:, c, :], start=False, stop=False)
                    i = pe.matmul(ps[:, :], e.hTl[:, t.r, chunk], wh[:, c, :], start=False, stop=(c == 3))
                i.then_inc(signal, 1)

            def keys(t):
                second(t, 0, e.ps[5], e.kW2h, e.kW2l, (lgr, t.n * PR), m2k)

            def values(t):
                second(t, 1, e.ps[6], e.vW2h, e.vW2l, (vo, t.n), m2v)

            def row(t):
                hold(pe, (lgr, t.n * PR + PR), (rc, t.n))
                pe.transpose(e.ps[7][0:H, t.u * P:(t.u + 1) * P], e.lg[:, t.u, 0:H], e.ident[:, :]).then_inc(rt, 1)

            steps(pe, [(1, hidden), (4, attributes), (0, keys), (3, first), (0, values), (-1, row)])

        @block.scalar
        def _(a):
            def turned_in(t):
                hold(a, (ta, t.n + 1))
                a.activation(e.eaTh[:, t.u, :], e.ps[0][:, t.u * P:(t.u + 1) * P], ACT.Copy).then_inc(eac, 1)

            def root(t):
                hold(a, (vare, t.n + 1))
                a.activation(e.sd2[:, t.r, :], e.va2[:, t.r, :], ACT.Sqrt).then_inc(sdr, 1)

            def normalize(t):
                hold(a, (norm, t.n + 1))
                for k in range(2):
                    hid = e.hid[:, t.r, k * D:(k + 1) * D]
                    a.activation(hid, hid, ACT.Identity, bias=e.nb2[:, t.r, k:k + 1],
                                 scale=e.rs2[:, t.r, k:k + 1]).then_inc(xnr, 1)

            def units(t):
                for k in range(2):
                    hold(a, (tx, 2 * t.n + 1 + k), (low, 2 * t.n - 1 + k))
                    for c in range(4):
                        i = a.activation(e.units[:, (4 * k + c) * P:(4 * k + c + 1) * P], e.ps[3 + k][:, c * P:(c + 1) * P],
                                         ACT.Relu, scale=e.gkvc[:, 4 * k + c:4 * k + c + 1],
                                         bias=e.bkvc[:, 4 * k + c:4 * k + c + 1])
                    i.then_inc(rl, 1)
                for k in range(2):
                    hold(a, (rl, 2 * t.n + 1 + k))
                    a.activation(e.hTh[:, t.r, k * D:(k + 1) * D], e.units[:, k * D:(k + 1) * D], ACT.Copy).then_inc(high, 1)

            def value_out(t):
                hold(a, (m2v, t.n + 1), (vst[t.r], t.turn * (8 * U) + t.u // 2 * 16))
                a.activation(e.vout[:, t.r, :], e.ps[6][:, :], ACT.Copy).then_inc(vo, 1)

            def row_out(t):
                hold(a, (rt, t.n + 1), (rst[t.u], t.turn * 16))
                a.activation(e.rowb[0:H, t.u * P:(t.u + 1) * P], e.ps[7][0:H, t.u * P:(t.u + 1) * P], ACT.Copy).then_inc(rc, 1)

            steps(a, [(1, units), (4, turned_in), (2, root), (2, normalize), (0, value_out), (-1, row_out)])

        @block.vector
        def _(v):
            def statistics(t):
                at = t.n * LN
                hold(v, (m1, t.n + 1), (got[0][t.u], t.turn * 16 + 16), (tx, 2 * t.n - 2))
                hid = e.hid[:, t.r, :]
                v.tensor_tensor(hid, M1, e.gkv[:, t.u, :], ALU.add).then_inc(added, 1)
                hold(v, (added, t.n + 1))
                for k in range(2):
                    v.bn_stats(e.st2[:, t.r, k, :], hid[:, k * D:(k + 1) * D]).then_inc(st, 1)
                hold(v, (st, at + 2))
                for k in range(2):
                    v.bn_aggr(e.mv2[:, t.r, k, :], e.st2[:, t.r, k, :]).then_inc(st, 1)
                hold(v, (st, at + 4))
                v.tensor_scalar(e.va2[:, t.r, :], e.mv2[:, t.r, :, 1], EPS, None, ALU.add).then_inc(vare, 1)

            def scales(t):
                hold(v, (sdr, t.n + 1))
                v.reciprocal(e.rs2[:, t.r, :], e.sd2[:, t.r, :]).then_inc(st, 1)
                hold(v, (st, t.n * LN + 5))
                v.scalar_tensor_tensor(out=e.nb2[:, t.r, :], in0=e.mv2[:, t.r, :, 0], scalar=-1.0, in1=e.rs2[:, t.r, :],
                                       op0=ALU.mult, op1=ALU.mult).then_inc(norm, 1)

            def lower(t):
                for k in range(2):
                    hold(v, (high, 2 * t.n + 1 + k))
                    v.tensor_tensor(e.hTl[:, t.r, k * D:(k + 1) * D], e.units[:, k * D:(k + 1) * D],
                                    e.hTh[:, t.r, k * D:(k + 1) * D], ALU.subtract).then_inc(low, 1)

            def attributes_lower(t):
                hold(v, (eac, t.n + 1))
                v.tensor_tensor(e.eaTl[:, t.u, :], e.ps[0][:, t.u * P:(t.u + 1) * P], e.eaTh[:, t.u, :],
                                ALU.subtract).then_inc(eal, 1)

            def product(t):
                hold(v, (m2k, t.n + 1), (got[1][t.u], t.turn * 16 + 16), (rt, t.n + (1 - U)))
                v.tensor_tensor(e.prod[:, :], e.ps[5][:, :], e.qg[:, t.u, 0:D], ALU.mult).then_inc(lgr, 1)
                hold(v, (lgr, t.n * PR + 1))
                v.tensor_reduce(e.lg[:, t.u, 0:H], e.prod.rearrange("p (h d) -> p h d", h=H), AX.X, ALU.add).then_inc(lgr, 1)
                hold(v, (lgr, t.n * PR + 2))
                v.tensor_tensor(e.lg[:, t.u, 0:H], e.lg[:, t.u, 0:H], e.qg[:, t.u, D:D + H], ALU.add).then_inc(lgr, 1)

            steps(v, [(2, statistics), (2, scales), (1, lower), (4, attributes_lower), (0, product)])


def logits_l3(e):
    H = 8
    nc = e.nc
    got = RingRows(e)
    stored = e.sem("a3_stored")
    turned, rows, ready, added, leaked, dests = (
        e.sem(f"a3_{f}") for f in ("turned", "rows", "ready", "added", "leaked", "dests"))
    with nc.Block() as block:
        @block.gpsimd
        def _(g):
            gather_loop(g, e, "a3", [(e.srcI, e.tes, e.sg)], added, [got.sems])

        @block.vector
        def _(v):
            def turn(it, r, big):
                hold(v, *got.of_turn(r, big), (dests, it + 1))
                v.tensor_tensor(e.lg2[:, :, :], e.sg[:, r * U:(r + 1) * U, :],
                                e.ps[1][:, 0:U * H].rearrange("p (u h) -> p u h", u=U),
                                ALU.add).then_inc(added, U)
                hold(v, (added, it * U + U))
                v.scalar_tensor_tensor(out=e.lg3[:, :, :], in0=e.lg2[:, :, :], scalar=0.2, in1=e.lg2[:, :, :],
                                       op0=ALU.mult, op1=ALU.max).then_inc(leaked, 1)
                hold(v, (leaked, it + 1), (turned, it))
                v.tensor_tensor(e.lg[:, :, 0:H], e.lg3[:, :, :], e.fac[:, bass.ds(it * U, U), :], ALU.mult).then_inc(ready, 1)
            ring_turns(v, turn)

        @block.tensor
        def _(pe):
            def destinations(it):
                hold(pe, (added, it * U))
                for u, blk in enumerate(node_blocks(e, it * U, U)):
                    i = at_destination(pe, e, e.ps[1][:, u * H:(u + 1) * H], it * U + u, blk, e.ted3, 0, H)
                i.then_inc(dests, 1)

            def turn(it):
                destinations(it + 1)
                row_transposes(pe, e, it, e.lg, H, ready, e.ps[0], rows, turned)
            destinations(0)
            turns(pe, NI - 1, turn)
            row_transposes(pe, e, NI - 1, e.lg, H, ready, e.ps[0], rows, turned)

        @block.scalar
        def _(a):
            def turn(it):
                hold(a, (turned, it + 1), (stored, it * 16))
                a.activation(e.rowb[0:H, :], e.ps[0][0:H, :], ACT.Copy).then_inc(rows, 1)
            turns(a, NI, turn)

        @block.sync
        def _(sp):
            def turn(it):
                hold(sp, (rows, it + 1))
                sp.dma_start(e.rowd[0:H, bass.ds(it * (U * P), U * P)], e.rowb[0:H, :]).then_inc(stored, 16)
            turns(sp, NI, turn)
            sp.wait_ge(stored, 16 * NI)


def load(e, name, pairs, later=()):
    done = e.sem(f"{name}_loaded")
    with e.nc.Block() as block:
        @block.sync
        def _(sp):
            for tile, src in pairs:
                sp.dma_start(tile, src, allow_slow_non_contiguous=True).then_inc(done, 16)
            for sem, tile, src in later:
                sp.dma_start(tile, src).then_inc(sem, 16)
            if pairs:
                sp.wait_ge(done, 16 * len(pairs))


def rows(w):
    return w.rearrange("(c p) n -> p c n", p=P)


def column(b):
    return b.rearrange("(c p) -> p c", p=P)


def line(b):
    return b.rearrange("(a n) -> a n", a=1)


def spread(b):
    return line(b).to_broadcast([P, b.shape[0]])


def program(nc, i, out):
    ctx = ExitStack()
    e = Env()
    e.nc = nc
    with ctx:
        uses = {}

        def sb(name, shape, dt=F32, scope=ctx):
            uses[name] = uses.get(name, 0) + 1
            t = scope.enter_context(nc.sbuf_tensor(f"{name}_{uses[name]}", shape, dt))
            return t

        sems = Env()
        sems.scope, sems.held = ctx.enter_context(ExitStack()), []

        def sem(name):
            handle = sems.scope.enter_context(nc.semaphore(name))
            sems.held.append(handle)
            return handle
        e.sem = sem
        sems.landed = [ctx.enter_context(nc.semaphore(f"landed{k}")) for k in range(7 * U)]
        sems.lent = 0
        e.ring_landed = [ctx.enter_context(nc.semaphore(f"ring_landed{u}")) for u in range(RING)]
        e.ring_base = Env()
        e.ring_base.count = 0

        def landed():
            sems.lent += U
            return sems.landed[sems.lent - U:sems.lent]
        e.landed = landed

        def renew():
            with nc.Block() as block:
                @block.gpsimd
                def _(g):
                    for handle in sems.held:
                        g.sem_clear(handle)
            sems.scope.close()
            sems.held.clear()

        def table(name, n, w):
            return nc.dram_tensor(f"d_{name}", [n, w], F32).ap()

        NN = NB * P
        e.rec = table("rec", SLOTS, RS)
        e.h3d = table("h3d", 64, SLOTS)
        e.dstd = table("dstd", SLOTS + 2, 1)
        e.rowd = table("rowd", 16, SLOTS)
        e.rowd2 = table("rowd2", 16, SLOTS)
        e.vd = table("vd", SLOTS, D)
        e.tq = table("tq", NN, D)
        e.tv = table("tv", NN, D)
        e.ts = table("ts", NN, D)
        e.th = table("th", NN, D)
        e.tkv = table("tkv", NN, 2 * D)
        e.tq2 = table("tq2", NN, D + 16)
        e.tes = table("tes", NN, 8)
        e.dlocd = table("dlocd", NT, P)

        e.psum = ctx.enter_context(nc.psum_tensor("psum", [P, 8 * 512], F32))
        e.ps = [e.psum[:, k * 512:(k + 1) * 512] for k in range(8)]
        e.acc = e.psum[:, 0:ACC]

        e.x = sb("x", [P, NB, D])
        e.h = sb("h", [P, NB, D])
        e.t0 = sb("t0", [P, NB, D])
        e.hT = sb("hT", [P, 4, NB * P])
        e.ident = sb("ident", [P, P])
        e.ones = sb("ones", [P, P])
        e.zeros = sb("zeros", [P, 512])
        e.lane = sb("lane", [P, P])
        e.srcI = sb("srcI", [P, NT], I32)
        e.dstI = sb("dstI", [P, NT], I32)
        e.idI = sb("idI", [P, NT], I32)
        e.blki = sb("blki", [P, NT], I32)
        e.dloc = sb("dloc", [P, NT])
        e.ohT = sb("ohT", [P, SLOTS], BF16)
        e.laneP = sb("laneP", [P, 1])
        e.asum = sb("asum", [P, NT, 8])
        e.fac = sb("fac", [P, NT, 8])
        e.srt = sb("srt", [P, NT, RS])
        e.pen = sb("pen", [P, 2, SEG])
        e.penF = sb("penF", [P, 16, SEG])
        e.penB = sb("penB", [P, 16, SEG])
        e.wrow = sb("wrow", [16, 2 * P])
        e.stats = sb("stats", [P, NB, 6])
        e.mv = sb("mv", [P, NB, 2])
        e.vare = sb("vare", [P, NB])
        e.sd = sb("sd", [P, NB])
        e.rstd = sb("rstd", [P, NB])
        e.nbias = sb("nbias", [P, NB])
        e.rden = sb("rden", [P, NB, 16])
        e.some = sb("some", [P, NB])
        e.idx = sb("idx", [P, 3, 2, IS], I32)
        e.lg = sb("lg", [P, U, 16])
        e.oh = sb("oh", [P, U, P])
        e.rowb = sb("rowb", [16, U * P])
        e.edge0 = sb("edge0", [P, 16])
        e.ends = sb("ends", [P, 16])
        e.carry = sb("carry", [16, P + 1])

        layer0 = ExitStack()
        e.g1c, e.b1lc, e.g2c, e.b2lc = (sb(name, [P, 4], F32, layer0) for name in ("g1c", "b1lc", "g2c", "b2lc"))
        s1 = ExitStack()
        e.tk3 = sb("tk3", [P, NB, 3, D], BF16, s1)
        with ExitStack() as sc:
            e.phantom = e.srt
            e.nodeno = sb("nodeno", [P, NB * P], F32, sc)
            e.window = sb("window", [P, 2 * EC], F32, sc)
            e.small = sb("small", [EP, EC, RS], F32, sc)
            e.dstf = sb("dstf", [EP, EC], F32, sc)
            e.base = sb("base", [P, NB * P], F32, sc)
            e.bsum = sb("bsum", [P, NB], F32, sc)
            e.bsumi = sb("bsumi", [P, NB], I32, sc)
            e.btile = sb("btile", [P, NB], I32, sc)
            e.bsize = sb("bsize", [P, NB], F32, sc)
            e.bend = sb("bend", [P, NB], F32, sc)
            e.bstart = sb("bstart", [P, NB], F32, sc)
            e.blk = sb("blk", [P, NT], F32, sc)
            e.junk = sb("junk", [EP, SC // 2, NB * P], F32, sc)
            e.junkw = sb("junkw", [EP, SC // 2, EC], F32, sc)
            e.slota = sb("slota", [EP, SC], F32, sc)
            e.slotb = sb("slotb", [EP, SC], F32, sc)
            e.recbuf = sb("recbuf", [EP, 2, SC, RS], F32, sc)
            e.slotbuf = sb("slotbuf", [EP, 2, SC], I32, sc)
            e.dstT = sb("dstT", [P, P], F32, sc)
            e.guard = sb("guard", [1, 2], F32, sc)
            e.seg3 = sb("seg3", [P, 3, SEG], F32, sc)
            e.whole = sb("whole", [P, 2], F32, sc)
            e.fack = sb("fack", [P, NT, 8], F32, sc)
            e.emb = sb("emb", [P, 8, 8], F32, sc)
            e.loads0 = [(e.emb.rearrange("p k h -> p (k h)"),
                         i["L3_gnn_et_emb"].rearrange("k (h a) -> a (k h)", a=1).to_broadcast([P, 64]))]
            e.ROWS_AT = 43
            e.Wqkv_in = e.sem("Wqkv_in")
            with ExitStack() as s2:
                e.lower = sb("lower", [P, P], F32, s2)
                e.lowerb = sb("lowerb", [P, P], BF16, s2)
                e.tile_at = sb("tile_at", [P, NT], F32, s2)
                e.onesb = sb("onesb", [P, P], BF16, s2)
                e.zerosb = sb("zerosb", [P, 512], BF16, s2)
                e.srcs = sb("srcs", [EP, EC], I32, s2)
                e.dsts = sb("dsts", [EP, EC], I32, s2)
                e.kinds = sb("kinds", [EP, EC], I32, s2)
                e.weights = sb("weights", [EP, EC], F32, s2)
                e.a4 = sb("a4", [EP, EC, 4], F32, s2)
                e.a8 = sb("a8", [EP, EC, 8], F32, s2)
                e.a8n = sb("a8n", [EP, EC, 8], F32, s2)
                e.mark = sb("mark", [EP, U, NB * P], BF16, s2)
                e.cnt = sb("cnt", [P, NB * P], F32, s2)
                prepare(e, i)
                lowb = e.sem("lowb")
                with nc.Block() as block:
                    @block.vector
                    def _(v):
                        v.tensor_copy(e.lowerb[:, :], e.lower[:, :]).then_inc(lowb, 1)
                        v.wait_ge(lowb, 1)
                count_edges(e)
                place_edges(e)
            with ExitStack() as s2:
                e.Wqkv = sb("Wqkv", [P, 4, 3 * D], F32, s2)
                e.bqkv = sb("bqkv", [1, 3 * D], F32, s2)
                e.tk_ = sb("tk_", [P, NB, D], F32, s2)
                e.tout = sb("tout", [P, QueriesKeysValues.SLOTS, D], F32, s2)
                e.rest = sb("rest", [P, NB, D], F32, s2)
                load(e, "w0a", [(e.g1c[:, :], column(i["L0_gnn_ln1_g"])), (e.b1lc[:, :], column(i["L0_gnn_ln1_b"])),
                                (e.g2c[:, :], column(i["L0_gnn_ln2_g"])), (e.b2lc[:, :], column(i["L0_gnn_ln2_b"]))],
                     [(e.Wqkv_in, e.Wqkv[:, :, :], rows(i["L0_gnn_Wqkv"])), (e.Wqkv_in, e.bqkv[:, :], line(i["L0_gnn_bqkv"]))])
                node_ln(e, "n0", e.x, e.h, ACT.Relu)
                scatter_records(e, QueriesKeysValues(e))
            with ExitStack() as s2:
                e.spread = sb("spread", [P, 2, SLOTS // 6], F32, s2)
                e.dlocT = sb("dlocT", [P, P], F32, s2)
                load_sorted(e)

        renew()
        with layer0 as sc:
            with ExitStack() as s2:
                e.Wm1 = sb("Wm1", [8, 64], F32, s2)
                e.Wm2 = sb("Wm2", [64, 64], F32, s2)
                e.Wm3 = sb("Wm3", [64, 64], F32, s2)
                e.fin = sb("fin", [P, U, 8], F32, s2)
                e.fT = sb("fT", [8, U * P], F32, s2)
                e.hh1 = sb("hh1", [64, U * P], F32, s2)
                e.hh2 = sb("hh2", [64, U * P], F32, s2)
                e.h3 = sb("h3", [64, U * P], F32, s2)
                load(e, "wm", [(e.Wm1[:, :], i["L1_gnn_W_mlp1"]), (e.Wm2[:, :], i["L1_gnn_W_mlp2"]),
                               (e.Wm3[:, :], i["L1_gnn_W_mlp3"])])
                edge_buffers(e, sb, s2)
                logits_l0(e, RadialLayers(e))
                segment_softmax(e, "s0", 8, False)
                weighted_sums(e, "b0", 8, e.tv)
                divide_sums(e, "d0", 8, "max")
            s1.close()
            with ExitStack() as s2:
                e.h1 = sb("h1", [P, NB, D], F32, s2)
                e.Wo = sb("Wo", [P, 4, D], F32, s2)
                e.bor = sb("bor", [P, D], F32, s2)
                e.W1 = sb("W1", [P, 4, 4 * D], F32, s2)
                e.b1c = sb("b1c", [P, 16], F32, s2)
                e.W2 = sb("W2", [P, 16, D], F32, s2)
                e.b2r = sb("b2r", [P, D], F32, s2)
                e.uT = sb("uT", [P, 4, NB * P], F32, s2)
                e.W1_in, e.W2_in = e.sem("W1_in"), e.sem("W2_in")
                load(e, "w0b", [(e.Wo[:, :, :], rows(i["L0_gnn_Wo"])), (e.bor[:, :], spread(i["L0_gnn_bo"])),
                                (e.b1c[:, :], column(i["L0_gnn_b1"]))],
                     [(e.W1_in, e.W1[:, :, :], rows(i["L0_gnn_W1"])), (e.W2_in, e.W2[:, :, :], rows(i["L0_gnn_W2"])),
                      (e.W2_in, e.b2r[:, :], spread(i["L0_gnn_b2"]))])

                def h_and_bias(v, steps):
                    for b in range(NB):
                        steps(v.tensor_tensor(e.h[:, b, :], e.h[:, b, :], e.bor[:, :], ALU.add))
                node_linear(e, "wo", [e.t0], e.hT, None, ACT.Copy, [(e.Wo[:, :, :], None)],
                            lambda v, b, n, ps: v.tensor_tensor(e.h1[:, b, :], ps[:, :], e.h[:, b, :], ALU.add),
                            before=h_and_bias)
                node_linear(e, "ln2", [e.t0], e.hT, (e.g2c, e.b2lc), ACT.Identity, [], None, ln=(e.h1, e.t0))
                ffn(e)

        renew()
        with ExitStack() as sc:
            e.gb0 = sb("gb0", [P, RING, D], F32, sc)
            e.Wup0 = sb("Wup0", [P, P], F32, sc)
            e.Wup1 = sb("Wup1", [P, P], F32, sc)
            e.Wm4 = sb("Wm4", [64, 512], F32, sc)
            e.Wo0 = sb("Wo0", [P, 2, P], F32, sc)
            e.Wo1 = sb("Wo1", [P, 2, P], F32, sc)
            e.h3r = sb("h3r", [64, RING, P], F32, sc)
            e.t2 = sb("t2", [P, RING, P], F32, sc)
            e.msgs = sb("msgs", [P, RING, D], F32, sc)
            e.marks = sb("marks", [P, RING, P], F32, sc)
            e.dot = sb("dot", [P, U, 3, P], F32, sc)
            e.dT = sb("dT", [P, 8, NB * P], F32, sc)
            load(e, "w1", [(e.Wup0[:, :], i["L1_gnn_W_up0"]), (e.Wup1[:, :], i["L1_gnn_W_up1"]), (e.Wm4[:, :], i["L1_gnn_W_mlp4"]),
                           (e.Wo0[:, :, :], rows(i["L1_gnn_W_out0"])), (e.Wo1[:, :, :], rows(i["L1_gnn_W_out1"]))])
            node_ln(e, "n1", e.x, e.h, ACT.Relu)
            l1_table(e)
            store_table(e, "t1", [(e.ts, e.t0[:, :, :])])
            l1_pass(e, "p1", False)
            take_sums(e, "p1", e.h)
            l1_pass(e, "p2", True)
            take_sums(e, "p2", e.t0)
            l1_out(e, e.h, e.t0)

        renew()
        with ExitStack() as sc:
            e.hvb2 = sb("hvb2", [P, D], F32, sc)
            with ExitStack() as s2:
                e.prod, e.hvW1e = sb("prod", [P, D], F32, s2), sb("hvW1e", [P, D], F32, s2)
                e.hkW1e = e.prod
                e.gkv = sb("gkv", [P, U, 2 * D], F32, s2)
                e.hkW2, e.hvW2 = (e.gkv[:, 2 * k:2 * k + 2, :].rearrange("p u (c n) -> p (u c) n", c=2) for k in range(2))
                e.gnc = sb("gnc", [P, 4], F32, s2)
                e.bnc = sb("bnc", [P, 4], F32, s2)
                e.gkvc = sb("gkvc", [P, 8], F32, s2)
                e.bkvc = sb("bkvc", [P, 8], F32, s2)
                with ExitStack() as s3:
                    e.hkW1 = sb("hkW1", [P, 4, D], F32, s3)
                    e.hvW1 = sb("hvW1", [P, 4, D], F32, s3)
                    e.hqW1 = sb("hqW1", [P, 4, D], F32, s3)
                    e.hqW2 = sb("hqW2", [P, 4, D], F32, s3)
                    e.hkb1 = sb("hkb1", [P, D], F32, s3)
                    e.hvb1 = sb("hvb1", [P, D], F32, s3)
                    e.hqb1 = sb("hqb1", [P, D], F32, s3)
                    e.hqb2 = sb("hqb2", [P, D], F32, s3)
                    e.gqc = sb("gqc", [P, 4], F32, s3)
                    e.bqc = sb("bqc", [P, 4], F32, s3)
                    e.hkb2 = sb("hkb2", [P, D], F32, s3)
                    e.tkv_ = sb("tkv_", [P, NB, 2 * D], F32, s3)
                    e.tq2_ = sb("tq2_", [P, NB, D + 16], F32, s3)
                    first, second, edges = e.sem("w2_first"), e.sem("w2_second"), e.sem("w2_edges")
                    loads = [(first, e.hkW1[:, :, :], rows(i["L2_gnn_hk_W1"][0:D, :])),
                             (first, e.hvW1[:, :, :], rows(i["L2_gnn_hv_W1"][0:D, :])),
                             (first, e.hqW1[:, :, :], rows(i["L2_gnn_hq_W1"])),
                             (first, e.hkb1[:, :], spread(i["L2_gnn_hk_b1"])), (first, e.hvb1[:, :], spread(i["L2_gnn_hv_b1"])),
                             (first, e.hqb1[:, :], spread(i["L2_gnn_hq_b1"])),
                             (second, e.hqW2[:, :, :], rows(i["L2_gnn_hq_W2"])), (second, e.hqb2[:, :], spread(i["L2_gnn_hq_b2"])),
                             (second, e.hkb2[:, :], spread(i["L2_gnn_hk_b2"])), (second, e.hvb2[:, :], spread(i["L2_gnn_hv_b2"])),
                             (edges, e.hkW2[:, :, :], rows(i["L2_gnn_hk_W2"])), (edges, e.hvW2[:, :, :], rows(i["L2_gnn_hv_W2"])),
                             (edges, e.hkW1e[:, :], i["L2_gnn_hk_W1"][D:D + P, :]),
                             (edges, e.hvW1e[:, :], i["L2_gnn_hv_W1"][D:D + P, :])]
                    load(e, "w2a", [(e.gnc[:, :], column(i["L2_gnn_no_g"])), (e.bnc[:, :], column(i["L2_gnn_no_be"])),
                                    (e.gqc[:, :], column(i["L2_gnn_hq_g"])), (e.bqc[:, :], column(i["L2_gnn_hq_be"])),
                                    (e.gkvc[:, 0:4], column(i["L2_gnn_hk_g"])), (e.gkvc[:, 4:8], column(i["L2_gnn_hv_g"])),
                                    (e.bkvc[:, 0:4], column(i["L2_gnn_hk_be"])), (e.bkvc[:, 4:8], column(i["L2_gnn_hv_be"]))],
                         loads)
                    node_ln(e, "n2", e.x, e.h, ACT.Relu)

                    def evac2(v, b, n, ps):
                        out = e.tkv_[:, b, n * D:(n + 1) * D] if n < 2 else e.t0[:, b, :]
                        return v.tensor_tensor(out, ps[:, :], (e.hkb1, e.hvb1, e.hqb1)[n][:, :], ALU.add)
                    node_linear(e, "kv1", [e.h], e.hT, None, ACT.Copy,
                                [(e.hkW1[:, :, :], None), (e.hvW1[:, :, :], None),
                                 (e.hqW1[:, :, :], None)], evac2, needs=[(first, 16 * 6)])
                    scale = 1.0 / math.sqrt(32.0)
                    node_linear(e, "q2", [e.t0], e.hT, (e.gqc, e.bqc), ACT.Relu, [(e.hqW2[:, :, :], None)],
                                lambda v, b, n, ps: v.scalar_tensor_tensor(
                                    out=e.tq2_[:, b, 0:D], in0=ps[:, :], scalar=scale, in1=e.hqb2[:, :],
                                    op0=ALU.mult, op1=ALU.add),
                                ln=(e.t0, e.t0), needs=[(second, 16 * 4)],
                                before=lambda v, steps: steps(v.tensor_scalar(e.hqb2[:, :], e.hqb2[:, :], scale, None, ALU.mult)))
                    dots = e.sem("qb2")
                    with nc.Block() as block:
                        @block.vector
                        def _(v):
                            hold(v, (second, 16 * 4))
                            for b in range(NB):
                                v.tensor_tensor(e.t0[:, b, :], e.tq2_[:, b, 0:D], e.hkb2[:, :], ALU.mult).then_inc(dots, 1)
                            v.wait_ge(dots, NB)
                            for b in range(NB):
                                v.tensor_reduce(e.tq2_[:, b, D:D + 16], e.t0[:, b, :].rearrange("p (h d) -> p h d", h=16),
                                                AX.X, ALU.add).then_inc(dots, 1)
                            v.wait_ge(dots, 2 * NB)
                    store_table(e, "t2", [(e.tkv, e.tkv_[:, :, :]), (e.tq2, e.tq2_[:, :, :])])
                with ExitStack() as s3:
                    e.kW1h, e.kW1l, e.vW1h, e.vW1l = (sb(n, [P, D], F32R, s3) for n in ("kW1h", "kW1l", "vW1h", "vW1l"))
                    e.kW2h, e.kW2l, e.vW2h, e.vW2l = (sb(n, [P, 4, D], F32R, s3) for n in ("kW2h", "kW2l", "vW2h", "vW2l"))
                    split_weights(e, "w2s", [(w[:, c, :], h[:, c, :], l[:, c, :]) for c in range(4)
                                             for w, h, l in ((e.hkW2, e.kW2h, e.kW2l), (e.hvW2, e.vW2h, e.vW2l))]
                                  + [(e.hkW1e[:, :], e.kW1h[:, :], e.kW1l[:, :]), (e.hvW1e[:, :], e.vW1h[:, :], e.vW1l[:, :])],
                                  [(edges, 16 * 4)])
                    e.ea = sb("ea", [P, U, P], F32, s3)
                    e.eaTh = sb("eaTh", [P, U, P], F32R, s3)
                    e.eaTl = sb("eaTl", [P, U, P], F32R, s3)
                    e.qg = sb("qg", [P, U, D + 16], F32, s3)
                    e.hid = sb("hid", [P, 2, 2 * D], F32, s3)
                    e.nb2 = sb("nb2", [P, 2, 2], F32, s3)
                    e.units = sb("units", [P, 2 * D], F32, s3)
                    e.hTh = sb("hTh", [P, 2, 2 * D], F32R, s3)
                    e.hTl = sb("hTl", [P, 2, 2 * D], F32R, s3)
                    e.vout = sb("vout", [P, 2, D], F32, s3)
                    e.st2 = sb("st2", [P, 2, 2, 6], F32, s3)
                    e.mv2 = sb("mv2", [P, 2, 2, 2], F32, s3)
                    e.va2 = sb("va2", [P, 2, 2], F32, s3)
                    e.sd2 = sb("sd2", [P, 2, 2], F32, s3)
                    e.rs2 = sb("rs2", [P, 2, 2], F32, s3)
                    e.attributes = i["edge_attr_128"][:, :]
                    l2_edges(e)
                e.noW1 = sb("noW1", [P, 8, D], F32, s2)
                e.noW2 = sb("noW2", [P, 4, D], F32, s2)
                e.nob1 = sb("nob1", [P, D], F32, s2)
                e.nob2 = sb("nob2", [P, D], F32, s2)
                no_first, no_second = e.sem("no_first"), e.sem("no_second")
                with ExitStack() as s3:
                    edge_buffers(e, sb, s3)
                    segment_softmax(e, "s2", 16, False)
                    weighted_sums(e, "b2", 16, None, [
                        (no_first, e.noW1[:, :, :], rows(i["L2_gnn_no_W1"])), (no_first, e.nob1[:, :], spread(i["L2_gnn_no_b1"])),
                        (no_second, e.noW2[:, :, :], rows(i["L2_gnn_no_W2"])), (no_first, e.nob2[:, :], spread(i["L2_gnn_no_b2"]))])
                    divide_sums(e, "d2", 16, "max", bias=e.hvb2[:, :])
                e.catT = sb("catT", [P, 8, NB * P], F32, s2)
                e.t1 = sb("t1", [P, NB, D], F32, s2)

                def x_h_and_bias(v, steps):
                    for b in range(NB):
                        steps(v.tensor_tensor(e.x[:, b, :], e.x[:, b, :], e.h[:, b, :], ALU.add))
                    steps.settle()
                    for b in range(NB):
                        steps(v.tensor_tensor(e.x[:, b, :], e.x[:, b, :], e.nob2[:, :], ALU.add))
                node_linear(e, "no1", [e.t0, e.h], e.catT, None, ACT.Copy, [(e.noW1[:, :, :], None)],
                            lambda v, b, n, ps: v.tensor_tensor(e.t1[:, b, :], ps[:, :], e.nob1[:, :], ALU.add),
                            needs=[(no_first, 48)], before=x_h_and_bias)
                node_linear(e, "no2", [e.t1], e.hT, (e.gnc, e.bnc), ACT.Relu, [(e.noW2[:, :, :], None)],
                            lambda v, b, n, ps: v.tensor_tensor(e.x[:, b, :], ps[:, :], e.x[:, b, :], ALU.add),
                            ln=(e.t1, e.t1), needs=[(no_second, 16)])

        renew()
        with ExitStack() as sc:
            edge_buffers(e, sb, sc)
            e.W3 = sb("W3", [P, 4, D], F32, sc)
            e.W3T = sb("W3T", [P, 4, D], F32, sc)
            e.asrc = sb("asrc", [P, D], F32, sc)
            e.adst = sb("adst", [P, D], F32, sc)
            e.gamma = sb("gamma", [P, D], F32, sc)
            e.beta = sb("beta", [P, D], F32, sc)
            e.tes_ = sb("tes_", [P, NB, 8], F32, sc)
            e.ted_ = sb("ted_", [P, NB, 8], F32, sc)
            e.t1 = sb("t1", [P, NB, D], F32, sc)
            e.ted3 = sb("ted3", [P, NB, 3, 8], BF16, sc)
            e.rest = sb("rest", [P, NB, 8], F32, sc)
            e.sg = sb("sg", [P, RING, 8], F32, sc)
            e.lg2 = sb("lg2", [P, U, 8], F32, sc)
            e.lg3 = sb("lg3", [P, U, 8], F32, sc)
            w3_in, dots_in, out_in = e.sem("w3_in"), e.sem("dots_in"), e.sem("out_in")
            load(e, "w3", [], [(w3_in, e.W3[:, :, :], rows(i["L3_gnn_W"])),
                               (dots_in, e.asrc[:, :], spread(i["L3_gnn_a_src"].rearrange("h d -> (h d)"))),
                               (dots_in, e.adst[:, :], spread(i["L3_gnn_a_dst"].rearrange("h d -> (h d)"))),
                               (out_in, e.gamma[:, :], spread(i["L3_gnn_ln_gamma"])),
                               (out_in, e.beta[:, :], spread(i["L3_gnn_ln_beta"]))])
            node_ln(e, "n3", e.x, e.h, ACT.Relu)
            wt_, wc_ = e.sem("w3_turned"), e.sem("w3_copied")
            with nc.Block() as block:
                @block.tensor
                def _(pe):
                    pe.wait_ge(w3_in, 16)
                    for c in range(4):
                        for r in range(4):
                            k = pe.transpose(e.ps[c][:, r * P:(r + 1) * P], e.W3[:, r, c * P:(c + 1) * P], e.ident[:, :])
                        k.then_inc(wt_, 1)

                @block.vector
                def _(v):
                    for c in range(4):
                        v.wait_ge(wt_, c + 1)
                        v.tensor_copy(e.W3T[:, c, :], e.ps[c][:, :]).then_inc(wc_, 1)
            parts = Env()

            def attention_loads(v, steps):
                parts.steps = steps
                v.wait_ge(dots_in, 32)

            def evac3(v, b, n, ps):
                st = parts.steps
                for k, vec in enumerate((e.asrc, e.adst)):
                    st(v.tensor_tensor(e.W3[:, 2 * (b % 2) + k, :], ps[:, :], vec[:, :], ALU.mult))
                st.settle()
                for k, dst in enumerate((e.tes_, e.ted_)):
                    st(v.tensor_reduce(dst[:, b, :], e.W3[:, 2 * (b % 2) + k, :].rearrange("p (h d) -> p h d", h=8), AX.X, ALU.add))
                return v.tensor_copy(e.t0[:, b, :], ps[:, :])
            node_linear(e, "l3", [e.h], e.hT, None, ACT.Copy, [(e.W3T[:, :, :], None)], evac3, before=attention_loads)
            split_table(e, "ted", e.ted3, e.ted_, 8)
            store_table(e, "t3", [(e.th, e.t0[:, :, :]), (e.tes, e.tes_[:, :, :])])
            logits_l3(e)
            segment_softmax(e, "s3", 8, True)
            weighted_sums(e, "b3", 8, e.th)
            divide_sums(e, "d3", 8, "add")
            fin = e.sem("fin")
            with nc.Block() as block:
                @block.vector
                def _(v):
                    for b in range(NB):
                        v.tensor_tensor(e.t0[:, b, :], e.t0[:, b, :], e.h[:, b, :], ALU.add).then_inc(fin, 1)
                    v.wait_ge(fin, NB)
            node_ln(e, "n4", e.t0, e.t1, ACT.Identity)
            stored = e.sem("stored")
            with nc.Block() as block:
                @block.vector
                def _(v):
                    st = Steps(v, fin, NB)
                    v.wait_ge(out_in, 32)
                    for op, vec in ((ALU.mult, e.gamma), (ALU.add, e.beta)):
                        for b in range(NB):
                            st(v.tensor_tensor(e.t1[:, b, :], e.t1[:, b, :], vec[:, :], op))
                        st.settle()
                    for b in range(NB):
                        st(v.tensor_tensor(e.x[:, b, :], e.t1[:, b, :], e.x[:, b, :], ALU.add))
                    st.settle()

                @block.sync
                def _(sp):
                    sp.wait_ge(fin, 4 * NB)
                    sp.dma_start(out[0:(NB - 1) * P, :].rearrange("(b p) n -> p b n", p=P), e.x[:, 0:NB - 1, :]).then_inc(stored, 16)
                    sp.dma_start(out[(NB - 1) * P:NODES, :], e.x[0:NODES - (NB - 1) * P, NB - 1, :]).then_inc(stored, 16)
                    sp.wait_ge(stored, 32)


def edge_buffers(e, sb, scope):
    e.gb0 = sb("gb0", [P, RING, D], F32, scope)
    e.gb2 = sb("gb2", [P, U, D], F32, scope)
    e.wt = sb("wt", [P, NT, 16], F32, scope)
    e.segA = sb("segA", [P, 16 * SEG], F32, scope)
    e.segF = sb("segF", [P, 16 * SEG], F32, scope)
    e.segB = sb("segB", [P, 16 * SEG], F32, scope)


def kernel(**inputs):
    import numpy as _np
    import concourse.bacc as _bacc
    from concourse import mybir as _mybir
    from concourse.bass_utils import run_bass_kernel_spmd as _run

    nc = _bacc.Bacc("TRN2", target_bir_lowering=False, num_devices=1)
    arrays, args = {}, {}
    for name, a in inputs.items():
        a = _np.ascontiguousarray(a)
        arrays[f"in_{name}"] = a
        args[name] = nc.dram_tensor(f"in_{name}", a.shape, _mybir.dt.from_np(a.dtype), kind="ExternalInput").ap()
    out = nc.dram_tensor("out_0", (NODES, D), _mybir.dt.float32, kind="ExternalOutput").ap()
    program(nc, args, out)
    r = _run(nc, [arrays], core_ids=[0])
    return r.results[0]["out_0"]
```
